# Optimizing a Trainium2 kernel written in Bass

```python
import numpy as np
import jax
import jax.numpy as jnp

def _softmax(x, axis=-1):
    return jax.nn.softmax(x, axis=axis)

def _gelu(x):
    return jax.nn.gelu(x, approximate=True)

def _silu(x):
    return jax.nn.silu(x)

def _sigmoid(x):
    return jax.nn.sigmoid(x)

def _layernorm(x, axis=-1, eps=1e-05):
    m = jnp.mean(x, axis=axis, keepdims=True)
    v = jnp.var(x, axis=axis, keepdims=True)
    return (x - m) / jnp.sqrt(v + eps)

def _scatter_add(tgt, idx, src, axis=0):
    return tgt.at[idx].add(src)

def _segment_sum(src, seg, n):
    return jax.ops.segment_sum(src, seg, n)
kernel_name = 'mk_gnn_resnorm_d2_gnn_r8_6a4e39'

def setup_inputs(seed: int=0):
    np.random.seed(seed)
    _w = jnp.asarray

    def _rec_inputs():
        import jax
        import jax.numpy as jnp
        _gk = jax.random.key(seed)
        x = -0.000202 + 1 * jax.random.normal(jax.random.fold_in(_gk, 1), (6250, 128), jnp.float32)
        src = jax.random.randint(jax.random.fold_in(_gk, 2), (100000,), 0, 6250, jnp.int32)
        dst = jnp.minimum((6250 * jax.random.uniform(jax.random.fold_in(_gk, 3), (100000,)) ** 2.0).astype(jnp.int32), 49999)
        _o = jnp.argsort(dst, stable=True)
        src = src[_o]
        dst = dst[_o]
        edge_attr_16 = -0.00010739 + 0.99994 * jax.random.normal(jax.random.fold_in(_gk, 12), (100000, 16), jnp.float32)
        return (x, src, dst, edge_attr_16)
    x, src, dst, edge_attr_16 = _rec_inputs()

    def _L0_gnn_setup():
        import jax, jax.numpy as jnp
        import numpy as np
        N_NODES = 6250
        N_EDGES = 100000
        IN_CH = 128
        EDGE_CH = 16
        MID_CH = 96
        OUT_CH = 128

        def _linear_params(key, fan_in, fan_out):
            k1, k2 = jax.random.split(key)
            bound = 1.0 / np.sqrt(fan_in)
            W = jax.random.uniform(k1, (fan_out, fan_in), jnp.float32, -bound, bound)
            b = jax.random.uniform(k2, (fan_out,), jnp.float32, -bound, bound)
            return (W, b)
        key = jax.random.key(seed)
        ks = jax.random.split(key, 10)
        x = jax.random.normal(ks[0], (N_NODES, IN_CH), jnp.float32)
        edge_attr = jax.random.normal(ks[1], (N_EDGES, EDGE_CH), jnp.float32)
        row = jnp.sort(jax.random.randint(ks[2], (N_EDGES,), 0, N_NODES, jnp.int32))
        col = jax.random.randint(ks[3], (N_EDGES,), 0, N_NODES, jnp.int32)
        W_m1, b_m1 = _linear_params(ks[4], IN_CH, MID_CH)
        W_m2, b_m2 = _linear_params(ks[5], IN_CH, MID_CH)
        W_me, b_me = _linear_params(ks[6], EDGE_CH, MID_CH)
        W_net, b_net = _linear_params(ks[7], MID_CH, MID_CH)
        W_o1, b_o1 = _linear_params(ks[8], IN_CH, OUT_CH)
        W_o2, b_o2 = _linear_params(ks[9], MID_CH, OUT_CH)
        return {'x': x, 'edge_attr': edge_attr, 'row': row, 'col': col, 'W_m1': W_m1, 'b_m1': b_m1, 'W_m2': W_m2, 'b_m2': b_m2, 'W_me': W_me, 'b_me': b_me, 'W_net': W_net, 'b_net': b_net, 'W_o1': W_o1, 'b_o1': b_o1, 'W_o2': W_o2, 'b_o2': b_o2}
    _L0_gnn_all = _L0_gnn_setup()
    _L0_gnn_in = {k: v for k, v in _L0_gnn_all.items() if k in ('W_m1', 'b_m1', 'W_m2', 'b_m2', 'W_me', 'b_me', 'W_net', 'b_net', 'W_o1', 'b_o1', 'W_o2', 'b_o2')}
    del _L0_gnn_all

    def _L1_gnn_setup():
        import jax, jax.numpy as jnp
        import numpy as np
        N_NODES = 6250
        HIDDEN = 128
        N_EDGES = 50000

        def _mlp_params(key, in_dim, hid, out_dim):
            k1, k2 = jax.random.split(key)
            W1 = jax.random.normal(k1, (in_dim, hid), dtype=jnp.float32) / np.sqrt(in_dim)
            b1 = jnp.zeros((hid,), dtype=jnp.float32)
            W2 = jax.random.normal(k2, (hid, out_dim), dtype=jnp.float32) / np.sqrt(hid)
            b2 = jnp.zeros((out_dim,), dtype=jnp.float32)
            return (W1, b1, W2, b2)

        def _mlp2(x, W1, b1, W2, b2):
            h = jax.nn.gelu(x @ W1 + b1, approximate=False)
            return h @ W2 + b2
        key = jax.random.key(seed)
        k_x, k_e, k_em, k_nm = jax.random.split(key, 4)
        node_latent = jax.random.normal(k_x, (N_NODES, HIDDEN), dtype=jnp.float32)
        edge_index = jax.random.randint(k_e, (2, N_EDGES), 0, N_NODES, dtype=jnp.int32)
        eW1, eb1, eW2, eb2 = _mlp_params(k_em, 2 * HIDDEN, HIDDEN, HIDDEN)
        nW1, nb1, nW2, nb2 = _mlp_params(k_nm, 2 * HIDDEN, HIDDEN, HIDDEN)
        return {'node_latent': node_latent, 'edge_index': edge_index, 'eW1': eW1, 'eb1': eb1, 'eW2': eW2, 'eb2': eb2, 'nW1': nW1, 'nb1': nb1, 'nW2': nW2, 'nb2': nb2}
    _L1_gnn_all = _L1_gnn_setup()
    _L1_gnn_in = {k: v for k, v in _L1_gnn_all.items() if k in ('eW1', 'eb1', 'eW2', 'eb2', 'nW1', 'nb1', 'nW2', 'nb2')}
    del _L1_gnn_all
    return {'x': x, 'src': src, 'dst': dst, 'edge_attr_16': edge_attr_16, 'L0_gnn_W_m1': _L0_gnn_in['W_m1'], 'L0_gnn_b_m1': _L0_gnn_in['b_m1'], 'L0_gnn_W_m2': _L0_gnn_in['W_m2'], 'L0_gnn_b_m2': _L0_gnn_in['b_m2'], 'L0_gnn_W_me': _L0_gnn_in['W_me'], 'L0_gnn_b_me': _L0_gnn_in['b_me'], 'L0_gnn_W_net': _L0_gnn_in['W_net'], 'L0_gnn_b_net': _L0_gnn_in['b_net'], 'L0_gnn_W_o1': _L0_gnn_in['W_o1'], 'L0_gnn_b_o1': _L0_gnn_in['b_o1'], 'L0_gnn_W_o2': _L0_gnn_in['W_o2'], 'L0_gnn_b_o2': _L0_gnn_in['b_o2'], 'L1_gnn_eW1': _L1_gnn_in['eW1'], 'L1_gnn_eb1': _L1_gnn_in['eb1'], 'L1_gnn_eW2': _L1_gnn_in['eW2'], 'L1_gnn_eb2': _L1_gnn_in['eb2'], 'L1_gnn_nW1': _L1_gnn_in['nW1'], 'L1_gnn_nb1': _L1_gnn_in['nb1'], 'L1_gnn_nW2': _L1_gnn_in['nW2'], 'L1_gnn_nb2': _L1_gnn_in['nb2']}

def reference(x, src, dst, edge_attr_16, L0_gnn_W_m1, L0_gnn_b_m1, L0_gnn_W_m2, L0_gnn_b_m2, L0_gnn_W_me, L0_gnn_b_me, L0_gnn_W_net, L0_gnn_b_net, L0_gnn_W_o1, L0_gnn_b_o1, L0_gnn_W_o2, L0_gnn_b_o2, L1_gnn_eW1, L1_gnn_eb1, L1_gnn_eW2, L1_gnn_eb2, L1_gnn_nW1, L1_gnn_nb1, L1_gnn_nW2, L1_gnn_nb2):
    import jax
    import jax.numpy as jnp

    def _L0_gnn_ref(x, edge_attr, row, col, W_m1, b_m1, W_m2, b_m2, W_me, b_me, W_net, b_net, W_o1, b_o1, W_o2, b_o2):
        import jax, jax.numpy as jnp
        import numpy as np
        N_NODES = 6250
        N_EDGES = 100000
        IN_CH = 128
        EDGE_CH = 16
        MID_CH = 96
        OUT_CH = 128

        def _linear_params(key, fan_in, fan_out):
            k1, k2 = jax.random.split(key)
            bound = 1.0 / np.sqrt(fan_in)
            W = jax.random.uniform(k1, (fan_out, fan_in), jnp.float32, -bound, bound)
            b = jax.random.uniform(k2, (fan_out,), jnp.float32, -bound, bound)
            return (W, b)
        msg_1 = x @ W_m1.T + b_m1
        msg_2 = x @ W_m2.T + b_m2
        msg_e = edge_attr @ W_me.T + b_me
        msg = jax.nn.relu(msg_1[row] + msg_2[col] + msg_e)
        msg = jax.nn.relu(msg @ W_net.T + b_net)
        agg = jax.ops.segment_max(msg, row, num_segments=N_NODES)
        agg = jnp.where(jnp.isfinite(agg), agg, 0.0)
        out = x @ W_o1.T + b_o1 + (agg @ W_o2.T + b_o2)
        return out

    def _L1_gnn_ref(node_latent, edge_index, eW1, eb1, eW2, eb2, nW1, nb1, nW2, nb2):
        import jax, jax.numpy as jnp
        import numpy as np
        N_NODES = 6250
        HIDDEN = 128
        N_EDGES = 50000

        def _mlp_params(key, in_dim, hid, out_dim):
            k1, k2 = jax.random.split(key)
            W1 = jax.random.normal(k1, (in_dim, hid), dtype=jnp.float32) / np.sqrt(in_dim)
            b1 = jnp.zeros((hid,), dtype=jnp.float32)
            W2 = jax.random.normal(k2, (hid, out_dim), dtype=jnp.float32) / np.sqrt(hid)
            b2 = jnp.zeros((out_dim,), dtype=jnp.float32)
            return (W1, b1, W2, b2)

        def _mlp2(x, W1, b1, W2, b2):
            h = jax.nn.gelu(x @ W1 + b1, approximate=False)
            return h @ W2 + b2
        src, dst = (edge_index[0], edge_index[1])
        edge_input = jnp.concatenate((node_latent[src], node_latent[dst]), axis=-1)
        message = _mlp2(edge_input, eW1, eb1, eW2, eb2)
        aggregated = jax.ops.segment_sum(message, dst, num_segments=node_latent.shape[0])
        node_update = _mlp2(jnp.concatenate((node_latent, aggregated), axis=-1), nW1, nb1, nW2, nb2)
        return node_latent + node_update
    edge_index = jnp.stack([src, dst])
    x = _layernorm(x + _L0_gnn_ref(x, edge_attr_16, src, dst, L0_gnn_W_m1, L0_gnn_b_m1, L0_gnn_W_m2, L0_gnn_b_m2, L0_gnn_W_me, L0_gnn_b_me, L0_gnn_W_net, L0_gnn_b_net, L0_gnn_W_o1, L0_gnn_b_o1, L0_gnn_W_o2, L0_gnn_b_o2), axis=-1)
    x = _layernorm(x + _L1_gnn_ref(x, edge_index, L1_gnn_eW1, L1_gnn_eb1, L1_gnn_eW2, L1_gnn_eb2, L1_gnn_nW1, L1_gnn_nb1, L1_gnn_nW2, L1_gnn_nb2), axis=-1)
    return x

_drawn_inputs = setup_inputs


def setup_inputs(seed=0):
    import zlib

    import numpy as np

    out = dict(_drawn_inputs(seed))
    spreads = {'L1_gnn_eb1': (0.0, 0.1),
     'L1_gnn_eb2': (0.0, 0.1),
     'L1_gnn_nb1': (0.0, 0.382),
     'L1_gnn_nb2': (0.0, 0.1)}
    factors = {'L0_gnn_b_m1': 5.328, 'L0_gnn_b_m2': 5.538}
    for name, (base, spread) in spreads.items():
        noise = np.random.default_rng([zlib.crc32(name.encode()), seed]).standard_normal(out[name].shape)
        drawn = base * np.exp(spread * noise) if base else spread * noise
        out[name] = jnp.asarray(drawn.astype(out[name].dtype))
    for name, factor in factors.items():
        out[name] = (out[name] * factor).astype(out[name].dtype)
    return out
```

```python
from contextlib import ExitStack, contextmanager

import concourse.bass as bass
from concourse import mybir

P = 128
ALU = mybir.AluOpType
ACT = mybir.ActivationFunctionType
AX = mybir.AxisListType
F32 = mybir.dt.float32
BF16 = mybir.dt.bfloat16
I32 = mybir.dt.int32
HB = 64
W = 32
C_SRC, C_HI, C_LO, C_DST = 16, 17, 18, 19
FAR = float(1 << 20)
EPS_LN = 1e-5


def sizes(n_nodes, n_edges):
    nb = -(-n_nodes // P)
    q = -(-(n_edges + P) // P)
    q += -q % 8
    ns = n_edges // P + nb + 1
    ns += -ns % 4
    return nb, q, ns


def pipeline(eng, count, stages, warm=2):
    def turn(k, u):
        for lag, stage in enumerate(stages):
            back = (lag - u + 1) // 2 if lag > u else 0
            kk, uu = k - back, (u - lag) % 2
            if isinstance(k, int) and not 0 <= 2 * kk + uu < count:
                continue
            stage(2 * kk + uu, uu, kk)
    pairs = count // 2
    warm = min(warm, pairs)
    for t in range(2 * warm):
        turn(t // 2, t % 2)
    if pairs > warm:
        with eng.Fori(warm, pairs) as k:
            turn(k, 0)
            turn(k, 1)
    for t in range(2 * pairs, count + len(stages) - 1):
        turn(t // 2, t % 2)


def wait(eng, sem, value):
    if not (isinstance(value, int) and value <= 0):
        eng.wait_ge(sem, value)


def pass_waits(eng, passed):
    eng.sem_inc(passed, 1)


class Chain:

    def __init__(self, eng, sem, per_turn=0):
        self.eng, self.sem, self.per, self.base, self.n = eng, sem, per_turn, 0, 0

    def turn(self, i):
        assert self.n in (0, self.per), (self.n, self.per)
        self.base, self.n = i * self.per, 0

    def add(self, ins):
        self.n += 1
        ins.then_inc(self.sem, 1)

    def settle(self):
        self.eng.wait_ge(self.sem, self.base + self.n)

    def __call__(self, ins):
        self.add(ins)
        self.settle()


def gnn(nc, E, x, xT, src, dst, edge_attr, wm12, bm12, w_e, w_net, b_net, wo1, wo2, bo,
        ew1a, ew1b, eb1, ew2, eb2, nw1a, nw1b, nb1, nw2, nb2, out):
    N, D = out.shape
    EP = src.shape[0]
    NB, QE, NS = sizes(N, E)
    assert QE * P == EP
    NP = NB * P
    F = w_net.shape[0]
    KA = edge_attr.shape[1]
    POS = NS * P
    G = NS // 4
    QC = QE // 8
    HN = NS // 2

    rec_d = nc.dram_tensor("edge_records", (EP, W), F32).ap()
    u_d = nc.dram_tensor("edge_in_src_order", (POS, F), F32).ap()
    s_d = nc.dram_tensor("running_max", (POS + P, F), F32).ap()
    keep_d = nc.dram_tensor("keep_flags", (POS, 1), F32).ap()
    a_d = nc.dram_tensor("src_table_1", (NP, D), F32).ap()

    whole = ExitStack()

    def sb(scope, name, shape, dt=F32):
        return scope.enter_context(nc.sbuf_tensor(name, shape, dt))

    def ps(scope, name, shape, dt=F32):
        return scope.enter_context(nc.psum_tensor(name, shape, dt))

    def sem(scope, name):
        return scope.enter_context(nc.semaphore(name))

    def bcast(ap, *shape):
        return ap.broadcast_to(shape)

    with whole:
        ident = sb(whole, "ident", [P, P])
        identb = sb(whole, "identb", [P, P], BF16)
        iota_b = sb(whole, "iota_b", [P, P], BF16)
        iota_f = sb(whole, "iota_f", [P, P])
        before = sb(whole, "before", [P, 4 * P])
        onesf = sb(whole, "onesf", [P, P])
        off_s = sb(whole, "off_s", [P, NS])
        dloc_s = sb(whole, "dloc_s", [P, NS])
        src_s = sb(whole, "src_s", [P, NS], I32)
        start_s = sb(whole, "start_s", [P, NS])
        end_s = sb(whole, "end_s", [P, NS])
        e0_row = sb(whole, "e0_row", [1, NS], I32)
        bd_row = sb(whole, "bd_row", [1, NS], I32)
        bs_row = sb(whole, "bs_row", [1, NS], I32)
        first_i = sb(whole, "first_i", [P, HB], I32)
        last_i = sb(whole, "last_i", [P, HB], I32)
        bnet_c = sb(whole, "bnet_c", [F, 1])
        wnet_s = sb(whole, "wnet_s", [F, F])
        we_s = sb(whole, "we_s", [P, 4, F])
        start_t = sb(whole, "start_t", [HB, P])
        rank_r = sb(whole, "rank_r", [HB, 2, P])

        layer0 = ExitStack()
        with layer0:
            m1 = sb(layer0, "m1", [P, NB, 3, F], BF16)
            m2 = sb(layer0, "m2", [P, NB, 3, F], BF16)
            with ExitStack() as t:
                src_i = sb(t, "src_i", [P, QE], I32)
                dst_i = sb(t, "dst_i", [P, QE], I32)
                hi_i = sb(t, "hi_i", [P, QE], I32)
                lo_i = sb(t, "lo_i", [P, QE], I32)
                src_f = sb(t, "src_f", [P, QE])
                dst_f = sb(t, "dst_f", [P, QE])
                hi_f = sb(t, "hi_f", [P, QE])
                lo_f = sb(t, "lo_f", [P, QE])
                attr = sb(t, "attr", [P, 2, QC * KA])
                rec = sb(t, "rec", [P, 2, QC, W])
                zero = sb(t, "zero", [P, 16 * F])
                cmp = sb(t, "cmp", [P, QE], BF16)
                below = sb(t, "below", [P, NB + 1])
                ohlo = sb(t, "ohlo", [P, 2, 4, P], BF16)
                ohhi = sb(t, "ohhi", [P, 2, 4, HB], BF16)
                iota_i = sb(t, "iota_i", [P, P], I32)
                iota_n = sb(t, "iota_n", [P, NS], I32)
                iota_s = sb(t, "iota_s", [P, NS])
                hist_s = sb(t, "hist_s", [HB, P])
                cum = sb(t, "cum", [HB, P])
                one_t = sb(t, "one_t", [HB, P])
                cnt = sb(t, "cnt", [HB, 2])
                cnt_i = sb(t, "cnt_i", [HB, 2], I32)
                steps_i = sb(t, "steps_i", [HB, 2], I32)
                steps = sb(t, "steps", [HB, 2])
                pre = sb(t, "pre", [HB, 2])
                pend = sb(t, "pend", [HB, 2])
                sd = sb(t, "sd", [HB, 1])
                wd = sb(t, "wd", [HB, 1])
                tri = sb(t, "tri", [HB, HB])
                ge = sb(t, "ge", [HB, 2, NS])
                own = sb(t, "own", [HB, 2, NS])
                val = sb(t, "val", [HB, NS])
                end_t = sb(t, "end_t", [HB, P])
                keep_one = sb(t, "keep_one", [P, NS])
                flag = sb(t, "flag", [HB, P])
                fidx = sb(t, "fidx", [HB, P])
                lidx = sb(t, "lidx", [HB, P])
                xt = sb(t, "xt", [P, 2, P])
                wm = sb(t, "wm", [P, 2 * F])
                bm = sb(t, "bm", [2, 2 * F])
                res = sb(t, "res", [P, 2, 2 * F])
                ps_hist = ps(t, "ps_hist", [HB, 512])
                ps_a = ps(t, "ps_a", [P, 512])
                ps_b = ps(t, "ps_b", [P, 512])
                ps_c = ps(t, "ps_c", [P, 512])
                ps_m = [ps(t, f"ps_m{k}", [P, 512]) for k in range(2)]

                edges_in = sem(t, "edges_in")
                attr_in = [sem(t, f"attr_in{k}") for k in range(2)]
                rec_out = [sem(t, f"rec_out{k}") for k in range(2)]
                consts = sem(t, "consts")
                weights_in = sem(t, "weights_in")
                zeros_out = sem(t, "zeros_out")
                columns = sem(t, "columns")
                attr_set = sem(t, "attr_set")
                cols_set = sem(t, "cols_set")
                pool_chain = sem(t, "pool_chain")
                onehots = sem(t, "onehots")
                counted = sem(t, "counted")
                dve_chain = sem(t, "dve_chain")
                blocks_counted = sem(t, "blocks_counted")
                to_pe = sem(t, "to_pe")
                to_dve = sem(t, "to_dve")
                xt_in = [sem(t, f"xt_in{k}") for k in range(2)]
                m_ready = sem(t, "m_ready")
                m_high = sem(t, "m_high")
                split_chain = sem(t, "split_chain")
                flags_out = sem(t, "flags_out")
                own_idx = sem(t, "own_idx")

                ZEROED, ALL_CONSTS = 1, 13

                with nc.Block() as block:
                    @block.sync
                    def _(sp):
                        sp.dma_start(src_i[:], src.rearrange("(p q) -> p q", p=P)).then_inc(edges_in, 16)
                        sp.dma_start(dst_i[:], dst.rearrange("(p q) -> p q", p=P)).then_inc(edges_in, 16)
                        attr_v = edge_attr.rearrange("(p c q) k -> c p (q k)", p=P, c=8)
                        rec_v = rec_d.rearrange("(p c q) w -> c p (q w)", p=P, c=8)
                        for c in range(2):
                            sp.dma_start(attr[:, c, :], attr_v[c]).then_inc(attr_in[c], 16)
                        for c in range(8):
                            k = c % 2
                            sp.wait_ge(attr_set, c + 1)
                            sp.wait_ge(cols_set, c + 1)
                            sp.dma_start(rec_v[c], rec[:, k].rearrange("p q w -> p (q w)")).then_inc(rec_out[k], 16)
                            if c + 2 < 8:
                                sp.dma_start(attr[:, k, :], attr_v[c + 2]).then_inc(attr_in[k], 16)

                        def load_x(b, k, n):
                            wait(sp, m_ready, b - 1)
                            sp.dma_start(xt[:, k, :], xT[:, bass.ds(b * P, P)]).then_inc(xt_in[k], 16)
                        pipeline(sp, NB, [load_x])
                        sp.wait_ge(consts, ZEROED)
                        u_v = u_d.rearrange("(p r) f -> p (r f)", p=P)
                        row = NS * F
                        pieces = 0
                        for c in range(0, row, 16 * F):
                            m = min(16 * F, row - c)
                            sp.dma_start(u_v[:, c:c + m], zero[:, 0:m]).then_inc(zeros_out, 16)
                            pieces += 1
                        sp.dma_start(s_d[POS:POS + P, :], zero[:, 0:F]).then_inc(zeros_out, 16)
                        for k in range(2):
                            sp.wait_ge(rec_out[k], 16 * 4)
                        sp.wait_ge(zeros_out, 16 * (pieces + 1))

                    @block.gpsimd
                    def _(pool):
                        g = nc.gpsimd
                        g.memset(zero[:], 0.0).then_inc(consts, 1)
                        g.memset(rec[:], 0.0).then_inc(consts, 1)
                        g.memset(we_s[:], 0.0).then_inc(consts, 1)
                        g.memset(onesf[:], 1.0).then_inc(consts, 1)
                        g.memset(one_t[:], 1.0).then_inc(consts, 1)
                        g.memset(before[:], 1.0).then_inc(pool_chain, 1)
                        g.memset(ident[:], 0.0).then_inc(pool_chain, 1)
                        g.memset(tri[:], 1.0).then_inc(pool_chain, 1)
                        g.iota(iota_i[:], pattern=[[1, P]], base=0, channel_multiplier=0).then_inc(pool_chain, 1)
                        g.iota(iota_n[:], pattern=[[1, NS]], base=0, channel_multiplier=0).then_inc(pool_chain, 1)
                        pool.wait_ge(pool_chain, 5)
                        g.tensor_copy(iota_f[:], iota_i[:]).then_inc(consts, 1)
                        g.tensor_copy(iota_b[:], iota_i[:]).then_inc(consts, 1)
                        g.tensor_copy(iota_s[:], iota_n[:]).then_inc(consts, 1)
                        g.affine_select(out=before[:], in_=before[:], compare_op=ALU.is_gt, fill=0.0,
                                        base=3 * P, pattern=[[-1, 4 * P]], channel_multiplier=1).then_inc(consts, 1)
                        g.affine_select(out=tri[:], in_=tri[:], compare_op=ALU.is_gt, fill=0.0,
                                        base=0, pattern=[[1, HB]], channel_multiplier=-1).then_inc(consts, 1)
                        g.affine_select(out=ident[:], in_=ident[:], compare_op=ALU.not_equal, fill=1.0,
                                        base=0, pattern=[[-1, P]], channel_multiplier=1).then_inc(pool_chain, 1)
                        pool.wait_ge(pool_chain, 6)
                        g.tensor_copy(identb[:], ident[:]).then_inc(consts, 1)
                        pool.wait_ge(columns, 4)
                        pool.wait_ge(consts, 11)
                        for c in range(8):
                            if c >= 2:
                                pool.wait_ge(rec_out[c % 2], 16 * (c // 2))
                            for col, table in ((C_SRC, src_f), (C_HI, hi_f), (C_LO, lo_f), (C_DST, dst_f)):
                                last = g.tensor_copy(rec[:, c % 2, :, col], table[:, c * QC:(c + 1) * QC])
                            last.then_inc(cols_set, 1)
                        g.memset(keep_one[:], 1.0).then_inc(pool_chain, 1)
                        pool.wait_ge(pool_chain, 7)
                        pool.dma_start(keep_d.rearrange("(p r) o -> p (r o)", p=P), keep_one[:]).then_inc(flags_out, 16)
                        pool.wait_ge(flags_out, 16)
                        pool.wait_ge(own_idx, 1)
                        for b in range(NB):
                            pool.indirect_dma_start(keep_d, bass.IndirectOffsetOnAxis(first_i[:, b:b + 1], 0),
                                                    zero[:, 0:1], None, bounds_check=POS - 1,
                                                    oob_is_err=False).then_inc(flags_out, 16)
                        pool.wait_ge(flags_out, 16 * (NB + 1))

                    @block.scalar
                    def _(act):
                        s = nc.scalar
                        for to, of in ((wm[:], wm12), (bm[:], bm12), (wnet_s[:], w_net), (bnet_c[:], b_net)):
                            act.dma_start(to, of).then_inc(weights_in, 16)
                        act.wait_ge(consts, 11)
                        for j in range(4):
                            act.dma_start(we_s[W * j:W * j + W, j, :], w_e).then_inc(weights_in, 16)
                        for c in range(8):
                            k = c % 2
                            act.wait_ge(attr_in[k], 16 * (c // 2 + 1))
                            if c >= 2:
                                act.wait_ge(rec_out[k], 16 * (c // 2))
                            s.copy(rec[:, k, :, 0:KA], attr[:, k].rearrange("p (q k) -> p q k", k=KA)).then_inc(attr_set, 1)

                        def high(b, k, n):
                            act.wait_ge(m_ready, b + 1)
                            s.copy(m1[:, bass.ds(b, 1), 0, :].rearrange("p a f -> p (a f)"), ps_m[k][:, 0:F])
                            s.copy(m2[:, bass.ds(b, 1), 0, :].rearrange("p a f -> p (a f)"), ps_m[k][:, F:2 * F]).then_inc(m_high, 1)
                        pipeline(act, NB, [high])

                    @block.vector
                    def _(dve):
                        v = nc.vector
                        ch = Chain(dve, dve_chain)
                        dve.wait_ge(edges_in, 32)
                        v.tensor_single_scalar(hi_i[:], src_i[:], 7, op=ALU.logical_shift_right)
                        ch(v.tensor_single_scalar(lo_i[:], src_i[:], P - 1, op=ALU.bitwise_and))
                        v.tensor_copy(src_f[:], src_i[:]).then_inc(columns, 1)
                        v.tensor_copy(hi_f[:], hi_i[:]).then_inc(columns, 1)
                        v.tensor_copy(lo_f[:], lo_i[:]).then_inc(columns, 1)
                        v.tensor_copy(dst_f[:], dst_i[:]).then_inc(columns, 1)
                        dve.wait_ge(columns, 4)
                        dve.wait_ge(consts, 11)

                        def onehot(g, k, n):
                            wait(dve, counted, g - 1)
                            for j in range(4):
                                v.tensor_scalar(ohlo[:, k, j, :], iota_b[:], lo_f[:, bass.ds(4 * g + j, 1)], None, ALU.is_equal)
                                last = v.tensor_scalar(ohhi[:, k, j, :], iota_b[:, 0:HB], hi_f[:, bass.ds(4 * g + j, 1)], None, ALU.is_equal)
                            last.then_inc(onehots, 1)
                        pipeline(dve, QE // 4, [onehot])
                        for b in range(NB + 1):
                            ch(v.tensor_scalar(cmp[:], dst_f[:], float(P * b), 0.0, ALU.is_lt, ALU.add,
                                               accum_out=below[:, b:b + 1]))
                        v.engine_nop().then_inc(to_pe, 1)

                        def parts(b, k, n):
                            wait(dve, m_high, b + 1)
                            pc.turn(b)
                            one = bass.ds(b, 1)
                            for m, c in ((m1, 0), (m2, F)):
                                hi = m[:, one, 0, :].rearrange("p a f -> p (a f)")
                                pc.add(v.tensor_tensor(res[:, 0, c:c + F], ps_m[k][:, c:c + F], hi, ALU.subtract))
                            pc.settle()
                            for m, c in ((m1, 0), (m2, F)):
                                pc.add(v.tensor_copy(m[:, one, 1, :].rearrange("p a f -> p (a f)"), res[:, 0, c:c + F]))
                            pc.settle()
                            for m, c in ((m1, 0), (m2, F)):
                                mid = m[:, one, 1, :].rearrange("p a f -> p (a f)")
                                pc.add(v.tensor_tensor(res[:, 1, c:c + F], res[:, 0, c:c + F], mid, ALU.subtract))
                            pc.settle()
                            for m, c in ((m1, 0), (m2, F)):
                                last = v.tensor_copy(m[:, one, 2, :].rearrange("p a f -> p (a f)"), res[:, 1, c:c + F])
                                pc.add(last)
                            pc.settle()
                        pc = Chain(dve, split_chain, 8)
                        pipeline(dve, NB, [parts])

                        dve.wait_ge(counted, QE // 4)
                        dve.wait_ge(to_dve, 1)
                        v.memset(cnt[:], 0.0)
                        v.tensor_copy(sd[0:NB, :], ps_a[0:NB, 0:1])
                        ch(v.tensor_copy(hist_s[:], ps_hist[:, 0:P]))
                        v.tensor_reduce(cnt[0:NB, 0:1], hist_s[0:NB, :], AX.X, ALU.add)
                        ch(v.tensor_tensor(cnt[0:NB, 1:2], ps_a[0:NB, 1:2], sd[0:NB, :], ALU.subtract))
                        ch(v.tensor_scalar(cnt_i[:], cnt[:], float(P - 1), None, ALU.add))
                        ch(v.tensor_single_scalar(steps_i[:], cnt_i[:], 7, op=ALU.logical_shift_right))
                        ch(v.tensor_copy(steps[:], steps_i[:]))
                        v.engine_nop().then_inc(to_pe, 1)
                        dve.wait_ge(to_dve, 2)
                        ch(v.tensor_copy(pre[:], ps_b[0:HB, 0:2]))
                        ch(v.tensor_tensor(pend[:], pre[:], steps[:], ALU.add))
                        for o in range(2):
                            v.tensor_scalar(ge[:, o], iota_s[0:HB, :], pre[:, o:o + 1], None, ALU.is_ge)
                        ch(v.tensor_scalar(wd[0:NB], pre[0:NB, 1:2], -float(P), -float(E), ALU.mult, ALU.add))
                        for o in range(2):
                            v.scalar_tensor_tensor(out=own[:, o], in0=iota_s[0:HB, :], scalar=pend[:, o:o + 1],
                                                   in1=ge[:, o], op0=ALU.is_lt, op1=ALU.mult)
                        ch(v.tensor_tensor(wd[0:NB], wd[0:NB], sd[0:NB], ALU.add))
                        ch(v.tensor_scalar(val[0:NB], iota_s[0:NB, :], float(P), wd[0:NB, :], ALU.mult, ALU.add))
                        ch(v.tensor_tensor(val[0:NB], val[0:NB], own[0:NB, 1], ALU.mult))
                        ch(v.tensor_tensor_scan(cum[:], one_t[:], hist_s[:], 0.0, ALU.mult, ALU.add))
                        ch(v.tensor_tensor(cum[:], cum[:], hist_s[:], ALU.subtract))
                        ch(v.tensor_scalar(start_t[:], one_t[:], pre[:, 0:1], float(P), ALU.mult, ALU.mult))
                        ch(v.tensor_tensor(start_t[:], start_t[:], cum[:], ALU.add))
                        v.tensor_copy(rank_r[:, 0], start_t[:])
                        v.tensor_scalar(flag[:], hist_s[:], 0.0, None, ALU.is_gt)
                        v.tensor_scalar(fidx[:], hist_s[:], 0.0, FAR, ALU.is_equal, ALU.mult)
                        ch(v.tensor_tensor(end_t[:], start_t[:], hist_s[:], ALU.add))
                        ch(v.tensor_tensor(fidx[:], fidx[:], start_t[:], ALU.add))
                        ch(v.scalar_tensor_tensor(out=lidx[:], in0=end_t[:], scalar=-float(POS + 1), in1=flag[:],
                                                  op0=ALU.add, op1=ALU.mult))
                        v.tensor_scalar(lidx[:], lidx[:], float(POS), None, ALU.add).then_inc(to_pe, 1)
                        dve.wait_ge(to_dve, 3)
                        v.tensor_copy(first_i[:], ps_a[:, 0:HB])
                        v.tensor_copy(last_i[:], ps_a[:, HB:2 * HB]).then_inc(own_idx, 1)
                        for h in range(2):
                            part = slice(h * HN, (h + 1) * HN)
                            one, two = (ps_b, ps_c) if h == 0 else (ps_c, ps_b)
                            dve.wait_ge(to_dve, 4 + 5 * h)
                            v.tensor_scalar(e0_row[:, part], one[0:1, 0:HN], float(E), None, ALU.add).then_inc(to_pe, 1)
                            dve.wait_ge(to_dve, 5 + 5 * h)
                            v.tensor_scalar(bs_row[:, part], two[0:1, 0:HN], -1.0, None, ALU.add).then_inc(to_pe, 1)
                            dve.wait_ge(to_dve, 6 + 5 * h)
                            v.tensor_scalar(bd_row[:, part], one[0:1, 0:HN], -1.0, None, ALU.add)
                            v.tensor_scalar(off_s[:, part], one[:, 0:HN], float(P), -float(P), ALU.mult, ALU.add).then_inc(to_pe, 1)
                            dve.wait_ge(to_dve, 7 + 5 * h)
                            v.scalar_tensor_tensor(out=start_s[:, part], in0=iota_s[:, part], scalar=-float(P), in1=two[:, 0:HN],
                                                   op0=ALU.mult, op1=ALU.add).then_inc(to_pe, 1)
                            dve.wait_ge(to_dve, 8 + 5 * h)
                            v.scalar_tensor_tensor(out=end_s[:, part], in0=iota_s[:, part], scalar=-float(P), in1=one[:, 0:HN],
                                                   op0=ALU.mult, op1=ALU.add).then_inc(to_pe, 1)

                    @block.tensor
                    def _(pe):
                        m = nc.tensor

                        def count(g, k, n, first=False, last=False):
                            pe.wait_ge(onehots, g + 1)
                            for j in range(4):
                                mm = m.matmul(ps_hist[:, 0:P], ohhi[:, k, j, :], ohlo[:, k, j, :],
                                              start=(first and j == 0), stop=(last and j == 3), skip_group_check=True)
                            mm.then_inc(counted, 1)
                        gc = QE // 4
                        count(0, 0, 0, first=True)
                        count(1, 1, 0)
                        with pe.Fori(1, gc // 2 - 1) as k:
                            count(2 * k, 0, k)
                            count(2 * k + 1, 1, k)
                        count(gc - 2, 0, 0)
                        count(gc - 1, 1, 0, last=True)

                        def tables(b, k, n):
                            pe.wait_ge(xt_in[k], 16 * (n + 1))
                            wait(pe, split_chain, 8 * (b - 1))
                            m.matmul(ps_m[k][:, 0:2 * F], xt[:, k, :], wm[:], start=True, stop=False)
                            m.matmul(ps_m[k][:, 0:2 * F], onesf[0:2, :], bm[:], start=False, stop=True).then_inc(m_ready, 1)
                        pe.wait_ge(consts, 11)
                        pe.wait_ge(weights_in, 16 * 8)
                        pipeline(pe, NB, [tables])
                        pe.wait_ge(to_pe, 1)
                        m.matmul(ps_a[0:NB, 0:1], below[:, 0:NB], onesf[:, 0:1], start=True, stop=True)
                        m.matmul(ps_a[0:NB, 1:2], below[:, 1:NB + 1], onesf[:, 0:1], start=True, stop=True).then_inc(to_dve, 1)
                        pe.wait_ge(to_pe, 2)
                        m.matmul(ps_b[0:HB, 0:2], tri[:], steps[:], start=True, stop=True).then_inc(to_dve, 1)
                        pe.wait_ge(to_pe, 3)
                        m.transpose(ps_a[:, 0:HB], fidx[:], ident[0:HB, 0:HB])
                        m.transpose(ps_a[:, HB:2 * HB], lidx[:], ident[0:HB, 0:HB]).then_inc(to_dve, 1)
                        done = 3
                        for h in range(2):
                            part = slice(h * HN, (h + 1) * HN)
                            for left, right in ((onesf[0:NB, :], val[0:NB, part]),
                                                      (onesf[0:NB, :], ge[0:NB, 0, part]),
                                                      (onesf[0:NB, :], ge[0:NB, 1, part]),
                                                      (start_t[0:NB, :], own[0:NB, 0, part]),
                                                      (end_t[0:NB, :], own[0:NB, 0, part])):
                                if done > 4:
                                    pe.wait_ge(to_pe, done - 1)
                                ps_x = (ps_b, ps_c)[(done - 3) % 2]
                                m.matmul(ps_x[:, 0:HN], left, right, start=True, stop=True).then_inc(to_dve, 1)
                                done += 1

            with ExitStack() as t:
                rec = sb(t, "rec_in", [P, 2, 4, W])
                inv = sb(t, "inv", [P, 2, 4])
                srcm = sb(t, "srcm", [P, 2, 4])
                him = sb(t, "him", [P, 2, 4])
                ohlo = sb(t, "ohlo_a", [P, 2, 4, P], BF16)
                ohhi = sb(t, "ohhi_a", [P, 2, 4, HB], BF16)
                ohd = sb(t, "ohd_a", [P, 2, 4, P], BF16)
                hiT = sb(t, "hiT", [HB, 2, 4, P])
                dstT = sb(t, "dstT", [P, 2, 4, P], BF16)
                recT = sb(t, "recT", [P, 2, P])
                junk = sb(t, "junk", [P, 4, 4 * P], BF16)
                junk2 = sb(t, "junk2", [P, 4, P], BF16)
                within = sb(t, "within", [P, 2, 4])
                across = sb(t, "across", [P, 2, 4])
                place = sb(t, "place", [P, 2, 4], I32)
                u = sb(t, "u", [P, 2, 4, F])
                ps_row = ps(t, "ps_row", [P, 512])
                ps_rec = ps(t, "ps_rec", [P, 512])
                ps_hi = ps(t, "ps_hi", [HB, 1024], BF16)
                ps_dst = ps(t, "ps_dst", [P, 1024], BF16)
                ps_cnt = ps(t, "ps_cnt", [P, 4, P])
                ps_new = ps(t, "ps_new", [HB, 512])
                ps_u_bank = ps(t, "ps_u", [P, 512])
                ps_u = ps_u_bank[:, 0:4 * F].rearrange("p (j f) -> p j f", j=4)
                rec_in = [sem(t, f"rec_in{k}") for k in range(2)]
                oh_ready = sem(t, "oh_ready")
                key_chain = sem(t, "key_chain")
                rec_turned = sem(t, "rec_turned")
                rows_ready = sem(t, "rows_ready")
                hi_turned = sem(t, "hi_turned")
                dst_turned = sem(t, "dst_turned")
                recT_ready = sem(t, "recT_ready")
                hiT_ready = sem(t, "hiT_ready")
                dstT_ready = sem(t, "dstT_ready")
                new_ready = sem(t, "new_ready")
                cnt_ready = sem(t, "cnt_ready")
                place_chain = sem(t, "place_chain")
                place_ready = sem(t, "place_ready")
                sum_ready = sem(t, "sum_ready")
                u_ready = sem(t, "u_ready")
                sent = [sem(t, f"sent{k}") for k in range(2)]
                passed = sem(t, "passed_a")
                passed_pe = sem(t, "passed_pe")

                with nc.Block() as block:
                    @block.sync
                    def _(sp):
                        def load(i, k, n):
                            wait(sp, oh_ready, i - 1)
                            wait(sp, rec_turned, i - 1)
                            for j in range(4):
                                e0 = sp.value_load(e0_row[0:1, bass.ds(4 * i + j, 1)], min_val=0, max_val=E)
                                sp.dma_start(rec[:, k, j, :], rec_d[bass.ds(e0, P), :]).then_inc(rec_in[k], 16)
                        pipeline(sp, G, [load])

                    @block.gpsimd
                    def _(pool):
                        def send(i, k, n):
                            pool.wait_ge(place_ready, i + 1)
                            pool.wait_ge(u_ready, i + 1)
                            pass_waits(pool, passed)
                            for j in range(4):
                                pool.indirect_dma_start(u_d, bass.IndirectOffsetOnAxis(place[:, k, j:j + 1], 0),
                                                        u[:, k, j, :], None, bounds_check=POS - 1,
                                                        oob_is_err=False).then_inc(sent[k], 16)
                        pipeline(pool, G, [send])
                        for k in range(2):
                            pool.wait_ge(sent[k], 64 * ((G + 1 - k) // 2))

                    @block.vector
                    def _(dve):
                        v = nc.vector
                        keys = Chain(dve, key_chain, 5)
                        places = Chain(dve, place_chain, 10)

                        def onehot(i, k, n):
                            dve.wait_ge(rec_in[k], 64 * (n + 1))
                            keys.turn(i)
                            now = bass.ds(4 * i, 4)
                            keys.add(v.tensor_tensor(dloc_s[:, now], rec[:, k, :, C_DST], off_s[:, now], ALU.subtract))
                            keys.add(v.tensor_scalar(src_s[:, now], rec[:, k, :, C_SRC], float(NP - 1), None, ALU.min))
                            keys.settle()
                            keys(v.tensor_scalar(inv[:, k], dloc_s[:, now], float(P), None, ALU.is_ge))
                            keys.add(v.scalar_tensor_tensor(out=him[:, k], in0=inv[:, k], scalar=1000.0, in1=rec[:, k, :, C_HI],
                                                            op0=ALU.mult, op1=ALU.add))
                            last = v.scalar_tensor_tensor(out=srcm[:, k], in0=inv[:, k], scalar=65536.0, in1=rec[:, k, :, C_SRC],
                                                          op0=ALU.mult, op1=ALU.add)
                            keys(last)
                            wait(dve, new_ready, i - 1)
                            wait(dve, dst_turned, i - 1)
                            for j in range(4):
                                v.tensor_scalar(ohlo[:, k, j, :], iota_b[:], rec[:, k, j, C_LO:C_LO + 1], None, ALU.is_equal)
                                v.tensor_scalar(ohhi[:, k, j, :], iota_b[:, 0:HB], him[:, k, j:j + 1], None, ALU.is_equal)
                                last = v.tensor_scalar(ohd[:, k, j, :], iota_b[:], dloc_s[:, bass.ds(4 * i + j, 1)], None, ALU.is_equal)
                            last.then_inc(oh_ready, 1)

                        def rank(i, k, n):
                            places.turn(i)
                            dve.wait_ge(rows_ready, i + 1)
                            for j in range(4):
                                last = v.scalar_tensor_tensor(
                                    out=junk[:, j, 0:P * (j + 1)], in0=ps_row[:, 0:P * (j + 1)], scalar=srcm[:, k, j:j + 1],
                                    in1=before[:, P * (3 - j):4 * P], op0=ALU.is_equal, op1=ALU.mult,
                                    accum_out=within[:, k, j:j + 1])
                                places.add(last)
                            dve.wait_ge(cnt_ready, i + 1)
                            for j in range(4):
                                last = v.tensor_tensor_reduce(junk2[:, j, :], ps_cnt[:, j, :], ohlo[:, k, j, :], 1.0, 0.0,
                                                              ALU.mult, ALU.add, across[:, k, j:j + 1])
                                places.add(last)
                            places.settle()
                            places(v.scalar_tensor_tensor(out=within[:, k], in0=inv[:, k], scalar=FAR, in1=within[:, k],
                                                          op0=ALU.mult, op1=ALU.add))
                            wait(dve, sent[k], 64 * n)
                            v.tensor_tensor(place[:, k], within[:, k], across[:, k], ALU.add).then_inc(place_ready, 1)
                            dve.wait_ge(new_ready, i + 1)
                            places(v.tensor_tensor(rank_r[:, 1 - k], rank_r[:, k], ps_new[:, 0:P], ALU.add))
                        pipeline(dve, G, [onehot, rank])

                    @block.tensor
                    def _(pe):
                        m = nc.tensor

                        def turn(i, k, n):
                            pe.wait_ge(rec_in[k], 64 * (n + 1))
                            wait(pe, recT_ready, i)
                            m.transpose(ps_rec[:, 0:P], rec[:, k].rearrange("p j w -> p (j w)"), ident[:]).then_inc(rec_turned, 1)
                            pe.wait_ge(key_chain, 5 * (i + 1))
                            wait(pe, place_chain, 10 * i - 6)
                            for j in range(4):
                                mm = m.transpose(ps_row[:, P * j:P * j + P], srcm[:, k, j:j + 1].broadcast_to([P, P]), ident[:])
                            mm.then_inc(rows_ready, 1)
                            pe.wait_ge(oh_ready, i + 1)
                            wait(pe, hiT_ready, i)
                            pass_waits(pe, passed_pe)
                            for j in range(4):
                                mm = m.transpose(ps_hi[:, P * j:P * j + P], ohhi[:, k, j, :], identb[:])
                            mm.then_inc(hi_turned, 1)
                            wait(pe, dstT_ready, i)
                            for j in range(4):
                                mm = m.transpose(ps_dst[:, P * j:P * j + P], ohd[:, k, j, :], identb[:])
                            mm.then_inc(dst_turned, 1)

                        def product(i, k, n):
                            pe.wait_ge(hiT_ready, i + 1)
                            wait(pe, place_chain, 10 * i)
                            for j in range(4):
                                mm = m.matmul(ps_cnt[:, j, :], hiT[:, k, j, :], rank_r[:, k, :], start=True, stop=True)
                            mm.then_inc(cnt_ready, 1)
                            for j in range(4):
                                mm = m.matmul(ps_new[:, 0:P], ohhi[:, k, j, :], ohlo[:, k, j, :], start=(j == 0), stop=(j == 3))
                            mm.then_inc(new_ready, 1)
                            pe.wait_ge(recT_ready, i + 1)
                            pe.wait_ge(dstT_ready, i + 1)
                            wait(pe, u_ready, i)
                            m.matmul(ps_u.rearrange("p j f -> p (j f)"), recT[:, k, :], we_s[:].rearrange("p j f -> p (j f)"),
                                     start=True, stop=False, skip_group_check=True)
                            for j in range(4):
                                b = pe.value_load(bd_row[0:1, bass.ds(4 * i + j, 1)], min_val=0, max_val=NB - 1)
                                for part in range(3):
                                    mm = m.matmul(ps_u[:, j, :], dstT[:, k, j, :], m2[:, bass.ds(b, 1), part, :].rearrange("p a f -> p (a f)"),
                                                  start=False, stop=(part == 2), skip_group_check=True)
                            mm.then_inc(sum_ready, 1)
                        pipeline(pe, G, [turn, product])

                    @block.scalar
                    def _(act):
                        s = nc.scalar

                        def turned(i, k, n):
                            act.wait_ge(rec_turned, i + 1)
                            wait(act, sum_ready, i - 1)
                            s.copy(recT[:, k, :], ps_rec[:, 0:P]).then_inc(recT_ready, 1)
                            act.wait_ge(hi_turned, i + 1)
                            s.copy(hiT[:, k].rearrange("p j e -> p (j e)"), ps_hi[:, 0:512]).then_inc(hiT_ready, 1)
                            act.wait_ge(dst_turned, i + 1)
                            s.copy(dstT[:, k].rearrange("p j e -> p (j e)"), ps_dst[:, 0:512]).then_inc(dstT_ready, 1)

                        def rows(i, k, n):
                            act.wait_ge(sum_ready, i + 1)
                            wait(act, sent[k], 64 * n)
                            s.copy(u[:, k], ps_u).then_inc(u_ready, 1)
                        pipeline(act, G, [turned, rows])

            with ExitStack() as t:
                u = sb(t, "u_in", [P, 2, 4, F])
                keep = sb(t, "keep", [F, 2, 4 * P])
                after = sb(t, "after", [P, 2, 4, P], BF16)
                oh = sb(t, "oh_b", [P, 2, 4, P], BF16)
                msg = sb(t, "msg", [F, 2, 4 * P])
                msg2 = sb(t, "msg2", [F, 2, 4 * P])
                top = sb(t, "top", [F, 2, 4 * P])
                row = sb(t, "row", [P, 2, 4, F])
                ps_pre = [ps(t, f"ps_pre{k}", [F, 512]) for k in range(2)]
                ps_net = [ps(t, f"ps_net{k}", [F, 512]) for k in range(2)]
                ps_top = [ps(t, f"ps_top{k}", [P, 4, P]) for k in range(2)]
                u_in = [sem(t, f"u_in{k}") for k in range(2)]
                keep_in = [sem(t, f"keep_in{k}") for k in range(2)]
                oh_ready = sem(t, "oh_ready_b")
                after_ready = sem(t, "after_ready")
                pre_ready = sem(t, "pre_ready")
                msg_ready = sem(t, "msg_ready")
                net_ready = sem(t, "net_ready")
                msg2_ready = sem(t, "msg2_ready")
                top_ready = sem(t, "top_ready")
                top_turned = sem(t, "top_turned")
                row_ready = sem(t, "row_ready")
                row_out = [sem(t, f"row_out{k}") for k in range(2)]
                passed = sem(t, "passed_b")
                with nc.Block() as block:
                    @block.sync
                    def _(sp):
                        def load(i, k, n):
                            wait(sp, pre_ready, i - 1)
                            sp.dma_start(u[:, k], u_d[bass.ds(4 * P * i, 4 * P), :].rearrange("(j p) f -> p j f", p=P)).then_inc(u_in[k], 16)
                            wait(sp, top_ready, i - 1)
                            pass_waits(sp, passed)
                            sp.dma_start(keep[:, k, :], keep_d[bass.ds(4 * P * i, 4 * P), :].rearrange("r o -> o r").broadcast_to([F, 4 * P])).then_inc(keep_in[k], 16)

                        def store(i, k, n):
                            sp.wait_ge(row_ready, i + 1)
                            sp.dma_start(s_d[bass.ds(4 * P * i, 4 * P), :].rearrange("(j p) f -> p j f", p=P), row[:, k]).then_inc(row_out[k], 16)

                        def nothing(i, k, n):
                            pass
                        pipeline(sp, G, [load, nothing, store])
                        for k in range(2):
                            sp.wait_ge(row_out[k], 16 * ((G + 1 - k) // 2))

                    @block.vector
                    def _(dve):
                        v = nc.vector

                        def onehot(i, k, n):
                            wait(dve, pre_ready, i - 1)
                            for j in range(4):
                                last = v.tensor_scalar(after[:, k, j, :], iota_b[:], start_s[:, bass.ds(4 * i + j, 1)], None, ALU.is_ge)
                            last.then_inc(after_ready, 1)
                            dve.wait_ge(after_ready, i + 1)
                            for j in range(4):
                                last = v.scalar_tensor_tensor(out=oh[:, k, j, :], in0=iota_b[:], scalar=end_s[:, bass.ds(4 * i + j, 1)],
                                                              in1=after[:, k, j, :], op0=ALU.is_lt, op1=ALU.mult)
                            last.then_inc(oh_ready, 1)

                        def scan(i, k, n):
                            dve.wait_ge(keep_in[k], 16 * (n + 1))
                            dve.wait_ge(msg2_ready, i + 1)
                            wait(dve, top_turned, i - 1)
                            wait(dve, top_ready, i)
                            first = isinstance(i, int) and i == 0
                            v.tensor_tensor_scan(top[:, k, :], keep[:, k, :], msg2[:, k, :],
                                                 0.0 if first else top[:, 1 - k, 4 * P - 1:4 * P],
                                                 ALU.mult, ALU.max).then_inc(top_ready, 1)
                        pipeline(dve, G, [onehot, scan])

                    @block.tensor
                    def _(pe):
                        m = nc.tensor

                        def pre(i, k, n):
                            pe.wait_ge(oh_ready, i + 1)
                            pe.wait_ge(u_in[k], 16 * (n + 1))
                            wait(pe, msg_ready, i - 1)
                            for j in range(4):
                                b = pe.value_load(bs_row[0:1, bass.ds(4 * i + j, 1)], min_val=0, max_val=NB - 1)
                                to = ps_pre[k][:, P * j:P * j + P]
                                m.matmul(to, u[:, k, j, :], ident[:], start=True, stop=False)
                                for part in range(3):
                                    mm = m.matmul(to, m1[:, bass.ds(b, 1), part, :].rearrange("p a f -> p (a f)"), oh[:, k, j, :],
                                                  start=False, stop=(part == 2))
                            mm.then_inc(pre_ready, 1)

                        def net(i, k, n):
                            pe.wait_ge(msg_ready, i + 1)
                            wait(pe, msg2_ready, i - 1)
                            m.matmul(ps_net[k][:], wnet_s[:], msg[:, k, :], start=True, stop=True).then_inc(net_ready, 1)

                        def turn(i, k, n):
                            pe.wait_ge(top_ready, i + 1)
                            wait(pe, row_ready, i - 1)
                            for j in range(4):
                                mm = m.transpose(ps_top[k][:, j, 0:F], top[:, k, P * j:P * j + P], ident[0:F, 0:F])
                            mm.then_inc(top_turned, 1)
                        pipeline(pe, G, [pre, net, turn])

                    @block.scalar
                    def _(act):
                        s = nc.scalar

                        def first(i, k, n):
                            act.wait_ge(pre_ready, i + 1)
                            wait(act, net_ready, i - 1)
                            s.activation(msg[:, k, :], ps_pre[k][:], ACT.Relu).then_inc(msg_ready, 1)

                        def second(i, k, n):
                            act.wait_ge(net_ready, i + 1)
                            wait(act, top_ready, i - 1)
                            s.activation(msg2[:, k, :], ps_net[k][:], ACT.Relu, bias=bnet_c[:]).then_inc(msg2_ready, 1)

                        def rows(i, k, n):
                            act.wait_ge(top_turned, i + 1)
                            wait(act, row_out[k], 16 * n)
                            s.copy(row[:, k], ps_top[k][:, :, 0:F]).then_inc(row_ready, 1)
                        pipeline(act, G, [first, second, rows])

        layer1 = ExitStack()
        with layer1:
            x1 = sb(layer1, "x1", [P, NB, D])
            x1T = sb(layer1, "x1T", [D, NP])
            hsumT = sb(layer1, "hsumT", [D, NP])
            deg = sb(layer1, "deg", [P, NB])
            bpart = sb(layer1, "bpart", [P, NB, 3, D], BF16)
            with ExitStack() as t:
                agg_all = sb(t, "agg_all", [P, NB, F])
                agg = sb(t, "agg", [P, 2, F])
                aggT = sb(t, "aggT", [F, 2, P])
                xt = sb(t, "xt_n", [P, 2, P])
                xr = sb(t, "xr", [P, 2, D])
                y = sb(t, "y", [P, 2, D])
                stats = sb(t, "stats", [P, 2, 6])
                mv = sb(t, "mv", [P, 2, 2])
                std = sb(t, "std", [P, 2, 1])
                rstd = sb(t, "rstd", [P, 2, 1])
                xs = sb(t, "xs", [P, 2, D])
                xsT = sb(t, "xsT", [P, 2, P])
                arow = sb(t, "arow", [P, 2, D])
                r1 = sb(t, "r1", [P, D])
                r2 = sb(t, "r2", [P, D])
                wo1_s = sb(t, "wo1_s", [D, D])
                wo2_s = sb(t, "wo2_s", [F, D])
                bo_s = sb(t, "bo_s", [2, D])
                ew1_s = sb(t, "ew1_s", [D, 2 * D])
                eb1_s = sb(t, "eb1_s", [1, 2 * D])
                eps_c = sb(t, "eps_c", [P, 1])
                ps_t = ps(t, "ps_t", [P, 512])
                ps_y = [ps(t, f"ps_y{k}", [P, 512]) for k in range(2)]
                ps_x = ps(t, "ps_x", [P, 512])
                ps_ab = [ps(t, f"ps_ab{k}", [P, 512]) for k in range(2)]
                agg_in = sem(t, "agg_in")
                w_in = sem(t, "w_in")
                x_in = [sem(t, f"x_in{k}") for k in range(2)]
                eps_set = sem(t, "eps_set")
                agg_ready = sem(t, "agg_ready")
                agg_turned = sem(t, "agg_turned")
                aggT_ready = sem(t, "aggT_ready")
                y_ready = sem(t, "y_ready")
                norm_chain = sem(t, "norm_chain")
                passed = sem(t, "passed_c")
                std_ready = sem(t, "std_ready")
                x1_ready = sem(t, "x1_ready")
                x1_turned = sem(t, "x1_turned")
                x1T_ready = sem(t, "x1T_ready")
                ab_ready = sem(t, "ab_ready")
                a_ready = sem(t, "a_ready")
                part_chain = sem(t, "part_chain")
                a_out = [sem(t, f"a_out{k}") for k in range(2)]
                with nc.Block() as block:
                    @block.gpsimd
                    def _(pool):
                        nc.gpsimd.memset(eps_c[:], EPS_LN).then_inc(eps_set, 1)
                        nc.gpsimd.memset(hsumT[:], 0.0).then_inc(eps_set, 1)
                        nc.gpsimd.memset(deg[:], 0.0).then_inc(eps_set, 1)
                        for b in range(NB):
                            pool.indirect_dma_start(agg_all[:, b, :], None, s_d,
                                                    bass.IndirectOffsetOnAxis(last_i[:, b:b + 1], 0)).then_inc(agg_in, 16)
                        pool.wait_ge(agg_in, 16 * NB)

                    @block.sync
                    def _(sp):
                        for to, of in ((wo1_s[:], wo1), (wo2_s[:], wo2), (bo_s[:], bo), (ew1_s[:, 0:D], ew1a),
                                       (ew1_s[:, D:2 * D], ew1b), (eb1_s[:], eb1)):
                            sp.dma_start(to, of).then_inc(w_in, 16)

                        def load(b, k, n):
                            wait(sp, y_ready, b - 1)
                            wait(sp, norm_chain, 5 * b - 9)
                            sp.dma_start(xt[:, k, :], xT[:, bass.ds(P * b, P)]).then_inc(x_in[k], 16)
                            sp.dma_start(xr[:, k, :], x[bass.ds(P * b, P), :]).then_inc(x_in[k], 16)

                        def nothing(b, k, n):
                            pass

                        def store(b, k, n):
                            sp.wait_ge(a_ready, b + 1)
                            sp.dma_start(a_d[bass.ds(P * b, P), :], arow[:, k, :]).then_inc(a_out[k], 16)
                        pipeline(sp, NB, [load, nothing, store])
                        sp.wait_ge(a_out[0], 16 * (NB - NB // 2))
                        sp.wait_ge(a_out[1], 16 * (NB // 2))

                    @block.scalar
                    def _(act):
                        s = nc.scalar
                        act.wait_ge(agg_in, 16 * NB)
                        act.wait_ge(eps_set, 1)

                        def fetch(b, k, n):
                            wait(act, agg_turned, b - 1)
                            s.copy(agg[:, k, :], agg_all[:, bass.ds(b, 1), :].rearrange("p a f -> p (a f)")).then_inc(agg_ready, 1)
                            act.wait_ge(agg_turned, b + 1)
                            wait(act, y_ready, b - 1)
                            s.copy(aggT[:, k, :], ps_t[0:F, 0:P]).then_inc(aggT_ready, 1)

                        def deviation(b, k, n):
                            act.wait_ge(norm_chain, 5 * b + 3)
                            wait(act, x1_ready, b - 1)
                            s.activation(std[:, k, :], mv[:, k, 1:2], ACT.Sqrt, bias=eps_c[:]).then_inc(std_ready, 1)

                        def tables(b, k, n):
                            act.wait_ge(x1_turned, b + 1)
                            wait(act, ab_ready, b - 1)
                            s.copy(xsT[:, k, :], ps_x[:, 0:P])
                            s.copy(x1T[:, bass.ds(P * b, P)], ps_x[:, 0:P]).then_inc(x1T_ready, 1)
                            act.wait_ge(ab_ready, b + 1)
                            wait(act, a_out[k], 16 * n)
                            s.copy(arow[:, k, :], ps_ab[k][:, 0:D])
                            s.copy(bpart[:, bass.ds(b, 1), 0, :].rearrange("p a f -> p (a f)"), ps_ab[k][:, D:2 * D]).then_inc(a_ready, 1)
                        pipeline(act, NB, [fetch, deviation, tables])

                    @block.tensor
                    def _(pe):
                        m = nc.tensor
                        pe.wait_ge(w_in, 16 * 6)

                        def turn(b, k, n):
                            pe.wait_ge(agg_ready, b + 1)
                            wait(pe, aggT_ready, b)
                            m.transpose(ps_t[0:F, 0:P], agg[:, k, :], ident[:]).then_inc(agg_turned, 1)

                        def update(b, k, n):
                            pe.wait_ge(aggT_ready, b + 1)
                            pe.wait_ge(x_in[k], 32 * (n + 1))
                            wait(pe, norm_chain, 5 * b - 9)
                            m.matmul(ps_y[k][:, 0:D], xt[:, k, :], wo1_s[:], start=True, stop=False)
                            m.matmul(ps_y[k][:, 0:D], onesf[0:2, :], bo_s[:], start=False, stop=False)
                            m.matmul(ps_y[k][:, 0:D], aggT[:, k, :], wo2_s[:], start=False, stop=True).then_inc(y_ready, 1)

                        def tables(b, k, n):
                            pe.wait_ge(x1_ready, b + 1)
                            wait(pe, x1T_ready, b)
                            m.transpose(ps_x[:, 0:P], xs[:, k, :], ident[:]).then_inc(x1_turned, 1)
                            pe.wait_ge(x1T_ready, b + 1)
                            wait(pe, part_chain, 4 * b - 7)
                            m.matmul(ps_ab[k][:, 0:2 * D], xsT[:, k, :], ew1_s[:], start=True, stop=False)
                            m.matmul(ps_ab[k][:, 0:2 * D], onesf[0:1, :], eb1_s[:], start=False, stop=True).then_inc(ab_ready, 1)
                        pipeline(pe, NB, [turn, update, tables])

                    @block.vector
                    def _(dve):
                        v = nc.vector
                        nch = Chain(dve, norm_chain, 5)
                        pch = Chain(dve, part_chain, 4)

                        def norm(b, k, n):
                            nch.turn(b)
                            dve.wait_ge(x_in[k], 32 * (n + 1))
                            dve.wait_ge(y_ready, b + 1)
                            nch(v.tensor_tensor(y[:, k, :], ps_y[k][:, 0:D], xr[:, k, :], ALU.add))
                            nch(v.bn_stats(stats[:, k, :], y[:, k, :]))
                            pass_waits(dve, passed)
                            nch(v.bn_aggr(mv[:, k, :], stats[:, k, :]))
                            dve.wait_ge(std_ready, b + 1)
                            nch(v.reciprocal(rstd[:, k, :], std[:, k, :]))
                            wait(dve, x1_turned, b - 1)
                            nch(v.tensor_scalar(xs[:, k, :], y[:, k, :], mv[:, k, 0:1], rstd[:, k, :], ALU.subtract, ALU.mult))
                            v.tensor_copy(x1[:, bass.ds(b, 1), :].rearrange("p a f -> p (a f)"), xs[:, k, :]).then_inc(x1_ready, 1)

                        def parts(b, k, n):
                            pch.turn(b)
                            dve.wait_ge(a_ready, b + 1)
                            part = [bpart[:, bass.ds(b, 1), q, :].rearrange("p a f -> p (a f)") for q in range(3)]
                            pch(v.tensor_tensor(r1[:], ps_ab[k][:, D:2 * D], part[0], ALU.subtract))
                            pch(v.tensor_copy(part[1], r1[:]))
                            pch(v.tensor_tensor(r2[:], r1[:], part[1], ALU.subtract))
                            pch(v.tensor_copy(part[2], r2[:]))
                        def nothing(b, k, n):
                            pass
                        pipeline(dve, NB, [nothing, norm, parts])

            with ExitStack() as t:
                idx = sb(t, "idx", [P, 2, 4], I32)
                a_rows = sb(t, "a_rows", [P, 2, 4, D])
                ohd = sb(t, "ohd_f", [P, 4, 4, P])
                dstT = sb(t, "dstT_b", [P, 2, 4, P], BF16)
                h = sb(t, "h", [P, 2, 4, D])
                ps_t = [ps(t, f"ps_tt{k}", [P, 512]) for k in range(2)]
                ps_h = [ps(t, f"ps_h{k}", [P, 4, D]) for k in range(2)]
                ps_s = [ps(t, f"ps_s{k}", [D, 4, P]) for k in range(2)]
                ps_n = [ps(t, f"ps_n{k}", [P, 512]) for k in range(2)]
                idx_ready = sem(t, "idx_ready")
                got = [sem(t, f"got{k}") for k in range(2)]
                passed = sem(t, "passed_d")
                oh_ready = sem(t, "oh_ready_c")
                dst_turned = sem(t, "dst_turned_b")
                dstT_ready = sem(t, "dstT_ready_b")
                pre_ready = sem(t, "pre_ready_b")
                h_ready = sem(t, "h_ready")
                sum_ready = sem(t, "sum_ready_b")
                add_chain = sem(t, "add_chain")
                with nc.Block() as block:
                    @block.gpsimd
                    def _(pool):
                        def fetch(i, k, n):
                            pool.wait_ge(idx_ready, i + 1)
                            wait(pool, pre_ready, i - 1)
                            pass_waits(pool, passed)
                            for j in range(4):
                                pool.indirect_dma_start(a_rows[:, k, j, :], None, a_d,
                                                        bass.IndirectOffsetOnAxis(idx[:, k, j:j + 1], 0)).then_inc(got[k], 16)
                        pipeline(pool, G, [fetch])

                    @block.vector
                    def _(dve):
                        v = nc.vector
                        adds = Chain(dve, add_chain, 8)

                        def prepare(i, k, n):
                            wait(dve, got[k], 64 * n)
                            v.tensor_copy(idx[:, k], src_s[:, bass.ds(4 * i, 4)]).then_inc(idx_ready, 1)

                        def onehot(i, k, n):
                            wait(dve, sum_ready, i - 1)
                            for j in range(4):
                                last = v.tensor_scalar(ohd[:, k, j, :], iota_f[:], dloc_s[:, bass.ds(4 * i + j, 1)], None, ALU.is_equal)
                            last.then_inc(oh_ready, 1)

                        def add(i, k, n):
                            adds.turn(i)
                            dve.wait_ge(sum_ready, i + 1)
                            for j in range(4):
                                b = dve.value_load(bd_row[0:1, bass.ds(4 * i + j, 1)], min_val=0, max_val=NB - 1)
                                at = hsumT[:, bass.ds(P * b, P)]
                                adds.add(v.tensor_tensor(at, at, ps_s[k][:, j, :], ALU.add))
                                dg = deg[:, bass.ds(b, 1)]
                                adds.add(v.tensor_tensor(dg, dg, ps_n[k][:, j:j + 1], ALU.add))
                                adds.settle()

                        def ahead(i, k, n):
                            prepare(i, k, n)
                        pipeline(dve, G, [prepare, onehot, add])

                    @block.tensor
                    def _(pe):
                        m = nc.tensor

                        def turn(i, k, n):
                            pe.wait_ge(oh_ready, i + 1)
                            wait(pe, dstT_ready, i - 1)
                            for j in range(4):
                                mm = m.transpose(ps_t[k][:, P * j:P * j + P], ohd[:, k, j, :], ident[:])
                            mm.then_inc(dst_turned, 1)
                            pe.wait_ge(got[k], 64 * (n + 1))
                            wait(pe, h_ready, i - 1)
                            m.matmul(ps_h[k][:].rearrange("p j d -> p (j d)"), ident[:], a_rows[:, k].rearrange("p j d -> p (j d)"),
                                     start=True, stop=False, skip_group_check=True)
                            pe.wait_ge(dstT_ready, i + 1)
                            for j in range(4):
                                b = pe.value_load(bd_row[0:1, bass.ds(4 * i + j, 1)], min_val=0, max_val=NB - 1)
                                for part in range(3):
                                    mm = m.matmul(ps_h[k][:, j, :], dstT[:, k, j, :], bpart[:, bass.ds(b, 1), part, :].rearrange("p a f -> p (a f)"),
                                                  start=False, stop=(part == 2), skip_group_check=True)
                            mm.then_inc(pre_ready, 1)

                        def sums(i, k, n):
                            pe.wait_ge(h_ready, i + 1)
                            wait(pe, add_chain, 8 * (i - 1))
                            for j in range(4):
                                m.matmul(ps_s[k][:, j, :], h[:, k, j, :], ohd[:, k, j, :], start=True, stop=True)
                                mm = m.matmul(ps_n[k][:, j:j + 1], ohd[:, k, j, :], onesf[:, 0:1], start=True, stop=True)
                            mm.then_inc(sum_ready, 1)

                        def nothing(i, k, n):
                            pass
                        pipeline(pe, G, [nothing, turn, sums])

                    @block.scalar
                    def _(act):
                        s = nc.scalar

                        def turned(i, k, n):
                            act.wait_ge(dst_turned, i + 1)
                            wait(act, pre_ready, i - 1)
                            s.copy(dstT[:, k].rearrange("p j e -> p (j e)"), ps_t[k][:]).then_inc(dstT_ready, 1)

                        def gelu(i, k, n):
                            act.wait_ge(pre_ready, i + 1)
                            wait(act, sum_ready, i - 1)
                            s.activation(h[:, k], ps_h[k][:], ACT.Gelu).then_inc(h_ready, 1)
                        pipeline(act, G, [turned, gelu])

            with ExitStack() as t:
                diag = sb(t, "diag", [P, 2, P])
                aggd = sb(t, "aggd", [P, 2, P])
                hid = sb(t, "hid", [P, 2, P])
                stats = sb(t, "stats_b", [P, 2, 6])
                mv = sb(t, "mv_b", [P, NB, 2])
                one_mv = sb(t, "one_mv", [P, 2, 2])
                std = sb(t, "std_b", [P, NB])
                rstd = sb(t, "rstd_b", [P, NB])
                yout = sb(t, "yout", [P, NB, D])
                ew2_s = sb(t, "ew2_s", [D, D])
                eb2_s = sb(t, "eb2_s", [P, D])
                nw1a_s = sb(t, "nw1a_s", [D, D])
                nw1b_s = sb(t, "nw1b_s", [D, D])
                nb1_c = sb(t, "nb1_c", [D, 1])
                nw2_s = sb(t, "nw2_s", [D, D])
                nb2_s = sb(t, "nb2_s", [1, D])
                eps_c = sb(t, "eps_d", [P, 1])
                ps_g = [ps(t, f"ps_g{k}", [P, 512]) for k in range(2)]
                ps_k = [ps(t, f"ps_k{k}", [P, 512]) for k in range(2)]
                ps_o = [ps(t, f"ps_o{k}", [P, 512]) for k in range(2)]
                w_in = sem(t, "w_in_b")
                eps_set = sem(t, "eps_set_b")
                diag_ready = sem(t, "diag_ready")
                g_ready = sem(t, "g_ready")
                aggd_ready = sem(t, "aggd_ready")
                k_ready = sem(t, "k_ready")
                hid_ready = sem(t, "hid_ready")
                o_ready = sem(t, "o_ready")
                y_chain = sem(t, "y_chain")
                var_ready = sem(t, "var_ready_b")
                passed = sem(t, "passed_e")
                std_ready = sem(t, "std_ready_b")
                r_ready = sem(t, "r_ready")
                out_ready = sem(t, "out_ready")
                stored = sem(t, "stored")
                with nc.Block() as block:
                    @block.gpsimd
                    def _(pool):
                        nc.gpsimd.memset(eps_c[:], EPS_LN).then_inc(eps_set, 1)

                    @block.sync
                    def _(sp):
                        for to, of in ((ew2_s[:], ew2), (eb2_s[:], eb2.broadcast_to([P, D])), (nw1a_s[:], nw1a), (nw1b_s[:], nw1b),
                                       (nb1_c[:], nb1), (nw2_s[:], nw2), (nb2_s[:], nb2)):
                            sp.dma_start(to, of).then_inc(w_in, 16)
                        per = 7
                        count = 0
                        for b in range(0, NB, per):
                            full = min(b + per, N // P)
                            sp.wait_ge(out_ready, min(b + per, NB))
                            if full > b:
                                sp.dma_start(out[P * b:P * full, :].rearrange("(b p) d -> p b d", p=P), yout[:, b:full, :]).then_inc(stored, 16)
                                count += 1
                        if N % P:
                            sp.dma_start(out[P * (N // P):N, :], yout[0:N % P, NB - 1, :]).then_inc(stored, 16)
                            count += 1
                        sp.wait_ge(stored, 16 * count)

                    @block.vector
                    def _(dve):
                        v = nc.vector
                        ych = Chain(dve, y_chain, 4)

                        def diagonal(b, k, n):
                            wait(dve, g_ready, b - 1)
                            v.tensor_scalar(diag[:, k, :], ident[:], deg[:, bass.ds(b, 1)], None, ALU.mult).then_inc(diag_ready, 1)

                        def result(b, k, n):
                            ych.turn(b)
                            dve.wait_ge(o_ready, b + 1)
                            xb = x1[:, bass.ds(b, 1), :].rearrange("p a f -> p (a f)")
                            ych(v.scalar_tensor_tensor(out=xb, in0=xb, scalar=2.0, in1=ps_o[k][:, 0:D], op0=ALU.mult, op1=ALU.add))
                            pass_waits(dve, passed)
                            ych(v.bn_stats(stats[:, k, :], xb))
                            pass_waits(dve, passed)
                            ych(v.bn_aggr(one_mv[:, k, :], stats[:, k, :]))
                            ych(v.tensor_copy(mv[:, bass.ds(b, 1), :].rearrange("p a f -> p (a f)"), one_mv[:, k, :]))
                        def nothing(b, k, n):
                            pass
                        pipeline(dve, NB, [diagonal, nothing, result])
                        v.engine_nop().then_inc(var_ready, 1)
                        dve.wait_ge(std_ready, 1)
                        v.reciprocal(rstd[:], std[:]).then_inc(r_ready, 1)
                        dve.wait_ge(r_ready, 1)

                        def normed(b, k, n):
                            one = bass.ds(b, 1)
                            v.tensor_scalar(yout[:, one, :].rearrange("p a f -> p (a f)"), x1[:, one, :].rearrange("p a f -> p (a f)"),
                                            mv[:, one, 0:1].rearrange("p a f -> p (a f)"), rstd[:, one], ALU.subtract, ALU.mult).then_inc(out_ready, 1)
                        pipeline(dve, NB, [normed])

                    @block.tensor
                    def _(pe):
                        m = nc.tensor
                        pe.wait_ge(w_in, 16 * 7)

                        def gather(b, k, n):
                            pe.wait_ge(diag_ready, b + 1)
                            wait(pe, aggd_ready, b - 1)
                            cols = bass.ds(P * b, P)
                            m.matmul(ps_g[k][:, 0:P], ew2_s[:], hsumT[:, cols], start=True, stop=False)
                            m.matmul(ps_g[k][:, 0:P], eb2_s[:], diag[:, k, :], start=False, stop=True).then_inc(g_ready, 1)

                        def hidden(b, k, n):
                            pe.wait_ge(aggd_ready, b + 1)
                            wait(pe, hid_ready, b - 1)
                            m.matmul(ps_k[k][:, 0:P], nw1a_s[:], x1T[:, bass.ds(P * b, P)], start=True, stop=False)
                            m.matmul(ps_k[k][:, 0:P], nw1b_s[:], aggd[:, k, :], start=False, stop=True).then_inc(k_ready, 1)

                        def update(b, k, n):
                            pe.wait_ge(hid_ready, b + 1)
                            wait(pe, y_chain, 4 * b - 7)
                            m.matmul(ps_o[k][:, 0:D], hid[:, k, :], nw2_s[:], start=True, stop=False)
                            m.matmul(ps_o[k][:, 0:D], onesf[0:1, :], nb2_s[:], start=False, stop=True).then_inc(o_ready, 1)
                        pipeline(pe, NB, [gather, hidden, update])

                    @block.scalar
                    def _(act):
                        s = nc.scalar
                        act.wait_ge(w_in, 16 * 7)

                        def summed(b, k, n):
                            act.wait_ge(g_ready, b + 1)
                            wait(act, k_ready, b - 1)
                            s.copy(aggd[:, k, :], ps_g[k][:, 0:P]).then_inc(aggd_ready, 1)

                        def gelu(b, k, n):
                            act.wait_ge(k_ready, b + 1)
                            wait(act, o_ready, b - 1)
                            s.activation(hid[:, k, :], ps_k[k][:, 0:P], ACT.Gelu, bias=nb1_c[:]).then_inc(hid_ready, 1)
                        pipeline(act, NB, [summed, gelu])
                        act.wait_ge(var_ready, 1)
                        act.wait_ge(eps_set, 1)
                        s.activation(std[:], mv[:, :, 1], ACT.Sqrt, bias=eps_c[:]).then_inc(std_ready, 1)


_ARGS = ["x", "xT", "src", "dst", "edge_attr", "wm12", "bm12", "w_e", "w_net", "b_net", "wo1", "wo2", "bo",
         "ew1a", "ew1b", "eb1", "ew2", "eb2", "nw1a", "nw1b", "nb1", "nw2", "nb2"]


def lay_out(i):
    import numpy as np
    a = {k: np.asarray(v) for k, v in i.items()}
    n, e = a["x"].shape[0], a["src"].shape[0]
    nb, q, _ = sizes(n, e)
    rows, edges = nb * P, q * P

    def pad(v, m, fill=0):
        return np.concatenate([v, np.full((m - v.shape[0],) + v.shape[1:], fill, v.dtype)])

    x = pad(a["x"], rows)
    ka = a["edge_attr_16"].shape[1]
    f = a["L0_gnn_W_net"].shape[0]
    d = x.shape[1]
    o = {
        "x": x, "xT": x.T,
        "src": pad(a["src"], edges, rows), "dst": pad(a["dst"], edges, rows),
        "edge_attr": pad(a["edge_attr_16"], edges),
        "wm12": np.concatenate([a["L0_gnn_W_m1"].T, a["L0_gnn_W_m2"].T], 1),
        "bm12": np.stack([np.concatenate([a["L0_gnn_b_m1"], a["L0_gnn_b_m2"]]),
                          np.concatenate([np.zeros_like(a["L0_gnn_b_me"]), a["L0_gnn_b_me"]])]),
        "w_e": pad(a["L0_gnn_W_me"].T, W),
        "w_net": a["L0_gnn_W_net"].T, "b_net": a["L0_gnn_b_net"][:, None],
        "wo1": a["L0_gnn_W_o1"].T, "wo2": a["L0_gnn_W_o2"].T,
        "bo": np.stack([a["L0_gnn_b_o1"], a["L0_gnn_b_o2"]]),
        "ew1a": a["L1_gnn_eW1"][:d], "ew1b": a["L1_gnn_eW1"][d:], "eb1": np.concatenate([np.zeros_like(a["L1_gnn_eb1"]), a["L1_gnn_eb1"]])[None],
        "ew2": a["L1_gnn_eW2"], "eb2": a["L1_gnn_eb2"][None],
        "nw1a": a["L1_gnn_nW1"][:d], "nw1b": a["L1_gnn_nW1"][d:], "nb1": a["L1_gnn_nb1"][:, None],
        "nw2": a["L1_gnn_nW2"], "nb2": a["L1_gnn_nb2"][None],
    }
    return {k: np.ascontiguousarray(o[k]) for k in _ARGS}, n, e


def program(nc, arrays, n, e):
    args = []
    for name in _ARGS:
        v = arrays[name]
        args.append(nc.dram_tensor(f"in_{name}", v.shape, mybir.dt.from_np(v.dtype), kind="ExternalInput").ap())
    out = nc.dram_tensor("out_0", (n, arrays["x"].shape[1]), F32, kind="ExternalOutput").ap()
    gnn(nc, e, *args, out)


def kernel(**inputs):
    import concourse.bacc as bacc
    from concourse.bass_utils import run_bass_kernel_spmd

    nc = bacc.Bacc("TRN2", target_bir_lowering=False, num_devices=1)
    arrays, n, e = lay_out(inputs)
    program(nc, arrays, n, e)
    r = run_bass_kernel_spmd(nc, [{f"in_{k}": v for k, v in arrays.items()}], core_ids=[0])
    return r.results[0]["out_0"]
```

```python
from contextlib import ExitStack, contextmanager

import concourse.bass as bass
from concourse import mybir

P = 128
ALU = mybir.AluOpType
ACT = mybir.ActivationFunctionType
AX = mybir.AxisListType
F32 = mybir.dt.float32
BF16 = mybir.dt.bfloat16
I32 = mybir.dt.int32
HB = 64
W = 32
C_SRC, C_HI, C_LO, C_DST = 16, 17, 18, 19
FAR = float(1 << 20)
EPS_LN = 1e-5


def sizes(n_nodes, n_edges):
    nb = -(-n_nodes // P)
    q = -(-(n_edges + P) // P)
    q += -q % 8
    ns = n_edges // P + nb + 1
    ns += -ns % 4
    return nb, q, ns


def pipeline(eng, count, stages, cool=0, unroll=4):
    most = max(lag for lag, _ in stages)
    warm = most + 2 * unroll
    warm += -warm % unroll
    end = (count - cool) // unroll * unroll

    def turn(k, u):
        for lag, stage in stages:
            n, v = k + (u - lag) // unroll, (u - lag) % unroll
            if isinstance(k, int) and not 0 <= unroll * n + v < count:
                continue
            stage(unroll * n + v, v, n)

    def straight(first, last):
        for t in range(first, last):
            turn(t // unroll, t % unroll)
    if end - warm < 2 * unroll:
        warm = end = 0
    straight(0, warm)
    if end:
        with eng.Fori(warm // unroll, end // unroll) as k:
            for u in range(unroll):
                turn(k, u)
    straight(end, count + most)


def offsets(nc, engine, row, last):
    _, values = nc.values_load_multi_w_load_instructions(row, engines=[engine], min_val=0, max_val=last,
                                                         skip_runtime_bounds_check_because="the table holds block starts only")
    return values


def past(sems, u, n, back=0):
    return sems[(u - back) % 4], n + (u - back) // 4 + 1


def wait(eng, sem, value):
    if not (isinstance(value, int) and value <= 0):
        eng.wait_ge(sem, value)


def pass_waits(eng, passed):
    eng.sem_inc(passed, 1)


class Chain:

    def __init__(self, eng, sem, per_turn=0):
        self.eng, self.sem, self.per, self.base, self.n = eng, sem, per_turn, 0, 0

    def turn(self, i):
        assert self.n in (0, self.per), (self.n, self.per)
        self.base, self.n = i * self.per, 0

    def add(self, ins):
        self.n += 1
        ins.then_inc(self.sem, 1)

    def settle(self):
        self.eng.wait_ge(self.sem, self.base + self.n)

    def __call__(self, ins):
        self.add(ins)
        self.settle()


def gnn(nc, E, x, xT, src, dst, edge_attr, wm12, bm12, w_e, w_net, b_net, wo1, wo2, bo,
        ew1a, ew1b, eb1, ew2, eb2, nw1a, nw1b, nb1, nw2, nb2, out):
    N, D = out.shape
    EP = src.shape[0]
    NB, QE, NS = sizes(N, E)
    assert QE * P == EP
    NP = NB * P
    F = w_net.shape[0]
    KA = edge_attr.shape[1]
    POS = NS * P
    G = NS // 4
    QC = QE // 8
    HN = NS // 2

    rec_d = nc.dram_tensor("edge_records", (EP, W), F32).ap()
    moved_d = nc.dram_tensor("edge_records_moved", (EP, W), F32).ap()
    u_d = nc.dram_tensor("edge_in_src_order", (POS, F), F32).ap()
    s_d = nc.dram_tensor("running_max", (POS + P, F), F32).ap()
    keep_d = nc.dram_tensor("keep_flags", (POS, 1), F32).ap()
    a_d = nc.dram_tensor("src_table_1", (NP, D), F32).ap()

    whole = ExitStack()

    def sb(scope, name, shape, dt=F32):
        return scope.enter_context(nc.sbuf_tensor(name, shape, dt))

    def ps(scope, name, shape, dt=F32):
        return scope.enter_context(nc.psum_tensor(name, shape, dt))

    def sem(scope, name):
        return scope.enter_context(nc.semaphore(name))

    def bcast(ap, *shape):
        return ap.broadcast_to(shape)

    with whole:
        ident = sb(whole, "ident", [P, P])
        identb = sb(whole, "identb", [P, P], BF16)
        iota_b = sb(whole, "iota_b", [P, P], BF16)
        iota_f = sb(whole, "iota_f", [P, P])
        before = sb(whole, "before", [P, 4 * P])
        onesf = sb(whole, "onesf", [P, P])
        off_s = sb(whole, "off_s", [P, NS])
        dloc_s = sb(whole, "dloc_s", [P, NS])
        src_s = sb(whole, "src_s", [P, NS], I32)
        start_s = sb(whole, "start_s", [P, NS])
        end_s = sb(whole, "end_s", [P, NS])
        e0_row = sb(whole, "e0_row", [1, NS], I32)
        df_row = sb(whole, "df_row", [1, NS], I32)
        dd_row = sb(whole, "dd_row", [1, NS], I32)
        db_row = sb(whole, "db_row", [1, NS], I32)
        sf_row = sb(whole, "sf_row", [1, NS], I32)
        first_i = sb(whole, "first_i", [P, HB], I32)
        last_i = sb(whole, "last_i", [P, HB], I32)
        bnet_c = sb(whole, "bnet_c", [F, 1])
        wnet_s = sb(whole, "wnet_s", [F, F])
        we_s = sb(whole, "we_s", [P, 4, F])
        unsorted_i = sb(whole, "unsorted_i", [1, 1], I32)
        onesb = sb(whole, "onesb", [P, P], BF16)
        far_c = sb(whole, "far_c", [HB, 1])
        start_t = sb(whole, "start_t", [HB, P])
        rank_r = sb(whole, "rank_r", [HB, 4, P])

        layer0 = ExitStack()
        with layer0:
            m1 = sb(layer0, "m1", [P, NB * F])
            m2 = sb(layer0, "m2", [P, NB * F])
            with ExitStack() as t:
                src_i = sb(t, "src_i", [P, QE], I32)
                dst_i = sb(t, "dst_i", [P, QE], I32)
                hi_i = sb(t, "hi_i", [P, QE], I32)
                lo_i = sb(t, "lo_i", [P, QE], I32)
                src_f = sb(t, "src_f", [P, QE])
                dst_f = sb(t, "dst_f", [P, QE])
                hi_f = sb(t, "hi_f", [P, QE])
                lo_f = sb(t, "lo_f", [P, QE])
                attr = sb(t, "attr", [P, 2, QC * KA])
                rec = sb(t, "rec", [P, 2, QC, W])
                zero = sb(t, "zero", [P, 16 * F])
                cmp = sb(t, "cmp", [P, QE], BF16)
                below = sb(t, "below", [P, NB + 1])
                next_i = sb(t, "next_i", [P, 2], I32)
                next_f = sb(t, "next_f", [P, 2])
                drops = sb(t, "drops", [P, 2])
                ohlo = sb(t, "ohlo", [P, 4, 4, P], BF16)
                ohhi = sb(t, "ohhi", [P, 4, 4, HB], BF16)
                iota_i = sb(t, "iota_i", [P, P], I32)
                iota_n = sb(t, "iota_n", [P, NS], I32)
                iota_s = sb(t, "iota_s", [P, NS])
                hist_s = sb(t, "hist_s", [HB, P])
                cum = sb(t, "cum", [HB, P])
                one_t = sb(t, "one_t", [HB, P])
                cnt = sb(t, "cnt", [HB, 2])
                cnt_i = sb(t, "cnt_i", [HB, 2], I32)
                steps_i = sb(t, "steps_i", [HB, 2], I32)
                steps = sb(t, "steps", [HB, 2])
                pre = sb(t, "pre", [HB, 2])
                pend = sb(t, "pend", [HB, 2])
                sd = sb(t, "sd", [HB, 1])
                wd = sb(t, "wd", [HB, 1])
                tri = sb(t, "tri", [HB, HB])
                ge = sb(t, "ge", [HB, 2, NS])
                own = sb(t, "own", [HB, 2, NS])
                val = sb(t, "val", [HB, NS])
                end_t = sb(t, "end_t", [HB, P])
                keep_one = sb(t, "keep_one", [P, NS])
                flag = sb(t, "flag", [HB, P])
                fidx = sb(t, "fidx", [HB, P])
                lidx = sb(t, "lidx", [HB, P])
                xt = sb(t, "xt", [P, 4, P])
                wm = sb(t, "wm", [P, 2 * F])
                bm = sb(t, "bm", [2, 2 * F])
                ps_hist = ps(t, "ps_hist", [HB, 512])
                ps_a = ps(t, "ps_a", [P, 512])
                ps_b = ps(t, "ps_b", [P, 512])
                ps_c = ps(t, "ps_c", [P, 512])
                ps_m = [ps(t, f"ps_m{k}", [P, 512]) for k in range(2)]

                edges_in = sem(t, "edges_in")
                attr_in = [sem(t, f"attr_in{k}") for k in range(2)]
                rec_out = [sem(t, f"rec_out{k}") for k in range(2)]
                consts = sem(t, "consts")
                weights_in = sem(t, "weights_in")
                zeros_out = sem(t, "zeros_out")
                columns = sem(t, "columns")
                attr_set = sem(t, "attr_set")
                cols_set = sem(t, "cols_set")
                pool_chain = sem(t, "pool_chain")
                onehots = sem(t, "onehots")
                counted = sem(t, "counted")
                dve_chain = sem(t, "dve_chain")
                blocks_counted = sem(t, "blocks_counted")
                to_pe = sem(t, "to_pe")
                to_dve = sem(t, "to_dve")
                xt_in = [sem(t, f"xt_in{k}") for k in range(4)]
                m_ready = sem(t, "m_ready")
                m_taken = sem(t, "m_taken")
                flags_out = sem(t, "flags_out")
                own_idx = sem(t, "own_idx")

                ZEROED, ALL_CONSTS = 1, 13

                with nc.Block() as block:
                    @block.sync
                    def _(sp):
                        sp.dma_start(src_i[:], src.rearrange("(p q) -> p q", p=P)).then_inc(edges_in, 16)
                        sp.dma_start(dst_i[:], dst.rearrange("(p q) -> p q", p=P)).then_inc(edges_in, 16)
                        sp.dma_start(next_i[0:P - 1, :], dst.rearrange("(p q) -> p q", p=P)[1:P, 0:2]).then_inc(edges_in, 16)
                        sp.dma_start(next_i[P - 1:P, :], dst.rearrange("(p q) -> p q", p=P)[P - 1:P, QE - 2:QE]).then_inc(edges_in, 16)
                        attr_v = edge_attr.rearrange("(p c q) k -> c p (q k)", p=P, c=8)
                        rec_v = rec_d.rearrange("(p c q) w -> c p (q w)", p=P, c=8)
                        for c in range(2):
                            sp.dma_start(attr[:, c, :], attr_v[c]).then_inc(attr_in[c], 16)
                        for c in range(8):
                            k = c % 2
                            sp.wait_ge(attr_set, c + 1)
                            sp.wait_ge(cols_set, c + 1)
                            sp.dma_start(rec_v[c], rec[:, k].rearrange("p q w -> p (q w)")).then_inc(rec_out[k], 16)
                            if c + 2 < 8:
                                sp.dma_start(attr[:, k, :], attr_v[c + 2]).then_inc(attr_in[k], 16)

                        def load_x(b, u, n):
                            wait(sp, m_ready, b - 3)
                            sp.dma_start(xt[:, u, :], xT[:, bass.ds(b * P, P)]).then_inc(xt_in[u], 16)
                        pipeline(sp, NB, [(0, load_x)])
                        sp.wait_ge(consts, ZEROED)
                        u_v = u_d.rearrange("(p r) f -> p (r f)", p=P)
                        row = NS * F
                        pieces = 0
                        for c in range(0, row, 16 * F):
                            m = min(16 * F, row - c)
                            sp.dma_start(u_v[:, c:c + m], zero[:, 0:m]).then_inc(zeros_out, 16)
                            pieces += 1
                        sp.dma_start(s_d[POS:POS + P, :], zero[:, 0:F]).then_inc(zeros_out, 16)
                        for k in range(2):
                            sp.wait_ge(rec_out[k], 16 * 4)
                        sp.wait_ge(zeros_out, 16 * (pieces + 1))

                    @block.gpsimd
                    def _(pool):
                        g = nc.gpsimd
                        g.memset(zero[:], 0.0).then_inc(consts, 1)
                        g.memset(rec[:], 0.0).then_inc(consts, 1)
                        g.memset(we_s[:], 0.0).then_inc(consts, 1)
                        g.memset(onesf[:], 1.0).then_inc(consts, 1)
                        g.memset(one_t[:], 1.0).then_inc(consts, 1)
                        g.memset(onesb[:], 1.0).then_inc(consts, 1)
                        g.memset(before[:], 1.0).then_inc(pool_chain, 1)
                        g.memset(ident[:], 0.0).then_inc(pool_chain, 1)
                        g.memset(tri[:], 1.0).then_inc(pool_chain, 1)
                        g.memset(far_c[:], 0.0).then_inc(pool_chain, 1)
                        g.iota(iota_i[:], pattern=[[1, P]], base=0, channel_multiplier=0).then_inc(pool_chain, 1)
                        g.iota(iota_n[:], pattern=[[1, NS]], base=0, channel_multiplier=0).then_inc(pool_chain, 1)
                        pool.wait_ge(pool_chain, 6)
                        g.tensor_copy(iota_f[:], iota_i[:]).then_inc(consts, 1)
                        g.tensor_copy(iota_b[:], iota_i[:]).then_inc(consts, 1)
                        g.tensor_copy(iota_s[:], iota_n[:]).then_inc(consts, 1)
                        g.affine_select(out=before[:], in_=before[:], compare_op=ALU.is_gt, fill=0.0,
                                        base=3 * P, pattern=[[-1, 4 * P]], channel_multiplier=1).then_inc(consts, 1)
                        g.affine_select(out=tri[:], in_=tri[:], compare_op=ALU.is_gt, fill=0.0,
                                        base=0, pattern=[[1, HB]], channel_multiplier=-1).then_inc(consts, 1)
                        g.affine_select(out=ident[:], in_=ident[:], compare_op=ALU.not_equal, fill=1.0,
                                        base=0, pattern=[[-1, P]], channel_multiplier=1).then_inc(pool_chain, 1)
                        g.affine_select(out=far_c[:], in_=far_c[:], compare_op=ALU.not_equal, fill=FAR,
                                        base=-(HB - 1), pattern=[[0, 1]], channel_multiplier=1).then_inc(consts, 1)
                        pool.wait_ge(pool_chain, 7)
                        g.tensor_copy(identb[:], ident[:]).then_inc(consts, 1)
                        pool.wait_ge(columns, 4)
                        pool.wait_ge(consts, ALL_CONSTS)
                        for c in range(8):
                            if c >= 2:
                                pool.wait_ge(rec_out[c % 2], 16 * (c // 2))
                            for col, table in ((C_SRC, src_f), (C_HI, hi_f), (C_LO, lo_f), (C_DST, dst_f)):
                                last = g.tensor_copy(rec[:, c % 2, :, col], table[:, c * QC:(c + 1) * QC])
                            last.then_inc(cols_set, 1)
                        g.memset(keep_one[:], 1.0).then_inc(pool_chain, 1)
                        pool.wait_ge(pool_chain, 8)
                        pool.dma_start(keep_d.rearrange("(p r) o -> p (r o)", p=P), keep_one[:]).then_inc(flags_out, 16)
                        pool.wait_ge(flags_out, 16)
                        pool.wait_ge(own_idx, 1)
                        for b in range(NB):
                            pool.indirect_dma_start(keep_d, bass.IndirectOffsetOnAxis(first_i[:, b:b + 1], 0),
                                                    zero[:, 0:1], None, bounds_check=POS - 1,
                                                    oob_is_err=False).then_inc(flags_out, 16)
                        pool.wait_ge(flags_out, 16 * (NB + 1))

                    @block.scalar
                    def _(act):
                        s = nc.scalar
                        for to, of in ((wm[:], wm12), (bm[:], bm12), (wnet_s[:], w_net), (bnet_c[:], b_net)):
                            act.dma_start(to, of).then_inc(weights_in, 16)
                        act.wait_ge(consts, ALL_CONSTS)
                        for j in range(4):
                            act.dma_start(we_s[W * j:W * j + W, j, :], w_e).then_inc(weights_in, 16)
                        for c in range(8):
                            k = c % 2
                            act.wait_ge(attr_in[k], 16 * (c // 2 + 1))
                            if c >= 2:
                                act.wait_ge(rec_out[k], 16 * (c // 2))
                            s.copy(rec[:, k, :, 0:KA], attr[:, k].rearrange("p (q k) -> p q k", k=KA)).then_inc(attr_set, 1)

                        def keep_tables(b, u, n):
                            act.wait_ge(m_ready, b + 1)
                            s.copy(m1[:, bass.ds(b * F, F)], ps_m[u % 2][:, 0:F])
                            s.copy(m2[:, bass.ds(b * F, F)], ps_m[u % 2][:, F:2 * F]).then_inc(m_taken, 1)
                        pipeline(act, NB, [(0, keep_tables)])

                    @block.vector
                    def _(dve):
                        v = nc.vector
                        ch = Chain(dve, dve_chain)
                        dve.wait_ge(edges_in, 64)
                        v.tensor_single_scalar(hi_i[:], src_i[:], 7, op=ALU.logical_shift_right)
                        ch(v.tensor_single_scalar(lo_i[:], src_i[:], P - 1, op=ALU.bitwise_and))
                        v.tensor_copy(src_f[:], src_i[:]).then_inc(columns, 1)
                        v.tensor_copy(hi_f[:], hi_i[:]).then_inc(columns, 1)
                        v.tensor_copy(lo_f[:], lo_i[:]).then_inc(columns, 1)
                        v.tensor_copy(dst_f[:], dst_i[:]).then_inc(columns, 1)
                        dve.wait_ge(columns, 4)
                        dve.wait_ge(consts, ALL_CONSTS)

                        def onehot(g, u, n):
                            wait(dve, counted, g - 3)
                            now = bass.ds(4 * g, 4)
                            v.tensor_tensor(ohlo[:, u], bcast(lo_f[:, now].unsqueeze(2), P, 4, P),
                                            bcast(iota_b[:].unsqueeze(1), P, 4, P), ALU.is_equal)
                            v.tensor_tensor(ohhi[:, u], bcast(hi_f[:, now].unsqueeze(2), P, 4, HB),
                                            bcast(iota_b[:, 0:HB].unsqueeze(1), P, 4, HB), ALU.is_equal).then_inc(onehots, 1)
                        pipeline(dve, QE // 4, [(0, onehot)])
                        ch(v.tensor_copy(next_f[:], next_i[:]))
                        v.tensor_tensor(drops[:, 1:2], next_f[:, 0:1], dst_f[:, QE - 1:QE], ALU.is_lt)
                        ch(v.tensor_tensor(cmp[:, 0:QE - 1], dst_f[:, 1:QE], dst_f[:, 0:QE - 1], ALU.is_lt))
                        ch(v.tensor_reduce(drops[:, 0:1], cmp[:, 0:QE - 1], AX.X, ALU.add))
                        for b in range(NB + 1):
                            ch(v.tensor_scalar(cmp[:], dst_f[:], float(P * b), 0.0, ALU.is_lt, ALU.add,
                                               accum_out=below[:, b:b + 1]))
                        v.engine_nop().then_inc(to_pe, 1)

                        dve.wait_ge(counted, QE // 4)
                        dve.wait_ge(to_dve, 1)
                        v.memset(cnt[:], 0.0)
                        v.tensor_copy(sd[0:NB, :], ps_a[0:NB, 0:1])
                        v.tensor_copy(unsorted_i[:], ps_a[0:1, 2:3])
                        ch(v.tensor_copy(hist_s[:], ps_hist[:, 0:P]))
                        v.tensor_reduce(cnt[0:NB, 0:1], hist_s[0:NB, :], AX.X, ALU.add)
                        ch(v.tensor_tensor(cnt[0:NB, 1:2], ps_a[0:NB, 1:2], sd[0:NB, :], ALU.subtract))
                        ch(v.tensor_scalar(cnt_i[:], cnt[:], float(P - 1), None, ALU.add))
                        ch(v.tensor_single_scalar(steps_i[:], cnt_i[:], 7, op=ALU.logical_shift_right))
                        ch(v.tensor_copy(steps[:], steps_i[:]))
                        v.engine_nop().then_inc(to_pe, 1)
                        dve.wait_ge(to_dve, 2)
                        ch(v.tensor_copy(pre[:], ps_b[0:HB, 0:2]))
                        ch(v.tensor_tensor(pend[:], pre[:], steps[:], ALU.add))
                        for o in range(2):
                            v.tensor_scalar(ge[:, o], iota_s[0:HB, :], pre[:, o:o + 1], None, ALU.is_ge)
                        ch(v.tensor_scalar(wd[0:NB], pre[0:NB, 1:2], -float(P), -float(E), ALU.mult, ALU.add))
                        for o in range(2):
                            v.scalar_tensor_tensor(out=own[:, o], in0=iota_s[0:HB, :], scalar=pend[:, o:o + 1],
                                                   in1=ge[:, o], op0=ALU.is_lt, op1=ALU.mult)
                        ch(v.tensor_tensor(wd[0:NB], wd[0:NB], sd[0:NB], ALU.add))
                        ch(v.tensor_scalar(val[0:NB], iota_s[0:NB, :], float(P), wd[0:NB, :], ALU.mult, ALU.add))
                        ch(v.tensor_tensor(val[0:NB], val[0:NB], own[0:NB, 1], ALU.mult))
                        ch(v.tensor_tensor_scan(cum[:], one_t[:], hist_s[:], 0.0, ALU.mult, ALU.add))
                        ch(v.tensor_tensor(cum[:], cum[:], hist_s[:], ALU.subtract))
                        ch(v.tensor_scalar(start_t[:], one_t[:], pre[:, 0:1], float(P), ALU.mult, ALU.mult))
                        ch(v.tensor_tensor(start_t[:], start_t[:], cum[:], ALU.add))
                        v.tensor_scalar(rank_r[:, 0], start_t[:], far_c[:], None, ALU.add)
                        v.tensor_scalar(flag[:], hist_s[:], 0.0, None, ALU.is_gt)
                        v.tensor_scalar(fidx[:], hist_s[:], 0.0, FAR, ALU.is_equal, ALU.mult)
                        ch(v.tensor_tensor(end_t[:], start_t[:], hist_s[:], ALU.add))
                        ch(v.tensor_tensor(fidx[:], fidx[:], start_t[:], ALU.add))
                        ch(v.scalar_tensor_tensor(out=lidx[:], in0=end_t[:], scalar=-float(POS + 1), in1=flag[:],
                                                  op0=ALU.add, op1=ALU.mult))
                        v.tensor_scalar(lidx[:], lidx[:], float(POS), None, ALU.add).then_inc(to_pe, 1)
                        dve.wait_ge(to_dve, 3)
                        v.tensor_copy(first_i[:], ps_a[:, 0:HB])
                        v.tensor_copy(last_i[:], ps_a[:, HB:2 * HB]).then_inc(own_idx, 1)
                        for h in range(2):
                            part = slice(h * HN, (h + 1) * HN)
                            one, two = (ps_b, ps_c) if h == 0 else (ps_c, ps_b)
                            dve.wait_ge(to_dve, 4 + 5 * h)
                            v.tensor_scalar(e0_row[:, part], one[0:1, 0:HN], float(E), None, ALU.add).then_inc(to_pe, 1)
                            dve.wait_ge(to_dve, 5 + 5 * h)
                            v.tensor_scalar(sf_row[:, part], two[0:1, 0:HN], float(F), -float(F), ALU.mult, ALU.add).then_inc(to_pe, 1)
                            dve.wait_ge(to_dve, 6 + 5 * h)
                            v.tensor_scalar(db_row[:, part], one[0:1, 0:HN], -1.0, None, ALU.add)
                            v.tensor_scalar(df_row[:, part], one[0:1, 0:HN], float(F), -float(F), ALU.mult, ALU.add)
                            v.tensor_scalar(dd_row[:, part], one[0:1, 0:HN], float(D), -float(D), ALU.mult, ALU.add)
                            v.tensor_scalar(off_s[:, part], one[:, 0:HN], float(P), -float(P), ALU.mult, ALU.add).then_inc(to_pe, 1)
                            dve.wait_ge(to_dve, 7 + 5 * h)
                            v.scalar_tensor_tensor(out=start_s[:, part], in0=iota_s[:, part], scalar=-float(P), in1=two[:, 0:HN],
                                                   op0=ALU.mult, op1=ALU.add).then_inc(to_pe, 1)
                            dve.wait_ge(to_dve, 8 + 5 * h)
                            v.scalar_tensor_tensor(out=end_s[:, part], in0=iota_s[:, part], scalar=-float(P), in1=one[:, 0:HN],
                                                   op0=ALU.mult, op1=ALU.add).then_inc(to_pe, 1)

                    @block.tensor
                    def _(pe):
                        m = nc.tensor

                        def count(g, u, n):
                            pe.wait_ge(onehots, g + 1)
                            static = isinstance(g, int)
                            for j in range(4):
                                mm = m.matmul(ps_hist[:, 0:P], ohhi[:, u, j, :], ohlo[:, u, j, :],
                                              start=(static and g == 0 and j == 0),
                                              stop=(static and g == QE // 4 - 1 and j == 3), skip_group_check=True)
                            mm.then_inc(counted, 1)
                        pipeline(pe, QE // 4, [(0, count)], cool=1)

                        def tables(b, u, n):
                            pe.wait_ge(xt_in[u], 16 * (n + 1))
                            wait(pe, m_taken, b - 1)
                            m.matmul(ps_m[u % 2][:, 0:2 * F], xt[:, u, :], wm[:], start=True, stop=False)
                            m.matmul(ps_m[u % 2][:, 0:2 * F], onesf[0:2, :], bm[:], start=False, stop=True).then_inc(m_ready, 1)
                        pe.wait_ge(consts, ALL_CONSTS)
                        pe.wait_ge(weights_in, 16 * 8)
                        pipeline(pe, NB, [(0, tables)])
                        pe.wait_ge(to_pe, 1)
                        m.matmul(ps_a[0:NB, 0:1], below[:, 0:NB], onesf[:, 0:1], start=True, stop=True)
                        m.matmul(ps_a[0:1, 2:3], drops[:, 0:1], onesf[:, 0:1], start=True, stop=False)
                        m.matmul(ps_a[0:1, 2:3], drops[:, 1:2], onesf[:, 0:1], start=False, stop=True)
                        m.matmul(ps_a[0:NB, 1:2], below[:, 1:NB + 1], onesf[:, 0:1], start=True, stop=True).then_inc(to_dve, 1)
                        pe.wait_ge(to_pe, 2)
                        m.matmul(ps_b[0:HB, 0:2], tri[:], steps[:], start=True, stop=True).then_inc(to_dve, 1)
                        pe.wait_ge(to_pe, 3)
                        m.transpose(ps_a[:, 0:HB], fidx[:], ident[0:HB, 0:HB])
                        m.transpose(ps_a[:, HB:2 * HB], lidx[:], ident[0:HB, 0:HB]).then_inc(to_dve, 1)
                        done = 3
                        for h in range(2):
                            part = slice(h * HN, (h + 1) * HN)
                            for left, right in ((onesf[0:NB, :], val[0:NB, part]),
                                                      (onesf[0:NB, :], ge[0:NB, 0, part]),
                                                      (onesf[0:NB, :], ge[0:NB, 1, part]),
                                                      (start_t[0:NB, :], own[0:NB, 0, part]),
                                                      (end_t[0:NB, :], own[0:NB, 0, part])):
                                if done > 4:
                                    pe.wait_ge(to_pe, done - 1)
                                ps_x = (ps_b, ps_c)[(done - 3) % 2]
                                m.matmul(ps_x[:, 0:HN], left, right, start=True, stop=True).then_inc(to_dve, 1)
                                done += 1

            with ExitStack() as t:
                dst_i = sb(t, "dst_i_s", [P, QE], I32)
                hi_i = sb(t, "hi_i_s", [P, QE], I32)
                lo_i = sb(t, "lo_i_s", [P, QE], I32)
                dst_f = sb(t, "dst_f_s", [P, QE])
                hi_f = sb(t, "hi_f_s", [P, QE])
                lo_f = sb(t, "lo_f_s", [P, QE])
                key = sb(t, "key", [P, 1])
                ohlo = sb(t, "ohlo_s", [P, P], BF16)
                ohhi = sb(t, "ohhi_s", [P, HB], BF16)
                tri = sb(t, "tri_s", [HB, HB])
                hist_s = sb(t, "hist_s_s", [HB, P])
                one_t = sb(t, "one_t_s", [HB, P])
                cum = sb(t, "cum_s", [HB, P])
                free = sb(t, "free_s", [HB, P])
                hiT = sb(t, "hiT_s", [HB, P])
                junk = sb(t, "junk_s", [P, P], BF16)
                junk2 = sb(t, "junk2_s", [P, P], BF16)
                within = sb(t, "within_s", [P, 1])
                across = sb(t, "across_s", [P, 1])
                place = sb(t, "place_s", [P, 1], I32)
                rec = sb(t, "rec_s", [P, W])
                ps_hist = ps(t, "ps_hist_s", [HB, 512])
                ps_first = ps(t, "ps_first", [HB, 512])
                ps_row = ps(t, "ps_row_s", [P, 512])
                ps_hi = ps(t, "ps_hi_s", [P, 1024], BF16)
                ps_cnt = ps(t, "ps_cnt_s", [P, 512])
                ps_new = ps(t, "ps_new_s", [HB, 512])
                dst_in = sem(t, "dst_in")
                tri_ready = sem(t, "tri_ready")
                sort_chain = sem(t, "sort_chain")
                one_hot = sem(t, "one_hot")
                summed = sem(t, "summed")
                totals = sem(t, "totals")
                firsts = sem(t, "firsts")
                free_ready = sem(t, "free_ready")
                keyed = sem(t, "keyed")
                turned = sem(t, "turned")
                hiT_ready = sem(t, "hiT_ready_s")
                ranked = sem(t, "ranked")
                placed = sem(t, "placed")
                rec_read = sem(t, "rec_read")
                rec_moved = sem(t, "rec_moved")
                copied = sem(t, "copied")
                place_chain_s = sem(t, "place_chain_s")
                passed = sem(t, "passed_s")
                passed_pe = sem(t, "passed_pe_s")

                def edges_unsorted(eng):
                    return eng.If(eng.value_load(unsorted_i[0:1, 0:1], min_val=0, max_val=EP) > 0)

                with nc.Block() as block:
                    @block.sync
                    def _(sp):
                        with edges_unsorted(sp):
                            sp.dma_start(dst_i[:], dst.rearrange("(p q) -> p q", p=P)).then_inc(dst_in, 16)
                            columns = rec_d.rearrange("(p q) w -> p q w", p=P)

                            def load(q, u, n):
                                wait(sp, rec_moved, 16 * q)
                                sp.dma_start(rec[:], columns[:, bass.ds(q, 1), :].rearrange("p a w -> p (a w)")).then_inc(rec_read, 16)
                            pipeline(sp, QE, [(0, load)])
                            sp.wait_ge(rec_moved, 16 * QE)
                            for c in range(8):
                                part = slice(c * P * QC, (c + 1) * P * QC)
                                sp.dma_start(rec_d[part, :], moved_d[part, :]).then_inc(copied, 16)
                            sp.wait_ge(copied, 16 * 8)

                    @block.gpsimd
                    def _(pool):
                        with edges_unsorted(pool):
                            nc.gpsimd.memset(one_t[:], 1.0).then_inc(tri_ready, 1)
                            nc.gpsimd.memset(tri[:], 1.0).then_inc(tri_ready, 1)
                            pool.wait_ge(tri_ready, 2)
                            nc.gpsimd.affine_select(out=tri[:], in_=tri[:], compare_op=ALU.is_gt, fill=0.0,
                                                    base=0, pattern=[[1, HB]], channel_multiplier=-1).then_inc(tri_ready, 1)

                            def move(q, u, n):
                                pool.wait_ge(placed, q + 1)
                                pool.wait_ge(rec_read, 16 * (q + 1))
                                pass_waits(pool, passed)
                                pool.indirect_dma_start(moved_d, bass.IndirectOffsetOnAxis(place[:, 0:1], 0),
                                                        rec[:], None).then_inc(rec_moved, 16)
                            pipeline(pool, QE, [(0, move)])
                            pool.wait_ge(rec_moved, 16 * QE)

                    @block.vector
                    def _(dve):
                        with edges_unsorted(dve):
                            v = nc.vector
                            ch = Chain(dve, sort_chain)
                            dve.wait_ge(dst_in, 16)
                            v.tensor_single_scalar(hi_i[:], dst_i[:], 7, op=ALU.logical_shift_right)
                            ch(v.tensor_single_scalar(lo_i[:], dst_i[:], P - 1, op=ALU.bitwise_and))
                            v.tensor_copy(hi_f[:], hi_i[:])
                            v.tensor_copy(lo_f[:], lo_i[:])
                            ch(v.tensor_copy(dst_f[:], dst_i[:]))

                            def onehot(q):
                                now = bass.ds(q, 1)
                                v.tensor_scalar(ohlo[:], iota_b[:], lo_f[:, now], None, ALU.is_equal)
                                v.tensor_scalar(ohhi[:], iota_b[:, 0:HB], hi_f[:, now], None, ALU.is_equal).then_inc(one_hot, 1)

                            def count(q, u, n):
                                wait(dve, summed, q)
                                onehot(q)
                            pipeline(dve, QE, [(0, count)])
                            dve.wait_ge(summed, QE)
                            dve.wait_ge(tri_ready, 3)
                            ch(v.tensor_copy(hist_s[:], ps_hist[:, 0:P]))
                            v.tensor_tensor_scan(cum[:], one_t[:], hist_s[:], 0.0, ALU.mult, ALU.add).then_inc(totals, 1)
                            dve.wait_ge(firsts, 1)
                            dve.wait_ge(totals, 1)
                            ch(v.tensor_tensor(cum[:], cum[:], hist_s[:], ALU.subtract))
                            v.scalar_tensor_tensor(out=free[:], in0=one_t[:], scalar=ps_first[:, 0:1], in1=cum[:],
                                                   op0=ALU.mult, op1=ALU.add).then_inc(free_ready, 1)
                            places = Chain(dve, place_chain_s, 2)

                            def rank(q, u, n):
                                places.turn(q)
                                wait(dve, ranked, q)
                                wait(dve, rec_moved, 16 * q)
                                v.tensor_copy(key[:], dst_f[:, bass.ds(q, 1)]).then_inc(keyed, 1)
                                onehot(q)
                                dve.wait_ge(ranked, q + 1)
                                dve.wait_ge(keyed, q + 1)
                                places.add(v.scalar_tensor_tensor(out=junk[:], in0=ps_row[:, 0:P], scalar=key[:],
                                                                  in1=before[:, 3 * P:4 * P], op0=ALU.is_equal, op1=ALU.mult,
                                                                  accum_out=within[:]))
                                places.add(v.tensor_tensor_reduce(junk2[:], ps_cnt[:, 0:P], ohlo[:], 1.0, 0.0,
                                                                  ALU.mult, ALU.add, across[:]))
                                v.tensor_tensor(free[:], free[:], ps_new[:, 0:P], ALU.add).then_inc(free_ready, 1)
                                places.settle()
                                v.tensor_tensor(place[:], within[:], across[:], ALU.add).then_inc(placed, 1)
                                dve.wait_ge(free_ready, q + 2)
                            pipeline(dve, QE, [(0, rank)])

                    @block.tensor
                    def _(pe):
                        with edges_unsorted(pe):
                            m = nc.tensor

                            def count(q, u, n):
                                pe.wait_ge(one_hot, q + 1)
                                m.matmul(ps_hist[:, 0:P], ohhi[:], ohlo[:], start=(isinstance(q, int) and q == 0),
                                         stop=(isinstance(q, int) and q == QE - 1), skip_group_check=True).then_inc(summed, 1)
                            pipeline(pe, QE, [(0, count)], cool=1)
                            pe.wait_ge(totals, 1)
                            m.matmul(ps_first[:, 0:1], tri[:], cum[:, P - 1:P], start=True, stop=True).then_inc(firsts, 1)

                            def rank(q, u, n):
                                pe.wait_ge(keyed, q + 1)
                                m.transpose(ps_row[:, 0:P], key[:].broadcast_to([P, P]), ident[:])
                                pe.wait_ge(one_hot, QE + q + 1)
                                pass_waits(pe, passed_pe)
                                m.transpose(ps_hi[0:HB, 0:P], ohhi[:], identb[:]).then_inc(turned, 1)
                                m.matmul(ps_new[:, 0:P], ohhi[:], ohlo[:], start=True, stop=True)
                                pe.wait_ge(hiT_ready, q + 1)
                                pe.wait_ge(free_ready, q + 1)
                                m.matmul(ps_cnt[:, 0:P], hiT[:], free[:], start=True, stop=True).then_inc(ranked, 1)
                            pipeline(pe, QE, [(0, rank)])

                    @block.scalar
                    def _(act):
                        with edges_unsorted(act):
                            def copy(q, u, n):
                                act.wait_ge(turned, q + 1)
                                wait(act, ranked, q)
                                nc.scalar.copy(hiT[:], ps_hi[0:HB, 0:P]).then_inc(hiT_ready, 1)
                            pipeline(act, QE, [(0, copy)])

            with ExitStack() as t:
                rec = sb(t, "rec_in", [P, 4, 4, W])
                inv = sb(t, "inv", [P, 4, 4])
                srcm = sb(t, "srcm", [P, 4, 4])
                him = sb(t, "him", [P, 4, 4])
                ohlo = sb(t, "ohlo_a", [P, 4, 4, P], BF16)
                ohhi = sb(t, "ohhi_a", [P, 4, 4, HB], BF16)
                ohd = sb(t, "ohd_a", [P, 4, 4, P], BF16)
                hiT = sb(t, "hiT", [HB, 2, 4, P])
                dstT = sb(t, "dstT", [P, 2, 4, P])
                recT = sb(t, "recT", [P, 2, P])
                junk = sb(t, "junk", [P, 4, 4 * P], BF16)
                junk2 = sb(t, "junk2", [P, 4, P], BF16)
                within = sb(t, "within", [P, 2, 4])
                across = sb(t, "across", [P, 2, 4])
                place = sb(t, "place", [P, 4, 4], I32)
                ur = sb(t, "u", [P, 4, 4, F])
                ps_row = [ps(t, f"ps_row{k}", [P, 512]) for k in range(2)]
                ps_cnt = [ps(t, f"ps_cnt{k}", [P, 4, P]) for k in range(2)]
                ps_rec = ps(t, "ps_rec", [P, 512])
                ps_oh = ps(t, "ps_oh", [P, 2, 512], BF16)
                ps_new = ps(t, "ps_new", [HB, 512])
                ps_u_bank = ps(t, "ps_u", [P, 512])
                ps_u = ps_u_bank[:, 0:4 * F].rearrange("p (j f) -> p j f", j=4)
                rec_in = [sem(t, f"rec_in{k}") for k in range(4)]
                oh_ready = sem(t, "oh_ready")
                key_chain = sem(t, "key_chain")
                rec_turned = sem(t, "rec_turned")
                rows_ready = sem(t, "rows_ready")
                oh_turned = sem(t, "oh_turned")
                recT_ready = sem(t, "recT_ready")
                ohT_ready = sem(t, "ohT_ready")
                new_ready = sem(t, "new_ready")
                cnt_ready = sem(t, "cnt_ready")
                place_chain = sem(t, "place_chain")
                place_ready = sem(t, "place_ready")
                next_ready = sem(t, "next_ready")
                sum_ready = sem(t, "sum_ready")
                u_ready = sem(t, "u_ready")
                sent = [sem(t, f"sent{k}") for k in range(4)]
                passed = sem(t, "passed_a")
                passed_pe = sem(t, "passed_pe")

                with nc.Block() as block:
                    @block.sync
                    def _(sp):
                        def load(i, u, n):
                            wait(sp, oh_ready, i - 3)
                            wait(sp, rec_turned, i - 3)
                            for j in range(4):
                                e0 = sp.value_load(e0_row[0:1, bass.ds(4 * i + j, 1)], min_val=0, max_val=E)
                                sp.dma_start(rec[:, u, j, :], rec_d[bass.ds(e0, P), :]).then_inc(rec_in[u], 16)
                        pipeline(sp, G, [(0, load)])

                    @block.gpsimd
                    def _(pool):
                        def send(i, u, n):
                            pool.wait_ge(place_ready, i + 1)
                            pool.wait_ge(u_ready, i + 1)
                            pass_waits(pool, passed)
                            for j in range(4):
                                pool.indirect_dma_start(u_d, bass.IndirectOffsetOnAxis(place[:, u, j:j + 1], 0),
                                                        ur[:, u, j, :], None, bounds_check=POS - 1,
                                                        oob_is_err=False).then_inc(sent[u], 16)
                        pipeline(pool, G, [(0, send)])
                        for k in range(4):
                            pool.wait_ge(sent[k], 64 * len(range(k, G, 4)))

                    @block.vector
                    def _(dve):
                        v = nc.vector
                        keys = Chain(dve, key_chain, 5)
                        places = Chain(dve, place_chain, 8)

                        def advance(i, u, n):
                            dve.wait_ge(new_ready, i + 1)
                            wait(dve, cnt_ready, i - 2)
                            wait(dve, next_ready, i)
                            v.tensor_tensor(rank_r[:, (u + 1) % 4], rank_r[:, u], ps_new[:, 0:P], ALU.add).then_inc(next_ready, 1)

                        def onehot(i, u, n):
                            dve.wait_ge(rec_in[u], 64 * (n + 1))
                            wait(dve, oh_turned, i - 3)
                            wait(dve, new_ready, i - 3)
                            wait(dve, rows_ready, i - 3)
                            keys.turn(i)
                            now = bass.ds(4 * i, 4)
                            keys.add(v.tensor_tensor(dloc_s[:, now], rec[:, u, :, C_DST], off_s[:, now], ALU.subtract))
                            v.tensor_tensor(ohlo[:, u], bcast(rec[:, u, :, C_LO:C_LO + 1], P, 4, P),
                                            bcast(iota_b[:].unsqueeze(1), P, 4, P), ALU.is_equal)
                            keys.settle()
                            keys.add(v.tensor_scalar(inv[:, u], dloc_s[:, now], float(P), None, ALU.is_ge))
                            v.tensor_tensor(ohd[:, u], bcast(dloc_s[:, now].unsqueeze(2), P, 4, P),
                                            bcast(iota_b[:].unsqueeze(1), P, 4, P), ALU.is_equal)
                            keys.settle()
                            keys.add(v.scalar_tensor_tensor(out=him[:, u], in0=inv[:, u], scalar=float(HB - 1), in1=rec[:, u, :, C_HI],
                                                            op0=ALU.mult, op1=ALU.max))
                            keys.add(v.scalar_tensor_tensor(out=srcm[:, u], in0=inv[:, u], scalar=65536.0, in1=rec[:, u, :, C_SRC],
                                                            op0=ALU.mult, op1=ALU.add))
                            keys.add(v.tensor_scalar(src_s[:, now], rec[:, u, :, C_SRC], float(NP - 1), None, ALU.min))
                            keys.settle()
                            v.tensor_tensor(ohhi[:, u], bcast(him[:, u].unsqueeze(2), P, 4, HB),
                                            bcast(iota_b[:, 0:HB].unsqueeze(1), P, 4, HB), ALU.is_equal).then_inc(oh_ready, 1)

                        def rank(i, u, n):
                            k = u % 2
                            places.turn(i)
                            dve.wait_ge(rows_ready, i + 1)
                            for j in range(4):
                                places.add(v.scalar_tensor_tensor(
                                    out=junk[:, j, 0:P * (j + 1)], in0=ps_row[k][:, 0:P * (j + 1)], scalar=srcm[:, u, j:j + 1],
                                    in1=before[:, P * (3 - j):4 * P], op0=ALU.is_equal, op1=ALU.mult,
                                    accum_out=within[:, k, j:j + 1]))
                            dve.wait_ge(cnt_ready, i + 1)
                            for j in range(4):
                                places.add(v.tensor_tensor_reduce(junk2[:, j, :], ps_cnt[k][:, j, :], ohlo[:, u, j, :], 1.0, 0.0,
                                                                  ALU.mult, ALU.add, across[:, k, j:j + 1]))
                            s4, n4 = past(sent, u, n, 4)
                            wait(dve, s4, 64 * n4)
                            places.settle()
                            v.tensor_tensor(place[:, u], within[:, k], across[:, k], ALU.add).then_inc(place_ready, 1)
                        pipeline(dve, G, [(1, advance), (0, onehot), (2, rank)])

                    @block.tensor
                    def _(pe):
                        m = nc.tensor

                        def count(i, u, n):
                            k = u % 2
                            pe.wait_ge(ohT_ready, i + 1)
                            wait(pe, next_ready, i)
                            wait(pe, place_chain, 8 * (i - 1))
                            for j in range(4):
                                mm = m.matmul(ps_cnt[k][:, j, :], hiT[:, k, j, :], rank_r[:, u, :], start=True, stop=True)
                            mm.then_inc(cnt_ready, 1)
                            for j in range(4):
                                mm = m.transpose(ps_row[k][:, P * j:P * j + P], srcm[:, u, j:j + 1].broadcast_to([P, P]), ident[:])
                            mm.then_inc(rows_ready, 1)

                        def turn(i, u, n):
                            pe.wait_ge(rec_in[u], 64 * (n + 1))
                            wait(pe, recT_ready, i)
                            m.transpose(ps_rec[:, 0:P], rec[:, u].rearrange("p j w -> p (j w)"), ident[:]).then_inc(rec_turned, 1)
                            pe.wait_ge(oh_ready, i + 1)
                            wait(pe, next_ready, i)
                            for j in range(4):
                                mm = m.matmul(ps_new[:, 0:P], ohhi[:, u, j, :], ohlo[:, u, j, :], start=(j == 0), stop=(j == 3))
                            mm.then_inc(new_ready, 1)
                            wait(pe, ohT_ready, i)
                            pass_waits(pe, passed_pe)
                            for j in range(4):
                                m.transpose(ps_oh[0:HB, 0, P * j:P * j + P], ohhi[:, u, j, :], identb[:])
                            for j in range(4):
                                mm = m.transpose(ps_oh[:, 1, P * j:P * j + P], ohd[:, u, j, :], identb[:])
                            mm.then_inc(oh_turned, 1)

                        def product(i, u, n):
                            k = u % 2
                            pe.wait_ge(recT_ready, i + 1)
                            wait(pe, u_ready, i)
                            m.matmul(ps_u.rearrange("p j f -> p (j f)"), recT[:, k, :], we_s[:].rearrange("p j f -> p (j f)"),
                                     start=True, stop=False, skip_group_check=True)
                            at = offsets(nc, mybir.EngineType.PE, df_row[0:1, bass.ds(4 * i, 4)], NB * F - F)
                            for j in range(4):
                                mm = m.matmul(ps_u[:, j, :], dstT[:, k, j, :], m2[:, bass.ds(at[j], F)],
                                              start=False, stop=True, skip_group_check=True)
                            mm.then_inc(sum_ready, 1)
                        pipeline(pe, G, [(1, count), (0, turn), (1, product)])

                    @block.scalar
                    def _(act):
                        s = nc.scalar

                        def rows(i, u, n):
                            act.wait_ge(sum_ready, i + 1)
                            s4, n4 = past(sent, u, n, 4)
                            wait(act, s4, 64 * n4)
                            s.copy(ur[:, u], ps_u).then_inc(u_ready, 1)

                        def turned(i, u, n):
                            k = u % 2
                            act.wait_ge(rec_turned, i + 1)
                            wait(act, sum_ready, i - 1)
                            s.copy(recT[:, k, :], ps_rec[:, 0:P]).then_inc(recT_ready, 1)
                            act.wait_ge(oh_turned, i + 1)
                            wait(act, cnt_ready, i - 1)
                            s.copy(hiT[:, k].rearrange("p j e -> p (j e)"), ps_oh[0:HB, 0, :])
                            s.copy(dstT[:, k].rearrange("p j e -> p (j e)"), ps_oh[:, 1, :]).then_inc(ohT_ready, 1)
                        pipeline(act, G, [(2, rows), (0, turned)])

            with ExitStack() as t:
                u_in_s = sb(t, "u_in", [P, 4, 4, F])
                keep = sb(t, "keep", [1, 4, 4 * P])
                after = sb(t, "after", [P, 4, 4, P])
                oh = sb(t, "oh_b", [P, 4, 4, P])
                m1_s = sb(t, "m1_s", [P, 4, 4, F])
                msg = sb(t, "msg", [F, 2, 4 * P])
                msg2 = sb(t, "msg2", [F, 2, 4 * P])
                top = sb(t, "top", [F, 4, 4 * P])
                row = sb(t, "row", [P, 4, 4, F])
                ps_pre = [ps(t, f"ps_pre{k}", [F, 512]) for k in range(2)]
                ps_net = [ps(t, f"ps_net{k}", [F, 512]) for k in range(2)]
                ps_keep = [ps(t, f"ps_keep{k}", [F, 512]) for k in range(2)]
                ps_top = [ps(t, f"ps_top{k}", [P, 4, P]) for k in range(2)]
                u_in = [sem(t, f"u_in{k}") for k in range(4)]
                keep_in = [sem(t, f"keep_in{k}") for k in range(4)]
                m1_ready = sem(t, "m1_ready")
                oh_ready = sem(t, "oh_ready_b")
                after_ready = sem(t, "after_ready")
                pre_ready = sem(t, "pre_ready")
                msg_ready = sem(t, "msg_ready")
                net_ready = sem(t, "net_ready")
                msg2_ready = sem(t, "msg2_ready")
                top_ready = sem(t, "top_ready")
                top_turned = sem(t, "top_turned")
                row_ready = sem(t, "row_ready")
                row_out = [sem(t, f"row_out{k}") for k in range(4)]
                passed = sem(t, "passed_b")
                passed_pool = sem(t, "passed_pool")
                with nc.Block() as block:
                    @block.sync
                    def _(sp):
                        def load(i, u, n):
                            wait(sp, pre_ready, i - 3)
                            sp.dma_start(u_in_s[:, u], u_d[bass.ds(4 * P * i, 4 * P), :].rearrange("(j p) f -> p j f", p=P)).then_inc(u_in[u], 16)
                            wait(sp, net_ready, i - 3)
                            pass_waits(sp, passed)
                            sp.dma_start(keep[:, u, :], keep_d[bass.ds(4 * P * i, 4 * P), :].rearrange("r o -> o r")).then_inc(keep_in[u], 16)

                        def store(i, u, n):
                            sp.wait_ge(row_ready, i + 1)
                            sp.dma_start(s_d[bass.ds(4 * P * i, 4 * P), :].rearrange("(j p) f -> p j f", p=P), row[:, u]).then_inc(row_out[u], 16)
                        pipeline(sp, G, [(5, store), (0, load)])
                        for k in range(4):
                            sp.wait_ge(row_out[k], 16 * len(range(k, G, 4)))

                    @block.gpsimd
                    def _(pool):
                        def stage(i, u, n):
                            wait(pool, pre_ready, i - 3)
                            pass_waits(pool, passed_pool)
                            at = offsets(nc, mybir.EngineType.Pool, sf_row[0:1, bass.ds(4 * i, 4)], NB * F - F)
                            for j in range(4):
                                last = nc.gpsimd.tensor_copy(m1_s[:, u, j, :], m1[:, bass.ds(at[j], F)])
                            last.then_inc(m1_ready, 1)
                        pipeline(pool, G, [(0, stage)])

                    @block.vector
                    def _(dve):
                        v = nc.vector

                        def onehot(i, u, n):
                            wait(dve, pre_ready, i - 3)
                            now = bass.ds(4 * i, 4)
                            v.tensor_tensor(after[:, u], bcast(iota_f[:].unsqueeze(1), P, 4, P),
                                            bcast(start_s[:, now].unsqueeze(2), P, 4, P), ALU.is_ge).then_inc(after_ready, 1)
                            dve.wait_ge(after_ready, i + 1)
                            for j in range(4):
                                last = v.scalar_tensor_tensor(out=oh[:, u, j, :], in0=iota_f[:], scalar=end_s[:, bass.ds(4 * i + j, 1)],
                                                              in1=after[:, u, j, :], op0=ALU.is_lt, op1=ALU.mult)
                            last.then_inc(oh_ready, 1)

                        def scan(i, u, n):
                            k = u % 2
                            dve.wait_ge(msg2_ready, i + 1)
                            wait(dve, top_turned, i - 3)
                            wait(dve, top_ready, i)
                            first = isinstance(i, int) and i == 0
                            v.tensor_tensor_scan(top[:, u, :], ps_keep[k][:], msg2[:, k, :],
                                                 0.0 if first else top[:, (u - 1) % 4, 4 * P - 1:4 * P],
                                                 ALU.mult, ALU.max).then_inc(top_ready, 1)
                        pipeline(dve, G, [(3, scan), (0, onehot)])

                    @block.tensor
                    def _(pe):
                        m = nc.tensor

                        def pre(i, u, n):
                            pe.wait_ge(u_in[u], 16 * (n + 1))
                            wait(pe, msg_ready, i - 1)
                            pe.wait_ge(oh_ready, i + 1)
                            pe.wait_ge(m1_ready, i + 1)
                            for j in range(4):
                                to = ps_pre[u % 2][:, P * j:P * j + P]
                                m.matmul(to, u_in_s[:, u, j, :], ident[:], start=True, stop=False)
                                mm = m.matmul(to, m1_s[:, u, j, :], oh[:, u, j, :], start=False, stop=True)
                            mm.then_inc(pre_ready, 1)

                        def net(i, u, n):
                            k = u % 2
                            wait(pe, top_ready, i - 1)
                            pe.wait_ge(keep_in[u], 16 * (n + 1))
                            flags = keep[:, u, :].bitcast(BF16).rearrange("o (r h) -> o r h", h=2)[:, :, 1]
                            m.matmul(ps_keep[k][:], onesb[0:1, 0:F], flags, start=True, stop=True)
                            pe.wait_ge(msg_ready, i + 1)
                            m.matmul(ps_net[k][:], wnet_s[:], msg[:, k, :], start=True, stop=True).then_inc(net_ready, 1)

                        def turn(i, u, n):
                            pe.wait_ge(top_ready, i + 1)
                            wait(pe, row_ready, i - 1)
                            for j in range(4):
                                mm = m.transpose(ps_top[u % 2][:, j, 0:F], top[:, u, P * j:P * j + P], ident[0:F, 0:F])
                            mm.then_inc(top_turned, 1)
                        pipeline(pe, G, [(2, net), (4, turn), (1, pre)])

                    @block.scalar
                    def _(act):
                        s = nc.scalar

                        def first(i, u, n):
                            k = u % 2
                            act.wait_ge(pre_ready, i + 1)
                            wait(act, net_ready, i - 1)
                            s.activation(msg[:, k, :], ps_pre[k][:], ACT.Relu).then_inc(msg_ready, 1)

                        def second(i, u, n):
                            k = u % 2
                            act.wait_ge(net_ready, i + 1)
                            wait(act, top_ready, i - 1)
                            s.activation(msg2[:, k, :], ps_net[k][:], ACT.Relu, bias=bnet_c[:]).then_inc(msg2_ready, 1)

                        def rows(i, u, n):
                            act.wait_ge(top_turned, i + 1)
                            s4, n4 = past(row_out, u, n, 4)
                            wait(act, s4, 16 * n4)
                            s.copy(row[:, u], ps_top[u % 2][:, :, 0:F]).then_inc(row_ready, 1)
                        pipeline(act, G, [(2, second), (4, rows), (1, first)])

        layer1 = ExitStack()
        with layer1:
            x1 = sb(layer1, "x1", [P, NB, D])
            x1T = sb(layer1, "x1T", [D, NP])
            hsumT = sb(layer1, "hsumT", [D, NP])
            deg = sb(layer1, "deg", [P, NB])
            bpart = sb(layer1, "bpart", [P, NB * D])
            with ExitStack() as t:
                agg_all = sb(t, "agg_all", [P, NB, F])
                aggT = sb(t, "aggT", [F, 2, P])
                xt = sb(t, "xt_n", [P, 4, P])
                xr = sb(t, "xr", [P, 4, D])
                stats = sb(t, "stats", [P, NB, 6])
                mv = sb(t, "mv", [P, NB, 2])
                std = sb(t, "std", [P, NB])
                rstd = sb(t, "rstd", [P, NB])
                arow = sb(t, "arow", [P, 4, D])
                wo1_s = sb(t, "wo1_s", [D, D])
                wo2_s = sb(t, "wo2_s", [F, D])
                bo_s = sb(t, "bo_s", [2, D])
                ew1_s = sb(t, "ew1_s", [D, 2 * D])
                eb1_s = sb(t, "eb1_s", [1, 2 * D])
                eps_c = sb(t, "eps_c", [P, 1])
                ps_t = [ps(t, f"ps_t{k}", [P, 512]) for k in range(2)]
                ps_y = [ps(t, f"ps_y{k}", [P, 512]) for k in range(2)]
                ps_x = [ps(t, f"ps_x{k}", [P, 512]) for k in range(2)]
                ps_ab = [ps(t, f"ps_ab{k}", [P, 512]) for k in range(2)]
                agg_in = sem(t, "agg_in")
                w_in = sem(t, "w_in")
                x_in = [sem(t, f"x_in{k}") for k in range(4)]
                eps_set = sem(t, "eps_set")
                agg_turned = sem(t, "agg_turned")
                aggT_ready = sem(t, "aggT_ready")
                y_ready = sem(t, "y_ready")
                sum_chain = sem(t, "sum_chain")
                std_ready = sem(t, "std_ready")
                r_ready = sem(t, "r_ready_a")
                x1_ready = sem(t, "x1_ready")
                x1_turned = sem(t, "x1_turned")
                x1T_ready = sem(t, "x1T_ready")
                ab_ready = sem(t, "ab_ready")
                a_ready = sem(t, "a_ready")
                b_ready = sem(t, "b_ready")
                a_out = [sem(t, f"a_out{k}") for k in range(4)]
                with nc.Block() as block:
                    @block.gpsimd
                    def _(pool):
                        nc.gpsimd.memset(eps_c[:], EPS_LN).then_inc(eps_set, 1)
                        for b in range(NB):
                            pool.indirect_dma_start(agg_all[:, b, :], None, s_d,
                                                    bass.IndirectOffsetOnAxis(last_i[:, b:b + 1], 0)).then_inc(agg_in, 16)
                        nc.gpsimd.memset(hsumT[:], 0.0).then_inc(eps_set, 1)
                        nc.gpsimd.memset(deg[:], 0.0).then_inc(eps_set, 1)
                        pool.wait_ge(agg_in, 16 * NB)

                    @block.sync
                    def _(sp):
                        for to, of in ((wo1_s[:], wo1), (wo2_s[:], wo2), (bo_s[:], bo), (ew1_s[:, 0:D], ew1a),
                                       (ew1_s[:, D:2 * D], ew1b), (eb1_s[:], eb1)):
                            sp.dma_start(to, of).then_inc(w_in, 16)

                        def load(b, u, n):
                            wait(sp, y_ready, b - 3)
                            sp.dma_start(xt[:, u, :], xT[:, bass.ds(P * b, P)]).then_inc(x_in[u], 16)
                            wait(sp, sum_chain, 3 * (b - 3))
                            sp.dma_start(xr[:, u, :], x[bass.ds(P * b, P), :]).then_inc(x_in[u], 16)
                        pipeline(sp, NB, [(0, load)])

                        def store(b, u, n):
                            sp.wait_ge(a_ready, b + 1)
                            sp.dma_start(a_d[bass.ds(P * b, P), :], arow[:, u, :]).then_inc(a_out[u], 16)
                        pipeline(sp, NB, [(0, store)])
                        for k in range(4):
                            sp.wait_ge(a_out[k], 16 * len(range(k, NB, 4)))

                    @block.scalar
                    def _(act):
                        s = nc.scalar

                        def aggregate(b, u, n):
                            act.wait_ge(agg_turned, b + 1)
                            wait(act, y_ready, b - 1)
                            s.copy(aggT[:, u % 2, :], ps_t[u % 2][0:F, 0:P]).then_inc(aggT_ready, 1)
                        pipeline(act, NB, [(0, aggregate)])
                        act.wait_ge(sum_chain, 3 * NB)
                        act.wait_ge(eps_set, 1)
                        s.activation(std[:], mv[:, :, 1], ACT.Sqrt, bias=eps_c[:]).then_inc(std_ready, 1)

                        def tables(b, u, n):
                            act.wait_ge(ab_ready, b + 1)
                            s4, n4 = past(a_out, u, n, 4)
                            wait(act, s4, 16 * n4)
                            s.copy(arow[:, u, :], ps_ab[u % 2][:, 0:D]).then_inc(a_ready, 1)
                            s.copy(bpart[:, bass.ds(b * D, D)], ps_ab[u % 2][:, D:2 * D]).then_inc(b_ready, 1)

                        def turned(b, u, n):
                            act.wait_ge(x1_turned, b + 1)
                            s.copy(x1T[:, bass.ds(P * b, P)], ps_x[u % 2][:, 0:P]).then_inc(x1T_ready, 1)
                        pipeline(act, NB, [(1, tables), (0, turned)])

                    @block.tensor
                    def _(pe):
                        m = nc.tensor
                        pe.wait_ge(w_in, 16 * 6)

                        def update(b, u, n):
                            k = u % 2
                            pe.wait_ge(x_in[u], 32 * (n + 1))
                            wait(pe, sum_chain, 3 * (b - 1))
                            m.matmul(ps_y[k][:, 0:D], xt[:, u, :], wo1_s[:], start=True, stop=False)
                            m.matmul(ps_y[k][:, 0:D], onesf[0:2, :], bo_s[:], start=False, stop=False)
                            pe.wait_ge(aggT_ready, b + 1)
                            m.matmul(ps_y[k][:, 0:D], aggT[:, k, :], wo2_s[:], start=False, stop=True).then_inc(y_ready, 1)
                        for b in range(NB + 1):
                            if b < NB:
                                if b < 1:
                                    pe.wait_ge(agg_in, 16 * NB)
                                wait(pe, aggT_ready, b - 1)
                                m.transpose(ps_t[b % 2][0:F, 0:P], agg_all[:, b, :], ident[:]).then_inc(agg_turned, 1)
                            if b > 0:
                                update(b - 1, (b - 1) % 4, (b - 1) // 4)

                        for b in range(NB + 1):
                            if b < NB:
                                pe.wait_ge(x1_ready, b + 1)
                                wait(pe, x1T_ready, b - 1)
                                m.transpose(ps_x[b % 2][:, 0:P], x1[:, b, :], ident[:]).then_inc(x1_turned, 1)
                            if b > 0:
                                q = b - 1
                                pe.wait_ge(x1T_ready, q + 1)
                                wait(pe, b_ready, q - 1)
                                m.matmul(ps_ab[q % 2][:, 0:2 * D], x1T[:, P * q:P * q + P], ew1_s[:], start=True, stop=False)
                                m.matmul(ps_ab[q % 2][:, 0:2 * D], onesf[0:1, :], eb1_s[:], start=False, stop=True).then_inc(ab_ready, 1)

                    @block.vector
                    def _(dve):
                        v = nc.vector
                        sums = Chain(dve, sum_chain, 3)
                        for b in range(NB):
                            sums.turn(b)
                            dve.wait_ge(x_in[b % 4], 32 * (b // 4 + 1))
                            dve.wait_ge(y_ready, b + 1)
                            sums(v.tensor_tensor(x1[:, b, :], ps_y[b % 2][:, 0:D], xr[:, b % 4, :], ALU.add))
                            sums(v.bn_stats(stats[:, b, :], x1[:, b, :]))
                            sums(v.bn_aggr(mv[:, b, :], stats[:, b, :]))
                        dve.wait_ge(std_ready, 1)
                        v.reciprocal(rstd[:], std[:]).then_inc(r_ready, 1)
                        dve.wait_ge(r_ready, 1)

                        def normed(b, u, n):
                            one = bass.ds(b, 1)
                            xb = x1[:, one, :].rearrange("p a f -> p (a f)")
                            v.tensor_scalar(xb, xb, mv[:, one, 0:1].rearrange("p a f -> p (a f)"), rstd[:, one],
                                            ALU.subtract, ALU.mult).then_inc(x1_ready, 1)
                        pipeline(dve, NB, [(0, normed)])

            with ExitStack() as t:
                idx = sb(t, "idx", [P, 4, 4], I32)
                a_rows = sb(t, "a_rows", [P, 4, 4, D])
                ohd = sb(t, "ohd_f", [P, 4, 4, P])
                dstT = sb(t, "dstT_b", [P, 2, 4, P])
                h = sb(t, "h", [P, 2, 4, D])
                ps_t = [ps(t, f"ps_tt{k}", [P, 512]) for k in range(2)]
                ps_h = [ps(t, f"ps_h{k}", [P, 4, D]) for k in range(2)]
                ps_s = [ps(t, f"ps_s{k}", [D, 4, P]) for k in range(2)]
                ps_n = [ps(t, f"ps_n{k}", [P, 512]) for k in range(2)]
                idx_ready = sem(t, "idx_ready")
                got = [sem(t, f"got{k}") for k in range(4)]
                passed = sem(t, "passed_d")
                oh_ready = sem(t, "oh_ready_c")
                dst_turned = sem(t, "dst_turned_b")
                dstT_ready = sem(t, "dstT_ready_b")
                pre_ready = sem(t, "pre_ready_b")
                h_ready = sem(t, "h_ready")
                sum_ready = sem(t, "sum_ready_b")
                add_chain = sem(t, "add_chain")
                with nc.Block() as block:
                    @block.gpsimd
                    def _(pool):
                        def fetch(i, u, n):
                            pool.wait_ge(idx_ready, i + 1)
                            wait(pool, pre_ready, i - 3)
                            pass_waits(pool, passed)
                            for j in range(4):
                                pool.indirect_dma_start(a_rows[:, u, j, :], None, a_d,
                                                        bass.IndirectOffsetOnAxis(idx[:, u, j:j + 1], 0)).then_inc(got[u], 16)
                        pipeline(pool, G, [(0, fetch)])

                    @block.vector
                    def _(dve):
                        v = nc.vector
                        adds = Chain(dve, add_chain, 8)

                        def add(i, u, n):
                            k = u % 2
                            adds.turn(i)
                            dve.wait_ge(sum_ready, i + 1)
                            to = offsets(nc, mybir.EngineType.DVE, dd_row[0:1, bass.ds(4 * i, 4)], NP - P)
                            of = offsets(nc, mybir.EngineType.DVE, db_row[0:1, bass.ds(4 * i, 4)], NB - 1)
                            for j in range(4):
                                at = hsumT[:, bass.ds(to[j], P)]
                                adds.add(v.tensor_tensor(at, at, ps_s[k][:, j, :], ALU.add))
                                dg = deg[:, bass.ds(of[j], 1)]
                                adds.add(v.tensor_tensor(dg, dg, ps_n[k][:, j:j + 1], ALU.add))
                                adds.settle()

                        def onehot(i, u, n):
                            s4, n4 = past(got, u, n, 4)
                            wait(dve, s4, 64 * n4)
                            now = bass.ds(4 * i, 4)
                            v.tensor_copy(idx[:, u], src_s[:, now]).then_inc(idx_ready, 1)
                            wait(dve, sum_ready, i - 3)
                            v.tensor_tensor(ohd[:, u], bcast(dloc_s[:, now].unsqueeze(2), P, 4, P),
                                            bcast(iota_f[:].unsqueeze(1), P, 4, P), ALU.is_equal).then_inc(oh_ready, 1)
                        pipeline(dve, G, [(0, onehot), (4, add)])

                    @block.tensor
                    def _(pe):
                        m = nc.tensor

                        def turn(i, u, n):
                            pe.wait_ge(oh_ready, i + 1)
                            wait(pe, dstT_ready, i - 1)
                            for j in range(4):
                                mm = m.transpose(ps_t[u % 2][:, P * j:P * j + P], ohd[:, u, j, :], ident[:])
                            mm.then_inc(dst_turned, 1)

                        def pre(i, u, n):
                            k = u % 2
                            pe.wait_ge(got[u], 64 * (n + 1))
                            wait(pe, h_ready, i - 1)
                            m.matmul(ps_h[k][:].rearrange("p j d -> p (j d)"), ident[:], a_rows[:, u].rearrange("p j d -> p (j d)"),
                                     start=True, stop=False, skip_group_check=True)
                            pe.wait_ge(dstT_ready, i + 1)
                            at = offsets(nc, mybir.EngineType.PE, dd_row[0:1, bass.ds(4 * i, 4)], NP - P)
                            for j in range(4):
                                mm = m.matmul(ps_h[k][:, j, :], dstT[:, k, j, :], bpart[:, bass.ds(at[j], D)],
                                              start=False, stop=True, skip_group_check=True)
                            mm.then_inc(pre_ready, 1)

                        def sums(i, u, n):
                            k = u % 2
                            pe.wait_ge(h_ready, i + 1)
                            wait(pe, add_chain, 8 * (i - 1))
                            for j in range(4):
                                m.matmul(ps_s[k][:, j, :], h[:, k, j, :], ohd[:, u, j, :], start=True, stop=True)
                                mm = m.matmul(ps_n[k][:, j:j + 1], ohd[:, u, j, :], onesf[:, 0:1], start=True, stop=True)
                            mm.then_inc(sum_ready, 1)
                        pipeline(pe, G, [(3, sums), (2, pre), (1, turn)])

                    @block.scalar
                    def _(act):
                        s = nc.scalar

                        def turned(i, u, n):
                            k = u % 2
                            act.wait_ge(dst_turned, i + 1)
                            wait(act, pre_ready, i - 1)
                            s.copy(dstT[:, k].rearrange("p j e -> p (j e)"), ps_t[k][:]).then_inc(dstT_ready, 1)

                        def gelu(i, u, n):
                            k = u % 2
                            act.wait_ge(pre_ready, i + 1)
                            wait(act, sum_ready, i - 1)
                            s.activation(h[:, k], ps_h[k][:], ACT.Gelu).then_inc(h_ready, 1)
                        pipeline(act, G, [(2, gelu), (1, turned)])

            with ExitStack() as t:
                diag = sb(t, "diag", [P, 4, P])
                aggd = sb(t, "aggd", [P, 2, P])
                hid = sb(t, "hid", [P, 2, P])
                stats = sb(t, "stats_b", [P, NB, 6])
                mv = sb(t, "mv_b", [P, NB, 2])
                std = sb(t, "std_b", [P, NB])
                rstd = sb(t, "rstd_b", [P, NB])
                yout = sb(t, "yout", [P, NB, D])
                ew2_s = sb(t, "ew2_s", [D, D])
                eb2_s = sb(t, "eb2_s", [P, D])
                nw1a_s = sb(t, "nw1a_s", [D, D])
                nw1b_s = sb(t, "nw1b_s", [D, D])
                nb1_c = sb(t, "nb1_c", [D, 1])
                nw2_s = sb(t, "nw2_s", [D, D])
                nb2_s = sb(t, "nb2_s", [1, D])
                eps_c = sb(t, "eps_d", [P, 1])
                ps_g = [ps(t, f"ps_g{k}", [P, 512]) for k in range(2)]
                ps_k = [ps(t, f"ps_k{k}", [P, 512]) for k in range(2)]
                ps_o = [ps(t, f"ps_o{k}", [P, 512]) for k in range(2)]
                w_in = sem(t, "w_in_b")
                eps_set = sem(t, "eps_set_b")
                diag_ready = sem(t, "diag_ready")
                g_ready = sem(t, "g_ready")
                aggd_ready = sem(t, "aggd_ready")
                k_ready = sem(t, "k_ready")
                hid_ready = sem(t, "hid_ready")
                o_ready = sem(t, "o_ready")
                y_chain = sem(t, "y_chain")
                var_ready = sem(t, "var_ready_b")
                std_ready = sem(t, "std_ready_b")
                r_ready = sem(t, "r_ready")
                out_ready = sem(t, "out_ready")
                stored = sem(t, "stored")
                with nc.Block() as block:
                    @block.gpsimd
                    def _(pool):
                        nc.gpsimd.memset(eps_c[:], EPS_LN).then_inc(eps_set, 1)

                    @block.sync
                    def _(sp):
                        for to, of in ((ew2_s[:], ew2), (eb2_s[:], eb2.broadcast_to([P, D])), (nw1a_s[:], nw1a), (nw1b_s[:], nw1b),
                                       (nb1_c[:], nb1), (nw2_s[:], nw2), (nb2_s[:], nb2)):
                            sp.dma_start(to, of).then_inc(w_in, 16)
                        per = 7
                        count = 0
                        for b in range(0, NB, per):
                            full = min(b + per, N // P)
                            sp.wait_ge(out_ready, min(b + per, NB))
                            if full > b:
                                sp.dma_start(out[P * b:P * full, :].rearrange("(b p) d -> p b d", p=P), yout[:, b:full, :]).then_inc(stored, 16)
                                count += 1
                        if N % P:
                            sp.dma_start(out[P * (N // P):N, :], yout[0:N % P, NB - 1, :]).then_inc(stored, 16)
                            count += 1
                        sp.wait_ge(stored, 16 * count)

                    @block.vector
                    def _(dve):
                        v = nc.vector
                        ych = Chain(dve, y_chain, 3)

                        def diagonal(b, u, n):
                            wait(dve, g_ready, b - 3)
                            v.tensor_scalar(diag[:, u, :], ident[:], deg[:, bass.ds(b, 1)], None, ALU.mult).then_inc(diag_ready, 1)

                        def result(b):
                            ych.turn(b)
                            dve.wait_ge(o_ready, b + 1)
                            ych(v.scalar_tensor_tensor(out=x1[:, b, :], in0=x1[:, b, :], scalar=2.0, in1=ps_o[b % 2][:, 0:D], op0=ALU.mult, op1=ALU.add))
                            ych(v.bn_stats(stats[:, b, :], x1[:, b, :]))
                            ych(v.bn_aggr(mv[:, b, :], stats[:, b, :]))
                        for b in range(NB + 3):
                            if b < NB:
                                diagonal(b, b % 4, b // 4)
                            if b >= 3:
                                result(b - 3)
                        v.engine_nop().then_inc(var_ready, 1)
                        dve.wait_ge(std_ready, 1)
                        v.reciprocal(rstd[:], std[:]).then_inc(r_ready, 1)
                        dve.wait_ge(r_ready, 1)

                        def normed(b, u, n):
                            one = bass.ds(b, 1)
                            v.tensor_scalar(yout[:, one, :].rearrange("p a f -> p (a f)"), x1[:, one, :].rearrange("p a f -> p (a f)"),
                                            mv[:, one, 0:1].rearrange("p a f -> p (a f)"), rstd[:, one], ALU.subtract, ALU.mult).then_inc(out_ready, 1)
                        pipeline(dve, NB, [(0, normed)])

                    @block.tensor
                    def _(pe):
                        m = nc.tensor
                        pe.wait_ge(w_in, 16 * 7)

                        def gather(b, u, n):
                            k = u % 2
                            pe.wait_ge(diag_ready, b + 1)
                            wait(pe, aggd_ready, b - 1)
                            cols = bass.ds(P * b, P)
                            m.matmul(ps_g[k][:, 0:P], ew2_s[:], hsumT[:, cols], start=True, stop=False)
                            m.matmul(ps_g[k][:, 0:P], eb2_s[:], diag[:, u, :], start=False, stop=True).then_inc(g_ready, 1)

                        def hidden(b, u, n):
                            k = u % 2
                            pe.wait_ge(aggd_ready, b + 1)
                            wait(pe, hid_ready, b - 1)
                            m.matmul(ps_k[k][:, 0:P], nw1a_s[:], x1T[:, bass.ds(P * b, P)], start=True, stop=False)
                            m.matmul(ps_k[k][:, 0:P], nw1b_s[:], aggd[:, k, :], start=False, stop=True).then_inc(k_ready, 1)

                        def update(b, u, n):
                            k = u % 2
                            pe.wait_ge(hid_ready, b + 1)
                            wait(pe, y_chain, 3 * (b - 1))
                            m.matmul(ps_o[k][:, 0:D], hid[:, k, :], nw2_s[:], start=True, stop=False)
                            m.matmul(ps_o[k][:, 0:D], onesf[0:1, :], nb2_s[:], start=False, stop=True).then_inc(o_ready, 1)
                        pipeline(pe, NB, [(2, update), (1, hidden), (0, gather)])

                    @block.scalar
                    def _(act):
                        s = nc.scalar
                        act.wait_ge(w_in, 16 * 7)

                        def summed(b, u, n):
                            k = u % 2
                            act.wait_ge(g_ready, b + 1)
                            wait(act, k_ready, b - 1)
                            s.copy(aggd[:, k, :], ps_g[k][:, 0:P]).then_inc(aggd_ready, 1)

                        def gelu(b, u, n):
                            k = u % 2
                            act.wait_ge(k_ready, b + 1)
                            wait(act, o_ready, b - 1)
                            s.activation(hid[:, k, :], ps_k[k][:, 0:P], ACT.Gelu, bias=nb1_c[:]).then_inc(hid_ready, 1)
                        pipeline(act, NB, [(1, gelu), (0, summed)])
                        act.wait_ge(var_ready, 1)
                        act.wait_ge(eps_set, 1)
                        s.activation(std[:], mv[:, :, 1], ACT.Sqrt, bias=eps_c[:]).then_inc(std_ready, 1)


_ARGS = ["x", "xT", "src", "dst", "edge_attr", "wm12", "bm12", "w_e", "w_net", "b_net", "wo1", "wo2", "bo",
         "ew1a", "ew1b", "eb1", "ew2", "eb2", "nw1a", "nw1b", "nb1", "nw2", "nb2"]


def lay_out(i):
    import numpy as np
    a = {k: np.asarray(v) for k, v in i.items()}
    n, e = a["x"].shape[0], a["src"].shape[0]
    nb, q, _ = sizes(n, e)
    rows, edges = nb * P, q * P

    def pad(v, m, fill=0):
        return np.concatenate([v, np.full((m - v.shape[0],) + v.shape[1:], fill, v.dtype)])

    x = pad(a["x"], rows)
    ka = a["edge_attr_16"].shape[1]
    f = a["L0_gnn_W_net"].shape[0]
    d = x.shape[1]
    o = {
        "x": x, "xT": x.T,
        "src": pad(a["src"], edges, rows), "dst": pad(a["dst"], edges, rows),
        "edge_attr": pad(a["edge_attr_16"], edges),
        "wm12": np.concatenate([a["L0_gnn_W_m1"].T, a["L0_gnn_W_m2"].T], 1),
        "bm12": np.stack([np.concatenate([a["L0_gnn_b_m1"], a["L0_gnn_b_m2"]]),
                          np.concatenate([np.zeros_like(a["L0_gnn_b_me"]), a["L0_gnn_b_me"]])]),
        "w_e": pad(a["L0_gnn_W_me"].T, W),
        "w_net": a["L0_gnn_W_net"].T, "b_net": a["L0_gnn_b_net"][:, None],
        "wo1": a["L0_gnn_W_o1"].T, "wo2": a["L0_gnn_W_o2"].T,
        "bo": np.stack([a["L0_gnn_b_o1"], a["L0_gnn_b_o2"]]),
        "ew1a": a["L1_gnn_eW1"][:d], "ew1b": a["L1_gnn_eW1"][d:], "eb1": np.concatenate([np.zeros_like(a["L1_gnn_eb1"]), a["L1_gnn_eb1"]])[None],
        "ew2": a["L1_gnn_eW2"], "eb2": a["L1_gnn_eb2"][None],
        "nw1a": a["L1_gnn_nW1"][:d], "nw1b": a["L1_gnn_nW1"][d:], "nb1": a["L1_gnn_nb1"][:, None],
        "nw2": a["L1_gnn_nW2"], "nb2": a["L1_gnn_nb2"][None],
    }
    return {k: np.ascontiguousarray(o[k]) for k in _ARGS}, n, e


def program(nc, arrays, n, e):
    args = []
    for name in _ARGS:
        v = arrays[name]
        args.append(nc.dram_tensor(f"in_{name}", v.shape, mybir.dt.from_np(v.dtype), kind="ExternalInput").ap())
    out = nc.dram_tensor("out_0", (n, arrays["x"].shape[1]), F32, kind="ExternalOutput").ap()
    gnn(nc, e, *args, out)


def kernel(**inputs):
    import concourse.bacc as bacc
    from concourse.bass_utils import run_bass_kernel_spmd

    nc = bacc.Bacc("TRN2", target_bir_lowering=False, num_devices=1)
    arrays, n, e = lay_out(inputs)
    program(nc, arrays, n, e)
    r = run_bass_kernel_spmd(nc, [{f"in_{k}": v for k, v in arrays.items()}], core_ids=[0])
    return r.results[0]["out_0"]
```

```python
from contextlib import ExitStack, contextmanager

import concourse.bass as bass
from concourse import mybir

P = 128
ALU = mybir.AluOpType
ACT = mybir.ActivationFunctionType
AX = mybir.AxisListType
F32 = mybir.dt.float32
BF16 = mybir.dt.bfloat16
I32 = mybir.dt.int32
HB = 64
W = 32
C_SRC, C_HI, C_LO, C_DST = 16, 17, 18, 19
CH = 7
RESET = 2.0 ** 120
FAR = float(1 << 20)
EPS_LN = 1e-5


def sizes(n_nodes, n_edges):
    nb = -(-n_nodes // P)
    q = -(-(n_edges + P) // P)
    q += -q % 8
    ns = n_edges // P + nb + 1
    ns += -ns % 4
    return nb, q, ns


def pipeline(eng, count, stages, cool=0, unroll=4):
    most = max(lag for lag, _ in stages)
    warm = most + 2 * unroll
    warm += -warm % unroll
    end = (count - cool) // unroll * unroll

    def turn(k, u):
        for lag, stage in stages:
            n, v = k + (u - lag) // unroll, (u - lag) % unroll
            if isinstance(k, int) and not 0 <= unroll * n + v < count:
                continue
            stage(unroll * n + v, v, n)

    def straight(first, last):
        for t in range(first, last):
            turn(t // unroll, t % unroll)
    if end - warm < 2 * unroll:
        warm = end = 0
    straight(0, warm)
    if end:
        with eng.Fori(warm // unroll, end // unroll) as k:
            for u in range(unroll):
                turn(k, u)
    straight(end, count + most)


def offsets(nc, engine, row, last):
    _, values = nc.values_load_multi_w_load_instructions(row, engines=[engine], min_val=0, max_val=last,
                                                         skip_runtime_bounds_check_because="the table holds block starts only")
    return values


def past(sems, u, n, back=0):
    return sems[(u - back) % 4], n + (u - back) // 4 + 1


def wait(eng, sem, value):
    if not (isinstance(value, int) and value <= 0):
        eng.wait_ge(sem, value)


def pass_waits(eng, passed):
    eng.sem_inc(passed, 1)


class Chain:

    def __init__(self, eng, sem, per_turn=0):
        self.eng, self.sem, self.per, self.base, self.n = eng, sem, per_turn, 0, 0

    def turn(self, i):
        assert self.n in (0, self.per), (self.n, self.per)
        self.base, self.n = i * self.per, 0

    def add(self, ins):
        self.n += 1
        ins.then_inc(self.sem, 1)

    def settle(self):
        self.eng.wait_ge(self.sem, self.base + self.n)

    def __call__(self, ins):
        self.add(ins)
        self.settle()


def gnn(nc, E, x, xT, src, dst, edge_attr, wm12, bm12, w_e, w_net, b_net, wo1, wo2, bo,
        ew1a, ew1b, eb1, ew2, eb2, nw1a, nw1b, nb1, nw2, nb2, out):
    N, D = out.shape
    EP = src.shape[0]
    NB, QE, NS = sizes(N, E)
    assert QE * P == EP
    NP = NB * P
    F = w_net.shape[0]
    KA = edge_attr.shape[1]
    POS = NS * P
    G = NS // 4
    QC = QE // 8
    HN = NS // 2
    FULL = E // P

    rec_d = nc.dram_tensor("edge_records", (EP, W), F32).ap()
    moved_d = nc.dram_tensor("edge_records_moved", (EP, W), F32).ap()
    u_d = nc.dram_tensor("edge_in_src_order", (POS, F), F32).ap()
    s_d = nc.dram_tensor("running_max", (POS + P, F), F32).ap()
    a_d = nc.dram_tensor("src_table_1", (NP, D), F32).ap()

    whole = ExitStack()

    def sb(scope, name, shape, dt=F32):
        return scope.enter_context(nc.sbuf_tensor(name, shape, dt))

    def ps(scope, name, shape, dt=F32):
        return scope.enter_context(nc.psum_tensor(name, shape, dt))

    def sem(scope, name):
        return scope.enter_context(nc.semaphore(name))

    def bcast(ap, *shape):
        return ap.broadcast_to(shape)

    with whole:
        ident = sb(whole, "ident", [P, P])
        identb = sb(whole, "identb", [P, P], BF16)
        iota_b = sb(whole, "iota_b", [P, P], BF16)
        iota_f = sb(whole, "iota_f", [P, P])
        before = sb(whole, "before", [P, P])
        onesf = sb(whole, "onesf", [P, P])
        off_s = sb(whole, "off_s", [P, NS])
        dloc_s = sb(whole, "dloc_s", [P, NS])
        src_s = sb(whole, "src_s", [P, NS], I32)
        start_s = sb(whole, "start_s", [P, NS])
        end_s = sb(whole, "end_s", [P, NS])
        e0_row = sb(whole, "e0_row", [1, NS], I32)
        df_row = sb(whole, "df_row", [1, NS], I32)
        dd_row = sb(whole, "dd_row", [1, NS], I32)
        db_row = sb(whole, "db_row", [1, NS], I32)
        sf_row = sb(whole, "sf_row", [1, NS], I32)
        last_i = sb(whole, "last_i", [P, HB], I32)
        bnet_c = sb(whole, "bnet_c", [F, 1])
        wnet_s = sb(whole, "wnet_s", [F, F])
        we_s = sb(whole, "we_s", [P, 4, F])
        unsorted_i = sb(whole, "unsorted_i", [1, 1], I32)
        reset_b = sb(whole, "reset_b", [P, F], BF16)
        zero_rows = sb(whole, "zero_rows", [P, F])
        pad_i = sb(whole, "pad_i", [P, HB], I32)
        far_c = sb(whole, "far_c", [HB, 1])
        start_t = sb(whole, "start_t", [HB, P])
        rank_r = sb(whole, "rank_r", [HB, 4, P])

        EARLY = NB // 3

        def clear_pads(pool, b, done):
            pool.indirect_dma_start(u_d, bass.IndirectOffsetOnAxis(pad_i[:, b:b + 1], 0), zero_rows[:], None,
                                    bounds_check=POS - 1, oob_is_err=False).then_inc(done, 16)

        layer0 = ExitStack()
        with layer0:
            m1 = sb(layer0, "m1", [P, NB * F])
            m2 = sb(layer0, "m2", [P, NB * F])
            with ExitStack() as t:
                src_i = sb(t, "src_i", [P, QE], I32)
                dst_i = sb(t, "dst_i", [P, QE], I32)
                hi_i = sb(t, "hi_i", [P, QE], I32)
                lo_i = sb(t, "lo_i", [P, QE], I32)
                src_f = sb(t, "src_f", [P, QE])
                dst_f = sb(t, "dst_f", [P, QE])
                hi_f = sb(t, "hi_f", [P, QE], BF16)
                lo_f = sb(t, "lo_f", [P, QE], BF16)
                attr = sb(t, "attr", [P, 2, QC * KA])
                rec = sb(t, "rec", [P, 2, QC, W])
                cmp = sb(t, "cmp", [P, QE], BF16)
                below = sb(t, "below", [P, NB + 1])
                bounds = sb(t, "bounds", [P, P])
                sign = sb(t, "sign", [P, 2, QE], BF16)
                next_i = sb(t, "next_i", [P, 2], I32)
                next_f = sb(t, "next_f", [P, 2])
                drops = sb(t, "drops", [P, 2])
                ohlo = sb(t, "ohlo", [P, 4, 4, P], BF16)
                ohhi = sb(t, "ohhi", [P, 4, 4, HB], BF16)
                iota_i = sb(t, "iota_i", [P, P], I32)
                iota_n = sb(t, "iota_n", [P, NS], I32)
                iota_s = sb(t, "iota_s", [P, NS])
                hist_s = sb(t, "hist_s", [HB, P])
                cum = sb(t, "cum", [HB, P])
                one_t = sb(t, "one_t", [HB, P])
                cnt = sb(t, "cnt", [HB, 2])
                cnt_i = sb(t, "cnt_i", [HB, 2], I32)
                steps_i = sb(t, "steps_i", [HB, 2], I32)
                steps = sb(t, "steps", [HB, 2])
                pre = sb(t, "pre", [HB, 2])
                pend = sb(t, "pend", [HB, 2])
                sd = sb(t, "sd", [HB, 1])
                next_b = sb(t, "next_b", [HB, 1])
                wd = sb(t, "wd", [HB, 1])
                tri = sb(t, "tri", [HB, HB])
                ge = sb(t, "ge", [HB, 2, NS])
                own = sb(t, "own", [HB, 2, NS])
                val = sb(t, "val", [HB, NS])
                end_t = sb(t, "end_t", [HB, P])
                flag = sb(t, "flag", [HB, P])
                lidx = sb(t, "lidx", [HB, P])
                pidx = sb(t, "pidx", [HB, P])
                pfar = sb(t, "pfar", [HB, P])
                plast = sb(t, "plast", [HB, 1])
                xt = sb(t, "xt", [P, 4, P])
                wm = sb(t, "wm", [P, 2 * F])
                bm = sb(t, "bm", [2, 2 * F])
                ps_hist = ps(t, "ps_hist", [HB, 512])
                ps_a = ps(t, "ps_a", [P, 512])
                ps_b = ps(t, "ps_b", [P, 512])
                ps_c = ps(t, "ps_c", [P, 512])
                ps_m = [ps(t, f"ps_m{k}", [P, 512]) for k in range(2)]

                edges_in = sem(t, "edges_in")
                attr_in = [sem(t, f"attr_in{k}") for k in range(2)]
                rec_out = [sem(t, f"rec_out{k}") for k in range(2)]
                consts = sem(t, "consts")
                weights_in = sem(t, "weights_in")
                pads_ready = sem(t, "pads_ready")
                early_out = sem(t, "early_out")
                zeros_out = sem(t, "zeros_out")
                columns = sem(t, "columns")
                attr_set = sem(t, "attr_set")
                cols_set = sem(t, "cols_set")
                pool_chain = sem(t, "pool_chain")
                onehots = sem(t, "onehots")
                bounds_set = sem(t, "bounds_set")
                below_ready = sem(t, "below_ready")
                counted = sem(t, "counted")
                dve_chain = sem(t, "dve_chain")
                to_pe = sem(t, "to_pe")
                to_dve = sem(t, "to_dve")
                xt_in = [sem(t, f"xt_in{k}") for k in range(4)]
                m_ready = sem(t, "m_ready")
                m_taken = sem(t, "m_taken")

                ALONE = max(0, (QE // 4 - 2 * NB) // 4 * 4)
                ZEROED, ALL_CONSTS = 1, 13

                with nc.Block() as block:
                    @block.sync
                    def _(sp):
                        sp.dma_start(src_i[:], src.rearrange("(p q) -> p q", p=P)).then_inc(edges_in, 16)
                        sp.dma_start(dst_i[:], dst.rearrange("(p q) -> p q", p=P)).then_inc(edges_in, 16)
                        sp.dma_start(next_i[0:P - 1, :], dst.rearrange("(p q) -> p q", p=P)[1:P, 0:2]).then_inc(edges_in, 16)
                        sp.dma_start(next_i[P - 1:P, :], dst.rearrange("(p q) -> p q", p=P)[P - 1:P, QE - 2:QE]).then_inc(edges_in, 16)
                        attr_v = edge_attr.rearrange("(p c q) k -> c p (q k)", p=P, c=8)
                        rec_v = rec_d.rearrange("(p c q) w -> c p (q w)", p=P, c=8)
                        for c in range(2):
                            sp.dma_start(attr[:, c, :], attr_v[c]).then_inc(attr_in[c], 16)
                        sp.wait_ge(consts, ZEROED)
                        for step in range(FULL, NS):
                            sp.dma_start(u_d[P * step:P * step + P, :], zero_rows[:]).then_inc(zeros_out, 16)
                        sp.dma_start(s_d[POS:POS + P, :], zero_rows[:]).then_inc(zeros_out, 16)
                        for c in range(8):
                            k = c % 2
                            sp.wait_ge(attr_set, c + 1)
                            sp.wait_ge(cols_set, c + 1)
                            sp.dma_start(rec_v[c], rec[:, k].rearrange("p q w -> p (q w)")).then_inc(rec_out[k], 16)
                            if c + 2 < 8:
                                sp.dma_start(attr[:, k, :], attr_v[c + 2]).then_inc(attr_in[k], 16)

                        def load_x(b, u, n):
                            wait(sp, m_ready, b - 3)
                            sp.dma_start(xt[:, u, :], xT[:, bass.ds(b * P, P)]).then_inc(xt_in[u], 16)
                        pipeline(sp, NB, [(0, load_x)])
                        for k in range(2):
                            sp.wait_ge(rec_out[k], 16 * 4)
                        sp.wait_ge(zeros_out, 16 * (NS - FULL + 1))

                    @block.gpsimd
                    def _(pool):
                        g = nc.gpsimd
                        g.memset(zero_rows[:], 0.0).then_inc(consts, 1)
                        g.memset(rec[:], 0.0).then_inc(consts, 1)
                        g.memset(we_s[:], 0.0).then_inc(consts, 1)
                        g.memset(onesf[:], 1.0).then_inc(consts, 1)
                        g.memset(one_t[:], 1.0).then_inc(consts, 1)
                        g.memset(reset_b[:], -RESET).then_inc(consts, 1)
                        g.memset(before[:], 1.0).then_inc(pool_chain, 1)
                        g.memset(ident[:], 0.0).then_inc(pool_chain, 1)
                        g.memset(tri[:], 1.0).then_inc(pool_chain, 1)
                        g.memset(far_c[:], 0.0).then_inc(pool_chain, 1)
                        g.iota(iota_i[:], pattern=[[1, P]], base=0, channel_multiplier=0).then_inc(pool_chain, 1)
                        g.iota(iota_n[:], pattern=[[1, NS]], base=0, channel_multiplier=0).then_inc(pool_chain, 1)
                        pool.wait_ge(pool_chain, 6)
                        g.tensor_copy(iota_f[:], iota_i[:]).then_inc(consts, 1)
                        g.tensor_copy(iota_b[:], iota_i[:]).then_inc(consts, 1)
                        g.tensor_copy(iota_s[:], iota_n[:]).then_inc(consts, 1)
                        g.affine_select(out=before[:], in_=before[:], compare_op=ALU.is_gt, fill=0.0,
                                        base=0, pattern=[[-1, P]], channel_multiplier=1).then_inc(consts, 1)
                        g.affine_select(out=tri[:], in_=tri[:], compare_op=ALU.is_gt, fill=0.0,
                                        base=0, pattern=[[1, HB]], channel_multiplier=-1).then_inc(consts, 1)
                        g.affine_select(out=ident[:], in_=ident[:], compare_op=ALU.not_equal, fill=1.0,
                                        base=0, pattern=[[-1, P]], channel_multiplier=1).then_inc(pool_chain, 1)
                        g.affine_select(out=far_c[:], in_=far_c[:], compare_op=ALU.not_equal, fill=FAR,
                                        base=-(HB - 1), pattern=[[0, 1]], channel_multiplier=1).then_inc(consts, 1)
                        pool.wait_ge(pool_chain, 7)
                        g.tensor_copy(identb[:], ident[:]).then_inc(consts, 1)
                        pool.wait_ge(columns, 4)
                        pool.wait_ge(consts, ALL_CONSTS)
                        for c in range(8):
                            if c >= 2:
                                pool.wait_ge(rec_out[c % 2], 16 * (c // 2))
                            for col, table in ((C_SRC, src_f), (C_HI, hi_f), (C_LO, lo_f), (C_DST, dst_f)):
                                last = g.tensor_copy(rec[:, c % 2, :, col], table[:, c * QC:(c + 1) * QC])
                            last.then_inc(cols_set, 1)
                        pool.wait_ge(pads_ready, 1)
                        for b in range(EARLY):
                            clear_pads(pool, b, early_out)
                        pool.wait_ge(early_out, 16 * EARLY)

                    @block.scalar
                    def _(act):
                        s = nc.scalar
                        for to, of in ((wm[:], wm12), (bm[:], bm12), (wnet_s[:], w_net), (bnet_c[:], b_net)):
                            act.dma_start(to, of).then_inc(weights_in, 16)
                        act.wait_ge(consts, ALL_CONSTS)
                        for j in range(4):
                            act.dma_start(we_s[W * j:W * j + W, j, :], w_e).then_inc(weights_in, 16)
                        for c in range(8):
                            k = c % 2
                            act.wait_ge(attr_in[k], 16 * (c // 2 + 1))
                            if c >= 2:
                                act.wait_ge(rec_out[k], 16 * (c // 2))
                            s.copy(rec[:, k, :, 0:KA], attr[:, k].rearrange("p (q k) -> p q k", k=KA)).then_inc(attr_set, 1)

                        def keep_tables(b, u, n):
                            act.wait_ge(m_ready, b + 1)
                            s.copy(m1[:, bass.ds(b * F, F)], ps_m[u % 2][:, 0:F])
                            s.copy(m2[:, bass.ds(b * F, F)], ps_m[u % 2][:, F:2 * F]).then_inc(m_taken, 1)
                        def split(b):
                            wait(act, below_ready, b - 1)
                            s.activation(sign[:, b % 2, :], dst_f[:], ACT.Sign, scale=-1.0, bias=bounds[:, b:b + 1],
                                         accum_out=below[:, b:b + 1]).then_inc(below_ready, 1)
                        act.wait_ge(bounds_set, 1)
                        act.wait_ge(columns, 4)
                        for b in range(NB + 1):
                            split(b)
                            if b < NB:
                                keep_tables(b, b % 4, b // 4)

                    @block.vector
                    def _(dve):
                        v = nc.vector
                        ch = Chain(dve, dve_chain)
                        dve.wait_ge(edges_in, 64)
                        v.tensor_single_scalar(hi_i[:], src_i[:], 7, op=ALU.logical_shift_right)
                        ch(v.tensor_single_scalar(lo_i[:], src_i[:], P - 1, op=ALU.bitwise_and))
                        v.tensor_copy(src_f[:], src_i[:]).then_inc(columns, 1)
                        v.tensor_copy(hi_f[:], hi_i[:]).then_inc(columns, 1)
                        v.tensor_copy(lo_f[:], lo_i[:]).then_inc(columns, 1)
                        v.tensor_copy(dst_f[:], dst_i[:]).then_inc(columns, 1)
                        dve.wait_ge(columns, 4)
                        dve.wait_ge(consts, ALL_CONSTS)
                        v.tensor_scalar(bounds[:], iota_f[:], float(P), -0.5, ALU.mult, ALU.add).then_inc(bounds_set, 1)

                        def onehot(g, u, n):
                            wait(dve, counted, g - 3)
                            now = bass.ds(4 * g, 4)
                            v.tensor_tensor(ohlo[:, u], bcast(lo_f[:, now].unsqueeze(2), P, 4, P),
                                            bcast(iota_b[:].unsqueeze(1), P, 4, P), ALU.is_equal)
                            v.tensor_tensor(ohhi[:, u], bcast(hi_f[:, now].unsqueeze(2), P, 4, HB),
                                            bcast(iota_b[:, 0:HB].unsqueeze(1), P, 4, HB), ALU.is_equal).then_inc(onehots, 1)
                        pipeline(dve, QE // 4, [(0, onehot)])
                        ch(v.tensor_copy(next_f[:], next_i[:]))
                        v.tensor_tensor(drops[:, 1:2], next_f[:, 0:1], dst_f[:, QE - 1:QE], ALU.is_lt)
                        ch(v.tensor_tensor(cmp[:, 0:QE - 1], dst_f[:, 1:QE], dst_f[:, 0:QE - 1], ALU.is_lt))
                        ch(v.tensor_reduce(drops[:, 0:1], cmp[:, 0:QE - 1], AX.X, ALU.add))
                        v.engine_nop().then_inc(to_pe, 1)

                        dve.wait_ge(counted, QE // 4)
                        dve.wait_ge(to_dve, 1)
                        v.memset(cnt[:], 0.0)
                        v.tensor_scalar(sd[0:NB, :], ps_a[0:NB, 0:1], float(EP), 0.5, ALU.add, ALU.mult)
                        ch(v.tensor_scalar(next_b[0:NB, :], ps_a[0:NB, 1:2], float(EP), 0.5, ALU.add, ALU.mult))
                        v.tensor_copy(unsorted_i[:], ps_a[0:1, 2:3])
                        ch(v.tensor_copy(hist_s[:], ps_hist[:, 0:P]))
                        v.tensor_reduce(cnt[0:NB, 0:1], hist_s[0:NB, :], AX.X, ALU.add)
                        ch(v.tensor_tensor(cnt[0:NB, 1:2], next_b[0:NB, :], sd[0:NB, :], ALU.subtract))
                        ch(v.tensor_scalar(cnt_i[:], cnt[:], float(P - 1), None, ALU.add))
                        ch(v.tensor_single_scalar(steps_i[:], cnt_i[:], 7, op=ALU.logical_shift_right))
                        ch(v.tensor_copy(steps[:], steps_i[:]))
                        v.engine_nop().then_inc(to_pe, 1)
                        dve.wait_ge(to_dve, 2)
                        ch(v.tensor_copy(pre[:], ps_b[0:HB, 0:2]))
                        ch(v.tensor_tensor(pend[:], pre[:], steps[:], ALU.add))
                        v.tensor_scalar(plast[:], pend[:, 0:1], float(P), -float(P), ALU.mult, ALU.add)
                        for o in range(2):
                            v.tensor_scalar(ge[:, o], iota_s[0:HB, :], pre[:, o:o + 1], None, ALU.is_ge)
                        ch(v.tensor_scalar(wd[0:NB], pre[0:NB, 1:2], -float(P), -float(E), ALU.mult, ALU.add))
                        for o in range(2):
                            v.scalar_tensor_tensor(out=own[:, o], in0=iota_s[0:HB, :], scalar=pend[:, o:o + 1],
                                                   in1=ge[:, o], op0=ALU.is_lt, op1=ALU.mult)
                        ch(v.tensor_tensor(wd[0:NB], wd[0:NB], sd[0:NB], ALU.add))
                        ch(v.tensor_scalar(val[0:NB], iota_s[0:NB, :], float(P), wd[0:NB, :], ALU.mult, ALU.add))
                        ch(v.tensor_tensor(val[0:NB], val[0:NB], own[0:NB, 1], ALU.mult))
                        ch(v.tensor_tensor_scan(cum[:], one_t[:], hist_s[:], 0.0, ALU.mult, ALU.add))
                        ch(v.tensor_tensor(cum[:], cum[:], hist_s[:], ALU.subtract))
                        ch(v.tensor_scalar(start_t[:], one_t[:], pre[:, 0:1], float(P), ALU.mult, ALU.mult))
                        ch(v.tensor_tensor(start_t[:], start_t[:], cum[:], ALU.add))
                        v.tensor_scalar(rank_r[:, 0], start_t[:], far_c[:], None, ALU.add)
                        v.tensor_scalar(flag[:], hist_s[:], 0.0, None, ALU.is_gt)
                        ch(v.tensor_tensor(end_t[:], start_t[:], hist_s[:], ALU.add))
                        ch(v.tensor_scalar(pidx[:], iota_f[0:HB, :], plast[:], None, ALU.add))
                        ch(v.tensor_scalar(pfar[:], pidx[:], end_t[:, P - 1:P], FAR, ALU.is_lt, ALU.mult))
                        ch(v.tensor_tensor(pidx[:], pidx[:], pfar[:], ALU.add))
                        ch(v.scalar_tensor_tensor(out=lidx[:], in0=end_t[:], scalar=-float(POS + 1), in1=flag[:],
                                                  op0=ALU.add, op1=ALU.mult))
                        v.tensor_scalar(lidx[:], lidx[:], float(POS), None, ALU.add).then_inc(to_pe, 1)
                        dve.wait_ge(to_dve, 3)
                        v.tensor_copy(pad_i[:], ps_a[:, 2 * HB:3 * HB]).then_inc(pads_ready, 1)
                        v.tensor_copy(last_i[:], ps_a[:, HB:2 * HB])
                        for h in range(2):
                            part = slice(h * HN, (h + 1) * HN)
                            one, two = (ps_b, ps_c) if h == 0 else (ps_c, ps_b)
                            dve.wait_ge(to_dve, 4 + 5 * h)
                            v.tensor_scalar(e0_row[:, part], one[0:1, 0:HN], float(E), float(W), ALU.add, ALU.mult).then_inc(to_pe, 1)
                            dve.wait_ge(to_dve, 5 + 5 * h)
                            v.tensor_scalar(sf_row[:, part], two[0:1, 0:HN], float(F), -float(F), ALU.mult, ALU.add).then_inc(to_pe, 1)
                            dve.wait_ge(to_dve, 6 + 5 * h)
                            v.tensor_scalar(db_row[:, part], one[0:1, 0:HN], -1.0, None, ALU.add)
                            v.tensor_scalar(df_row[:, part], one[0:1, 0:HN], float(F), -float(F), ALU.mult, ALU.add)
                            v.tensor_scalar(dd_row[:, part], one[0:1, 0:HN], float(D), -float(D), ALU.mult, ALU.add)
                            v.tensor_scalar(off_s[:, part], one[:, 0:HN], float(P), -float(P), ALU.mult, ALU.add).then_inc(to_pe, 1)
                            dve.wait_ge(to_dve, 7 + 5 * h)
                            v.scalar_tensor_tensor(out=start_s[:, part], in0=iota_s[:, part], scalar=-float(P), in1=two[:, 0:HN],
                                                   op0=ALU.mult, op1=ALU.add).then_inc(to_pe, 1)
                            dve.wait_ge(to_dve, 8 + 5 * h)
                            v.scalar_tensor_tensor(out=end_s[:, part], in0=iota_s[:, part], scalar=-float(P), in1=one[:, 0:HN],
                                                   op0=ALU.mult, op1=ALU.add).then_inc(to_pe, 1)

                    @block.tensor
                    def _(pe):
                        m = nc.tensor

                        def count(g, u, n):
                            pe.wait_ge(onehots, g + 1)
                            static = isinstance(g, int)
                            for j in range(4):
                                mm = m.matmul(ps_hist[:, 0:P], ohhi[:, u, j, :], ohlo[:, u, j, :],
                                              start=(static and g == 0 and j == 0),
                                              stop=(static and g == QE // 4 - 1 and j == 3), skip_group_check=True)
                            mm.then_inc(counted, 1)
                        def tables(b, u, n):
                            pe.wait_ge(xt_in[u], 16 * (n + 1))
                            wait(pe, m_taken, b - 1)
                            m.matmul(ps_m[u % 2][:, 0:2 * F], xt[:, u, :], wm[:], start=True, stop=False)
                            m.matmul(ps_m[u % 2][:, 0:2 * F], onesf[0:2, :], bm[:], start=False, stop=True).then_inc(m_ready, 1)
                        pe.wait_ge(consts, ALL_CONSTS)
                        pe.wait_ge(weights_in, 16 * 8)
                        pipeline(pe, ALONE, [(0, count)])

                        def both(b, u, n):
                            for q in range(2):
                                count(ALONE + 2 * b + q, (2 * u + q) % 4, n)
                            tables(b, u, n)
                        if ALONE:
                            pipeline(pe, NB, [(0, both)], cool=1)
                        else:
                            pipeline(pe, NB, [(0, tables)])
                        for g in range(ALONE + 2 * NB if ALONE else 0, QE // 4):
                            count(g, g % 4, g // 4)
                        pe.wait_ge(to_pe, 1)
                        pe.wait_ge(below_ready, NB + 1)
                        m.matmul(ps_a[0:NB, 0:1], below[:, 0:NB], onesf[:, 0:1], start=True, stop=True)
                        m.matmul(ps_a[0:1, 2:3], drops[:, 0:1], onesf[:, 0:1], start=True, stop=False)
                        m.matmul(ps_a[0:1, 2:3], drops[:, 1:2], onesf[:, 0:1], start=False, stop=True)
                        m.matmul(ps_a[0:NB, 1:2], below[:, 1:NB + 1], onesf[:, 0:1], start=True, stop=True).then_inc(to_dve, 1)
                        pe.wait_ge(to_pe, 2)
                        m.matmul(ps_b[0:HB, 0:2], tri[:], steps[:], start=True, stop=True).then_inc(to_dve, 1)
                        pe.wait_ge(to_pe, 3)
                        m.transpose(ps_a[:, 2 * HB:3 * HB], pidx[:], ident[0:HB, 0:HB])
                        m.transpose(ps_a[:, HB:2 * HB], lidx[:], ident[0:HB, 0:HB]).then_inc(to_dve, 1)
                        done = 3
                        for h in range(2):
                            part = slice(h * HN, (h + 1) * HN)
                            for left, right in ((onesf[0:NB, :], val[0:NB, part]),
                                                      (onesf[0:NB, :], ge[0:NB, 0, part]),
                                                      (onesf[0:NB, :], ge[0:NB, 1, part]),
                                                      (start_t[0:NB, :], own[0:NB, 0, part]),
                                                      (end_t[0:NB, :], own[0:NB, 0, part])):
                                if done > 4:
                                    pe.wait_ge(to_pe, done - 1)
                                ps_x = (ps_b, ps_c)[(done - 3) % 2]
                                m.matmul(ps_x[:, 0:HN], left, right, start=True, stop=True).then_inc(to_dve, 1)
                                done += 1

            with ExitStack() as t:
                dst_i = sb(t, "dst_i_s", [P, QE], I32)
                hi_i = sb(t, "hi_i_s", [P, QE], I32)
                lo_i = sb(t, "lo_i_s", [P, QE], I32)
                dst_f = sb(t, "dst_f_s", [P, QE])
                hi_f = sb(t, "hi_f_s", [P, QE])
                lo_f = sb(t, "lo_f_s", [P, QE])
                key = sb(t, "key", [P, 1])
                ohlo = sb(t, "ohlo_s", [P, P], BF16)
                ohhi = sb(t, "ohhi_s", [P, HB], BF16)
                tri = sb(t, "tri_s", [HB, HB])
                hist_s = sb(t, "hist_s_s", [HB, P])
                one_t = sb(t, "one_t_s", [HB, P])
                cum = sb(t, "cum_s", [HB, P])
                free = sb(t, "free_s", [HB, P])
                hiT = sb(t, "hiT_s", [HB, P])
                junk = sb(t, "junk_s", [P, P], BF16)
                junk2 = sb(t, "junk2_s", [P, P], BF16)
                within = sb(t, "within_s", [P, 1])
                across = sb(t, "across_s", [P, 1])
                place = sb(t, "place_s", [P, 1], I32)
                rec = sb(t, "rec_s", [P, W])
                ps_hist = ps(t, "ps_hist_s", [HB, 512])
                ps_first = ps(t, "ps_first", [HB, 512])
                ps_row = ps(t, "ps_row_s", [P, 512])
                ps_hi = ps(t, "ps_hi_s", [P, 1024], BF16)
                ps_cnt = ps(t, "ps_cnt_s", [P, 512])
                ps_new = ps(t, "ps_new_s", [HB, 512])
                dst_in = sem(t, "dst_in")
                tri_ready = sem(t, "tri_ready")
                sort_chain = sem(t, "sort_chain")
                one_hot = sem(t, "one_hot")
                summed = sem(t, "summed")
                totals = sem(t, "totals")
                firsts = sem(t, "firsts")
                free_ready = sem(t, "free_ready")
                keyed = sem(t, "keyed")
                turned = sem(t, "turned")
                hiT_ready = sem(t, "hiT_ready_s")
                ranked = sem(t, "ranked")
                placed = sem(t, "placed")
                rec_read = sem(t, "rec_read")
                rec_moved = sem(t, "rec_moved")
                copied = sem(t, "copied")
                place_chain_s = sem(t, "place_chain_s")
                passed = sem(t, "passed_s")
                passed_pe = sem(t, "passed_pe_s")

                def edges_unsorted(eng):
                    return eng.If(eng.value_load(unsorted_i[0:1, 0:1], min_val=0, max_val=EP) > 0)

                with nc.Block() as block:
                    @block.sync
                    def _(sp):
                        with edges_unsorted(sp):
                            sp.dma_start(dst_i[:], dst.rearrange("(p q) -> p q", p=P)).then_inc(dst_in, 16)
                            columns = rec_d.rearrange("(p q) w -> p q w", p=P)

                            def load(q, u, n):
                                wait(sp, rec_moved, 16 * q)
                                sp.dma_start(rec[:], columns[:, bass.ds(q, 1), :].rearrange("p a w -> p (a w)")).then_inc(rec_read, 16)
                            pipeline(sp, QE, [(0, load)])
                            sp.wait_ge(rec_moved, 16 * QE)
                            for c in range(8):
                                part = slice(c * P * QC, (c + 1) * P * QC)
                                sp.dma_start(rec_d[part, :], moved_d[part, :]).then_inc(copied, 16)
                            sp.wait_ge(copied, 16 * 8)

                    @block.gpsimd
                    def _(pool):
                        with edges_unsorted(pool):
                            nc.gpsimd.memset(one_t[:], 1.0).then_inc(tri_ready, 1)
                            nc.gpsimd.memset(tri[:], 1.0).then_inc(tri_ready, 1)
                            pool.wait_ge(tri_ready, 2)
                            nc.gpsimd.affine_select(out=tri[:], in_=tri[:], compare_op=ALU.is_gt, fill=0.0,
                                                    base=0, pattern=[[1, HB]], channel_multiplier=-1).then_inc(tri_ready, 1)

                            def move(q, u, n):
                                pool.wait_ge(placed, q + 1)
                                pool.wait_ge(rec_read, 16 * (q + 1))
                                pass_waits(pool, passed)
                                pool.indirect_dma_start(moved_d, bass.IndirectOffsetOnAxis(place[:, 0:1], 0),
                                                        rec[:], None).then_inc(rec_moved, 16)
                            pipeline(pool, QE, [(0, move)])
                            pool.wait_ge(rec_moved, 16 * QE)

                    @block.vector
                    def _(dve):
                        with edges_unsorted(dve):
                            v = nc.vector
                            ch = Chain(dve, sort_chain)
                            dve.wait_ge(dst_in, 16)
                            v.tensor_single_scalar(hi_i[:], dst_i[:], 7, op=ALU.logical_shift_right)
                            ch(v.tensor_single_scalar(lo_i[:], dst_i[:], P - 1, op=ALU.bitwise_and))
                            v.tensor_copy(hi_f[:], hi_i[:])
                            v.tensor_copy(lo_f[:], lo_i[:])
                            ch(v.tensor_copy(dst_f[:], dst_i[:]))

                            def onehot(q):
                                now = bass.ds(q, 1)
                                v.tensor_scalar(ohlo[:], iota_b[:], lo_f[:, now], None, ALU.is_equal)
                                v.tensor_scalar(ohhi[:], iota_b[:, 0:HB], hi_f[:, now], None, ALU.is_equal).then_inc(one_hot, 1)

                            def count(q, u, n):
                                wait(dve, summed, q)
                                onehot(q)
                            pipeline(dve, QE, [(0, count)])
                            dve.wait_ge(summed, QE)
                            dve.wait_ge(tri_ready, 3)
                            ch(v.tensor_copy(hist_s[:], ps_hist[:, 0:P]))
                            v.tensor_tensor_scan(cum[:], one_t[:], hist_s[:], 0.0, ALU.mult, ALU.add).then_inc(totals, 1)
                            dve.wait_ge(firsts, 1)
                            dve.wait_ge(totals, 1)
                            ch(v.tensor_tensor(cum[:], cum[:], hist_s[:], ALU.subtract))
                            v.scalar_tensor_tensor(out=free[:], in0=one_t[:], scalar=ps_first[:, 0:1], in1=cum[:],
                                                   op0=ALU.mult, op1=ALU.add).then_inc(free_ready, 1)
                            places = Chain(dve, place_chain_s, 2)

                            def rank(q, u, n):
                                places.turn(q)
                                wait(dve, ranked, q)
                                wait(dve, rec_moved, 16 * q)
                                v.tensor_copy(key[:], dst_f[:, bass.ds(q, 1)]).then_inc(keyed, 1)
                                onehot(q)
                                dve.wait_ge(ranked, q + 1)
                                dve.wait_ge(keyed, q + 1)
                                places.add(v.scalar_tensor_tensor(out=junk[:], in0=ps_row[:, 0:P], scalar=key[:],
                                                                  in1=before[:], op0=ALU.is_equal, op1=ALU.mult,
                                                                  accum_out=within[:]))
                                places.add(v.tensor_tensor_reduce(junk2[:], ps_cnt[:, 0:P], ohlo[:], 1.0, 0.0,
                                                                  ALU.mult, ALU.add, across[:]))
                                v.tensor_tensor(free[:], free[:], ps_new[:, 0:P], ALU.add).then_inc(free_ready, 1)
                                places.settle()
                                v.tensor_tensor(place[:], within[:], across[:], ALU.add).then_inc(placed, 1)
                                dve.wait_ge(free_ready, q + 2)
                            pipeline(dve, QE, [(0, rank)])

                    @block.tensor
                    def _(pe):
                        with edges_unsorted(pe):
                            m = nc.tensor

                            def count(q, u, n):
                                pe.wait_ge(one_hot, q + 1)
                                m.matmul(ps_hist[:, 0:P], ohhi[:], ohlo[:], start=(isinstance(q, int) and q == 0),
                                         stop=(isinstance(q, int) and q == QE - 1), skip_group_check=True).then_inc(summed, 1)
                            pipeline(pe, QE, [(0, count)], cool=1)
                            pe.wait_ge(totals, 1)
                            m.matmul(ps_first[:, 0:1], tri[:], cum[:, P - 1:P], start=True, stop=True).then_inc(firsts, 1)

                            def rank(q, u, n):
                                pe.wait_ge(keyed, q + 1)
                                m.transpose(ps_row[:, 0:P], key[:].broadcast_to([P, P]), ident[:])
                                pe.wait_ge(one_hot, QE + q + 1)
                                pass_waits(pe, passed_pe)
                                m.transpose(ps_hi[0:HB, 0:P], ohhi[:], identb[:]).then_inc(turned, 1)
                                m.matmul(ps_new[:, 0:P], ohhi[:], ohlo[:], start=True, stop=True)
                                pe.wait_ge(hiT_ready, q + 1)
                                pe.wait_ge(free_ready, q + 1)
                                m.matmul(ps_cnt[:, 0:P], hiT[:], free[:], start=True, stop=True).then_inc(ranked, 1)
                            pipeline(pe, QE, [(0, rank)])

                    @block.scalar
                    def _(act):
                        with edges_unsorted(act):
                            def copy(q, u, n):
                                act.wait_ge(turned, q + 1)
                                wait(act, ranked, q)
                                nc.scalar.copy(hiT[:], ps_hi[0:HB, 0:P]).then_inc(hiT_ready, 1)
                            pipeline(act, QE, [(0, copy)])

            with ExitStack() as t:
                rec = sb(t, "rec_in", [P, 4, 4, W])
                inv = sb(t, "inv", [P, 4, 4])
                srcm = sb(t, "srcm", [P, 4, 4])
                him = sb(t, "him", [P, 4, 4])
                ohlo = sb(t, "ohlo_a", [P, 4, 4, P], BF16)
                ohhi = sb(t, "ohhi_a", [P, 4, 4, HB], BF16)
                ohd = sb(t, "ohd_a", [P, 4, 4, P], BF16)
                hiT = sb(t, "hiT", [HB, 4, 4, P])
                dstT = sb(t, "dstT", [P, 4, 4, P])
                recT = sb(t, "recT", [P, 4, P])
                junk = sb(t, "junk", [P, 4, P], BF16)
                new = sb(t, "new", [HB, 4, 4, P])
                junk2 = sb(t, "junk2", [P, 4, P], BF16)
                within = sb(t, "within", [P, 4, 4])
                across = sb(t, "across", [P, 4, 4])
                place = sb(t, "place", [P, 4, 4], I32)
                ur = sb(t, "u", [P, 4, 4, F])
                ps_row = [ps(t, f"ps_row{k}", [P, 512]) for k in range(2)]
                ps_cnt = [ps(t, f"ps_cnt{k}", [P, 4, P]) for k in range(2)]
                ps_rec = ps(t, "ps_rec", [P, 512])
                ps_oh = ps(t, "ps_oh", [P, 2, 512], BF16)
                ps_new = ps(t, "ps_new", [HB, 4, P])
                ps_u_bank = ps(t, "ps_u", [P, 512])
                ps_u = ps_u_bank[:, 0:4 * F].rearrange("p (j f) -> p j f", j=4)
                rec_in = [sem(t, f"rec_in{k}") for k in range(4)]
                oh_ready = sem(t, "oh_ready")
                key_chain = sem(t, "key_chain")
                rec_turned = sem(t, "rec_turned")
                rows_ready = sem(t, "rows_ready")
                oh_turned = sem(t, "oh_turned")
                recT_ready = sem(t, "recT_ready")
                ohT_ready = sem(t, "ohT_ready")
                new_ready = sem(t, "new_ready")
                new_taken = sem(t, "new_taken")
                cnt_ready = sem(t, "cnt_ready")
                place_chain = sem(t, "place_chain")
                place_ready = sem(t, "place_ready")
                next_ready = sem(t, "next_ready")
                sum_ready = sem(t, "sum_ready")
                u_ready = sem(t, "u_ready")
                sent = [sem(t, f"sent{k}") for k in range(4)]
                pads_set = sem(t, "pads_set")
                passed = sem(t, "passed_a")
                passed_pe = sem(t, "passed_pe")

                with nc.Block() as block:
                    @block.sync
                    def _(sp):
                        records = rec_d.rearrange("e w -> (e w)")

                        def load(i, u, n):
                            wait(sp, oh_ready, i - 3)
                            wait(sp, rec_turned, i - 3)
                            at = offsets(nc, mybir.EngineType.SP, e0_row[0:1, bass.ds(4 * i, 4)], E * W)
                            for j in range(4):
                                sp.dma_start(rec[:, u, j, :], records[bass.ds(at[j], P * W)].rearrange("(p w) -> p w", w=W)).then_inc(rec_in[u], 16)
                        pipeline(sp, G, [(0, load)])

                    @block.gpsimd
                    def _(pool):
                        def send(i, u, n):
                            pool.wait_ge(place_ready, i + 1)
                            pool.wait_ge(u_ready, i + 1)
                            pass_waits(pool, passed)
                            for j in range(4):
                                pool.indirect_dma_start(u_d, bass.IndirectOffsetOnAxis(place[:, u, j:j + 1], 0),
                                                        ur[:, u, j, :], None, bounds_check=POS - 1,
                                                        oob_is_err=False).then_inc(sent[u], 16)
                        for b in range(EARLY, NB):
                            clear_pads(pool, b, pads_set)
                        pipeline(pool, G, [(0, send)])
                        pool.wait_ge(pads_set, 16 * (NB - EARLY))
                        for k in range(4):
                            pool.wait_ge(sent[k], 64 * len(range(k, G, 4)))

                    @block.vector
                    def _(dve):
                        v = nc.vector

                        def local(i, u, n):
                            dve.wait_ge(rec_in[u], 64 * (n + 1))
                            now = bass.ds(4 * i, 4)
                            v.tensor_tensor(dloc_s[:, now], rec[:, u, :, C_DST], off_s[:, now], ALU.subtract).then_inc(key_chain, 1)

                        def invalid(i, u, n):
                            dve.wait_ge(key_chain, 4 * i + 1)
                            v.tensor_scalar(inv[:, u], dloc_s[:, bass.ds(4 * i, 4)], float(P), None, ALU.is_ge).then_inc(key_chain, 1)

                        def keys(i, u, n):
                            dve.wait_ge(key_chain, 4 * i + 2)
                            wait(dve, rows_ready, i - 3)
                            v.scalar_tensor_tensor(out=him[:, u], in0=inv[:, u], scalar=float(HB - 1), in1=rec[:, u, :, C_HI],
                                                   op0=ALU.mult, op1=ALU.max).then_inc(key_chain, 1)
                            v.scalar_tensor_tensor(out=srcm[:, u], in0=inv[:, u], scalar=65536.0, in1=rec[:, u, :, C_SRC],
                                                   op0=ALU.mult, op1=ALU.add).then_inc(key_chain, 1)
                            v.tensor_scalar(src_s[:, bass.ds(4 * i, 4)], rec[:, u, :, C_SRC], float(NP - 1), None, ALU.min)

                        def onehot(i, u, n):
                            wait(dve, oh_turned, i - 3)
                            wait(dve, new_ready, i - 3)
                            v.tensor_tensor(ohlo[:, u], bcast(rec[:, u, :, C_LO:C_LO + 1], P, 4, P),
                                            bcast(iota_b[:].unsqueeze(1), P, 4, P), ALU.is_equal)
                            v.tensor_tensor(ohd[:, u], bcast(dloc_s[:, bass.ds(4 * i, 4)].unsqueeze(2), P, 4, P),
                                            bcast(iota_b[:].unsqueeze(1), P, 4, P), ALU.is_equal)
                            dve.wait_ge(key_chain, 4 * i + 4)
                            v.tensor_tensor(ohhi[:, u], bcast(him[:, u].unsqueeze(2), P, 4, HB),
                                            bcast(iota_b[:, 0:HB].unsqueeze(1), P, 4, HB), ALU.is_equal).then_inc(oh_ready, 1)

                        def same_step(i, u, n):
                            dve.wait_ge(rows_ready, i + 1)
                            wait(dve, place_ready, i - 3)
                            for j in range(4):
                                v.scalar_tensor_tensor(
                                    out=junk[:, j, :], in0=ps_row[u % 2][:, P * j:P * j + P], scalar=srcm[:, u, j:j + 1],
                                    in1=before[:], op0=ALU.is_equal, op1=ALU.mult,
                                    accum_out=within[:, u, j:j + 1]).then_inc(place_chain, 1)

                        def steps_before(i, u, n):
                            dve.wait_ge(cnt_ready, i + 1)
                            for j in range(4):
                                v.tensor_tensor_reduce(junk2[:, j, :], ps_cnt[u % 2][:, j, :], ohlo[:, u, j, :], 1.0, 0.0,
                                                       ALU.mult, ALU.add, across[:, u, j:j + 1]).then_inc(place_chain, 1)

                        def advance(i, u, n):
                            dve.wait_ge(new_taken, i + 1)
                            wait(dve, cnt_ready, i - 2)
                            wait(dve, next_ready, i)
                            v.tensor_tensor(rank_r[:, (u + 1) % 4], rank_r[:, u], new[:, u, 3, :], ALU.add).then_inc(next_ready, 1)

                        def put(i, u, n):
                            dve.wait_ge(place_chain, 8 * (i + 1))
                            s4, n4 = past(sent, u, n, 4)
                            wait(dve, s4, 64 * n4)
                            v.tensor_tensor(place[:, u], within[:, u], across[:, u], ALU.add).then_inc(place_ready, 1)
                        pipeline(dve, G, [(0, local), (4, same_step), (0, invalid), (4, steps_before), (3, advance),
                                          (0, keys), (4, put), (0, onehot)])

                    @block.tensor
                    def _(pe):
                        m = nc.tensor

                        def count(i, u, n):
                            k = u % 2
                            pe.wait_ge(ohT_ready, i + 1)
                            wait(pe, next_ready, i)
                            wait(pe, place_chain, 8 * (i - 1))
                            for j in range(4):
                                mm = m.matmul(ps_cnt[k][:, j, :], hiT[:, u, j, :], rank_r[:, u, :], start=True, stop=(j == 0))
                                if j > 0:
                                    mm = m.matmul(ps_cnt[k][:, j, :], hiT[:, u, j, :], new[:, u, j - 1, :], start=False, stop=True)
                            mm.then_inc(cnt_ready, 1)
                            for j in range(4):
                                mm = m.transpose(ps_row[k][:, P * j:P * j + P], srcm[:, u, j:j + 1].broadcast_to([P, P]), ident[:])
                            mm.then_inc(rows_ready, 1)

                        def turn(i, u, n):
                            pe.wait_ge(rec_in[u], 64 * (n + 1))
                            wait(pe, recT_ready, i)
                            m.transpose(ps_rec[:, 0:P], rec[:, u].rearrange("p j w -> p (j w)"), ident[:]).then_inc(rec_turned, 1)
                            pe.wait_ge(oh_ready, i + 1)
                            wait(pe, new_taken, i)
                            for j in range(4):
                                for q in range(j + 1):
                                    mm = m.matmul(ps_new[:, j, :], ohhi[:, u, q, :], ohlo[:, u, q, :], start=(q == 0), stop=(q == j))
                            mm.then_inc(new_ready, 1)
                            wait(pe, ohT_ready, i)
                            pass_waits(pe, passed_pe)
                            for j in range(4):
                                m.transpose(ps_oh[0:HB, 0, P * j:P * j + P], ohhi[:, u, j, :], identb[:])
                            for j in range(4):
                                mm = m.transpose(ps_oh[:, 1, P * j:P * j + P], ohd[:, u, j, :], identb[:])
                            mm.then_inc(oh_turned, 1)

                        def product(i, u, n):
                            pe.wait_ge(recT_ready, i + 1)
                            wait(pe, u_ready, i)
                            m.matmul(ps_u.rearrange("p j f -> p (j f)"), recT[:, u, :], we_s[:].rearrange("p j f -> p (j f)"),
                                     start=True, stop=False, skip_group_check=True)
                            at = offsets(nc, mybir.EngineType.PE, df_row[0:1, bass.ds(4 * i, 4)], NB * F - F)
                            for j in range(4):
                                mm = m.matmul(ps_u[:, j, :], dstT[:, u, j, :], m2[:, bass.ds(at[j], F)],
                                              start=False, stop=True, skip_group_check=True)
                            mm.then_inc(sum_ready, 1)
                        pipeline(pe, G, [(3, count), (1, turn), (3, product)])

                    @block.scalar
                    def _(act):
                        s = nc.scalar

                        def rows(i, u, n):
                            act.wait_ge(sum_ready, i + 1)
                            s4, n4 = past(sent, u, n, 4)
                            wait(act, s4, 64 * n4)
                            s.copy(ur[:, u], ps_u).then_inc(u_ready, 1)

                        def turned(i, u, n):
                            act.wait_ge(rec_turned, i + 1)
                            wait(act, sum_ready, i - 3)
                            s.copy(recT[:, u, :], ps_rec[:, 0:P]).then_inc(recT_ready, 1)
                            act.wait_ge(new_ready, i + 1)
                            wait(act, cnt_ready, i - 3)
                            wait(act, next_ready, i - 3)
                            s.copy(new[:, u], ps_new[:]).then_inc(new_taken, 1)
                            act.wait_ge(oh_turned, i + 1)
                            s.copy(hiT[:, u].rearrange("p j e -> p (j e)"), ps_oh[0:HB, 0, :])
                            s.copy(dstT[:, u].rearrange("p j e -> p (j e)"), ps_oh[:, 1, :]).then_inc(ohT_ready, 1)
                        pipeline(act, G, [(4, rows), (1, turned)])

            with ExitStack() as t:
                u_in_s = sb(t, "u_in", [P, 4, 4, F])
                starts = sb(t, "starts", [P, 4, 4, P], BF16)
                after = sb(t, "after", [P, 4, 4, P])
                oh = sb(t, "oh_b", [P, 4, 4, P])
                m1_s = sb(t, "m1_s", [P, 4, 4, F])
                msg = sb(t, "msg", [F, 4, 4 * P])
                msg2 = sb(t, "msg2", [F, 2, 4 * P])
                top = sb(t, "top", [F, 4, 4 * P])
                row = sb(t, "row", [P, 4, 4, F])
                ps_pre = [ps(t, f"ps_pre{k}", [F, 512]) for k in range(2)]
                ps_net = [ps(t, f"ps_net{k}", [F, 512]) for k in range(2)]
                ps_reset = [ps(t, f"ps_reset{k}", [F, 512]) for k in range(2)]
                ps_top = [ps(t, f"ps_top{k}", [P, 4, P]) for k in range(2)]
                u_in = [sem(t, f"u_in{k}") for k in range(4)]
                m1_ready = sem(t, "m1_ready")
                starts_ready = sem(t, "starts_ready")
                oh_ready = sem(t, "oh_ready_b")
                after_ready = sem(t, "after_ready")
                pre_ready = sem(t, "pre_ready")
                msg_ready = sem(t, "msg_ready")
                net_ready = sem(t, "net_ready")
                msg2_ready = sem(t, "msg2_ready")
                top_ready = sem(t, "top_ready")
                top_turned = sem(t, "top_turned")
                row_ready = sem(t, "row_ready")
                row_out = [sem(t, f"row_out{k}") for k in range(4)]
                passed_pool = sem(t, "passed_pool")
                with nc.Block() as block:
                    @block.sync
                    def _(sp):
                        def load(i, u, n):
                            wait(sp, pre_ready, i - 3)
                            sp.dma_start(u_in_s[:, u], u_d[bass.ds(4 * P * i, 4 * P), :].rearrange("(j p) f -> p j f", p=P)).then_inc(u_in[u], 16)

                        def store(i, u, n):
                            sp.wait_ge(row_ready, i + 1)
                            sp.dma_start(s_d[bass.ds(4 * P * i, 4 * P), :].rearrange("(j p) f -> p j f", p=P), row[:, u]).then_inc(row_out[u], 16)
                        pipeline(sp, G, [(6, store), (0, load)])
                        for k in range(4):
                            sp.wait_ge(row_out[k], 16 * len(range(k, G, 4)))

                    @block.gpsimd
                    def _(pool):
                        def stage(i, u, n):
                            wait(pool, pre_ready, i - 3)
                            pass_waits(pool, passed_pool)
                            at = offsets(nc, mybir.EngineType.Pool, sf_row[0:1, bass.ds(4 * i, 4)], NB * F - F)
                            for j in range(4):
                                last = nc.gpsimd.tensor_copy(m1_s[:, u, j, :], m1[:, bass.ds(at[j], F)])
                            last.then_inc(m1_ready, 1)
                        pipeline(pool, G, [(0, stage)])

                    @block.vector
                    def _(dve):
                        v = nc.vector

                        def onehot(i, u, n):
                            wait(dve, pre_ready, i - 3)
                            now = bass.ds(4 * i, 4)
                            v.tensor_tensor(after[:, u], bcast(iota_f[:].unsqueeze(1), P, 4, P),
                                            bcast(start_s[:, now].unsqueeze(2), P, 4, P), ALU.is_ge).then_inc(after_ready, 1)
                            wait(dve, net_ready, i - 3)
                            v.tensor_tensor(starts[:, u], bcast(iota_f[:].unsqueeze(1), P, 4, P),
                                            bcast(start_s[:, now].unsqueeze(2), P, 4, P), ALU.is_equal).then_inc(starts_ready, 1)
                            dve.wait_ge(after_ready, i + 1)
                            for j in range(4):
                                last = v.scalar_tensor_tensor(out=oh[:, u, j, :], in0=iota_f[:], scalar=end_s[:, bass.ds(4 * i + j, 1)],
                                                              in1=after[:, u, j, :], op0=ALU.is_lt, op1=ALU.mult)
                            last.then_inc(oh_ready, 1)

                        def scan(i, u, n):
                            k = u % 2
                            dve.wait_ge(msg2_ready, i + 1)
                            wait(dve, top_turned, i - 3)
                            wait(dve, top_ready, i)
                            first = isinstance(i, int) and i == 0
                            v.tensor_tensor_scan(top[:, u, :], ps_reset[k][:], msg2[:, k, :],
                                                 0.0 if first else top[:, (u - 1) % 4, 4 * P - 1:4 * P],
                                                 ALU.add, ALU.max).then_inc(top_ready, 1)
                        pipeline(dve, G, [(4, scan), (0, onehot)])

                    @block.tensor
                    def _(pe):
                        m = nc.tensor

                        def pre(i, u, n):
                            pe.wait_ge(u_in[u], 16 * (n + 1))
                            wait(pe, msg_ready, i - 1)
                            pe.wait_ge(oh_ready, i + 1)
                            pe.wait_ge(m1_ready, i + 1)
                            for j in range(4):
                                to = ps_pre[u % 2][:, P * j:P * j + P]
                                m.matmul(to, u_in_s[:, u, j, :], ident[:], start=True, stop=False)
                                mm = m.matmul(to, m1_s[:, u, j, :], oh[:, u, j, :], start=False, stop=True)
                            mm.then_inc(pre_ready, 1)

                        def net(i, u, n):
                            k = u % 2
                            wait(pe, top_ready, i - 1)
                            pe.wait_ge(starts_ready, i + 1)
                            m.matmul(ps_reset[k][:], reset_b[:], starts[:, u].rearrange("p j e -> p (j e)"), start=True, stop=True)
                            pe.wait_ge(msg_ready, i + 1)
                            m.matmul(ps_net[k][:], wnet_s[:], msg[:, u, :], start=True, stop=True).then_inc(net_ready, 1)

                        def turn(i, u, n):
                            pe.wait_ge(top_ready, i + 1)
                            wait(pe, row_ready, i - 1)
                            for j in range(4):
                                mm = m.transpose(ps_top[u % 2][:, j, 0:F], top[:, u, P * j:P * j + P], ident[0:F, 0:F])
                            mm.then_inc(top_turned, 1)
                        pipeline(pe, G, [(3, net), (5, turn), (1, pre)])

                    @block.scalar
                    def _(act):
                        s = nc.scalar

                        def first(i, u, n):
                            k = u % 2
                            act.wait_ge(pre_ready, i + 1)
                            wait(act, net_ready, i - 3)
                            s.activation(msg[:, u, :], ps_pre[k][:], ACT.Relu).then_inc(msg_ready, 1)

                        def second(i, u, n):
                            k = u % 2
                            act.wait_ge(net_ready, i + 1)
                            wait(act, top_ready, i - 1)
                            s.activation(msg2[:, k, :], ps_net[k][:], ACT.Relu, bias=bnet_c[:]).then_inc(msg2_ready, 1)

                        def rows(i, u, n):
                            act.wait_ge(top_turned, i + 1)
                            s4, n4 = past(row_out, u, n, 4)
                            wait(act, s4, 16 * n4)
                            s.copy(row[:, u], ps_top[u % 2][:, :, 0:F]).then_inc(row_ready, 1)
                        pipeline(act, G, [(3, second), (5, rows), (1, first)])

        layer1 = ExitStack()
        with layer1:
            x1 = sb(layer1, "x1", [P, NB, D])
            x1T = sb(layer1, "x1T", [D, NP])
            hsumT = sb(layer1, "hsumT", [D, NP])
            deg = sb(layer1, "deg", [P, NB])
            bpart = sb(layer1, "bpart", [P, NB * D])
            with ExitStack() as t:
                agg_all = sb(t, "agg_all", [P, NB, F])
                aggT = sb(t, "aggT", [F, 2, P])
                stats = sb(t, "stats", [P, NB, 6])
                mv = sb(t, "mv", [P, NB, 2])
                std = sb(t, "std", [P, NB])
                rstd = sb(t, "rstd", [P, NB])
                arow = sb(t, "arow", [P, 2, CH, D])
                wo1_s = sb(t, "wo1_s", [D, D])
                wo2_s = sb(t, "wo2_s", [F, D])
                bo_s = sb(t, "bo_s", [P, 2, D])
                bo_sum = sb(t, "bo_sum", [P, 1, D])
                ew1_s = sb(t, "ew1_s", [D, 2 * D])
                eb1_s = sb(t, "eb1_s", [P, D])
                eps_c = sb(t, "eps_c", [P, 1])
                ps_t = [ps(t, f"ps_t{k}", [P, 512]) for k in range(2)]
                ps_y = [ps(t, f"ps_y{k}", [P, 512]) for k in range(2)]
                ps_x = [ps(t, f"ps_x{k}", [P, 512]) for k in range(2)]
                ps_ab = [ps(t, f"ps_ab{k}", [P, 512]) for k in range(2)]
                chunks = [list(range(c, min(c + CH, NB))) for c in range(0, NB, CH)]
                C = len(chunks)
                agg_in = [sem(t, f"agg_in{c}") for c in range(C)]
                w_in = sem(t, "w_in")
                x_in = [sem(t, f"x_in{c}") for c in range(C)]
                eps_set = sem(t, "eps_set")
                agg_turned = sem(t, "agg_turned")
                aggT_ready = sem(t, "aggT_ready")
                y_ready = sem(t, "y_ready")
                stats_ready = sem(t, "stats_ready")
                var_ready = sem(t, "var_ready_a")
                std_ready = sem(t, "std_ready")
                r_ready = sem(t, "r_ready_a")
                y_added = sem(t, "y_added")
                biased = sem(t, "biased")
                x1_ready = sem(t, "x1_ready")
                x1_turned = sem(t, "x1_turned")
                x1T_ready = sem(t, "x1T_ready")
                ab_ready = sem(t, "ab_ready")
                a_ready = sem(t, "a_ready")
                b_ready = sem(t, "b_ready")
                a_out = [sem(t, f"a_out{k}") for k in range(2)]
                with nc.Block() as block:
                    @block.gpsimd
                    def _(pool):
                        nc.gpsimd.memset(eps_c[:], EPS_LN).then_inc(eps_set, 1)
                        for b in range(NB):
                            pool.indirect_dma_start(agg_all[:, b, :], None, s_d,
                                                    bass.IndirectOffsetOnAxis(last_i[:, b:b + 1], 0)).then_inc(agg_in[b // CH], 16)
                        nc.gpsimd.memset(hsumT[:], 0.0).then_inc(eps_set, 1)
                        nc.gpsimd.memset(deg[:], 0.0).then_inc(eps_set, 1)

                    @block.sync
                    def _(sp):
                        for to, of in ((wo1_s[:], wo1), (wo2_s[:], wo2), (ew1_s[:, 0:D], ew1a), (ew1_s[:, D:2 * D], ew1b),
                                       (bo_s[:, 0, :], bo[0:1, :].broadcast_to([P, D])), (bo_s[:, 1, :], bo[1:2, :].broadcast_to([P, D])),
                                       (eb1_s[:], eb1.broadcast_to([P, D]))):
                            sp.dma_start(to, of).then_inc(w_in, 16)
                        for c, blocks in enumerate(chunks):
                            lo, hi = blocks[0], blocks[-1] + 1
                            sp.dma_start(x1T[:, P * lo:P * hi], xT[:, P * lo:P * hi]).then_inc(x_in[c], 16)
                            sp.dma_start(x1[:, lo:hi, :], x[P * lo:P * hi, :].rearrange("(b p) d -> p b d", p=P)).then_inc(x_in[c], 16)
                        for c, blocks in enumerate(chunks):
                            lo, hi = blocks[0], blocks[-1] + 1
                            sp.wait_ge(a_ready, hi)
                            sp.dma_start(a_d[P * lo:P * hi, :].rearrange("(b p) d -> p b d", p=P), arow[:, c % 2, 0:hi - lo, :]).then_inc(a_out[c % 2], 16)
                        for k in range(2):
                            sp.wait_ge(a_out[k], 16 * len(range(k, C, 2)))

                    @block.scalar
                    def _(act):
                        s = nc.scalar

                        def aggregate(b):
                            act.wait_ge(agg_turned, b + 1)
                            wait(act, y_ready, b - 1)
                            s.copy(aggT[:, b % 2, :], ps_t[b % 2][0:F, 0:P]).then_inc(aggT_ready, 1)

                        def tables(b):
                            act.wait_ge(ab_ready, b + 1)
                            c = b // CH
                            if c >= 2:
                                act.wait_ge(a_out[c % 2], 16 * (c // 2))
                            s.copy(arow[:, c % 2, b % CH, :], ps_ab[b % 2][:, 0:D]).then_inc(a_ready, 1)

                        def turned(b):
                            act.wait_ge(x1_turned, b + 1)
                            s.copy(x1T[:, P * b:P * b + P], ps_x[b % 2][:, 0:P]).then_inc(x1T_ready, 1)
                        act.wait_ge(eps_set, 1)
                        for c in range(C + 1):
                            for q in range(CH + 1):
                                if c < C and q < len(chunks[c]):
                                    aggregate(chunks[c][q])
                                if c > 0 and 0 < q <= len(chunks[c - 1]):
                                    tables(chunks[c - 1][q - 1])
                                if c > 0 and q < len(chunks[c - 1]):
                                    turned(chunks[c - 1][q])
                            if c < C:
                                lo, hi = chunks[c][0], chunks[c][-1] + 1
                                act.wait_ge(var_ready, hi)
                                s.activation(std[:, lo:hi], mv[:, lo:hi, 1], ACT.Sqrt, bias=eps_c[:]).then_inc(std_ready, 1)

                    @block.tensor
                    def _(pe):
                        m = nc.tensor
                        pe.wait_ge(w_in, 16 * 7)

                        def turn(b):
                            if b % CH == 0:
                                pe.wait_ge(agg_in[b // CH], 16 * len(chunks[b // CH]))
                            wait(pe, aggT_ready, b - 1)
                            m.transpose(ps_t[b % 2][0:F, 0:P], agg_all[:, b, :], ident[:]).then_inc(agg_turned, 1)

                        def update(b):
                            if b % CH == 0:
                                pe.wait_ge(x_in[b // CH], 32)
                            to = ps_y[b % 2][:, 0:D]
                            wait(pe, y_added, b - 1)
                            m.matmul(to, x1T[:, P * b:P * b + P], wo1_s[:], start=True, stop=False)
                            pe.wait_ge(aggT_ready, b + 1)
                            m.matmul(to, aggT[:, b % 2, :], wo2_s[:], start=False, stop=True).then_inc(y_ready, 1)

                        def turn_x1(b):
                            pe.wait_ge(x1_ready, b + 1)
                            wait(pe, x1T_ready, b - 1)
                            m.transpose(ps_x[b % 2][:, 0:P], x1[:, b, :], ident[:]).then_inc(x1_turned, 1)

                        def tables(b):
                            pe.wait_ge(x1T_ready, b + 1)
                            wait(pe, b_ready, b - 1)
                            to = ps_ab[b % 2]
                            m.matmul(to[:, 0:2 * D], x1T[:, P * b:P * b + P], ew1_s[:], start=True, stop=True).then_inc(ab_ready, 1)
                        for c in range(C + 1):
                            for q in range(CH + 1):
                                if c < C and q < len(chunks[c]):
                                    turn(chunks[c][q])
                                if c > 0 and q < len(chunks[c - 1]):
                                    turn_x1(chunks[c - 1][q])
                                if c < C and 0 < q <= len(chunks[c]):
                                    update(chunks[c][q - 1])
                                if c > 0 and 0 < q <= len(chunks[c - 1]):
                                    tables(chunks[c - 1][q - 1])

                    @block.vector
                    def _(dve):
                        v = nc.vector
                        dve.wait_ge(w_in, 16 * 7)
                        v.tensor_tensor(bo_sum[:, 0, :], bo_s[:, 0, :], bo_s[:, 1, :], ALU.add).then_inc(biased, 1)
                        dve.wait_ge(biased, 1)

                        def add(b):
                            dve.wait_ge(y_ready, b + 1)
                            v.tensor_tensor(x1[:, b, :], ps_y[b % 2][:, 0:D], x1[:, b, :], ALU.add).then_inc(y_added, 1)

                        def dst_table(b):
                            dve.wait_ge(a_ready, b + 1)
                            v.tensor_tensor(bpart[:, D * b:D * b + D], ps_ab[b % 2][:, D:2 * D], eb1_s[:], ALU.add).then_inc(b_ready, 1)
                        for c in range(C + 1):
                            blocks = chunks[c] if c < C else []
                            if blocks:
                                lo, hi = blocks[0], blocks[-1] + 1
                                dve.wait_ge(x_in[c], 32)
                                v.tensor_tensor(x1[:, lo:hi, :], x1[:, lo:hi, :], bcast(bo_sum[:], P, hi - lo, D), ALU.add).then_inc(biased, 1)
                                dve.wait_ge(biased, c + 2)
                            for q in range(CH):
                                if q < len(blocks):
                                    add(blocks[q])
                                if c > 0 and q < len(chunks[c - 1]):
                                    dst_table(chunks[c - 1][q])
                            if blocks:
                                dve.wait_ge(y_added, hi)
                                for b in blocks:
                                    v.bn_stats(stats[:, b, :], x1[:, b, :]).then_inc(stats_ready, 1)
                                dve.wait_ge(stats_ready, hi)
                                for b in blocks:
                                    v.bn_aggr(mv[:, b, :], stats[:, b, :]).then_inc(var_ready, 1)
                                dve.wait_ge(std_ready, c + 1)
                                v.reciprocal(rstd[:, lo:hi], std[:, lo:hi]).then_inc(r_ready, 1)
                                dve.wait_ge(r_ready, c + 1)
                                for b in blocks:
                                    v.tensor_scalar(x1[:, b, :], x1[:, b, :], mv[:, b, 0:1], rstd[:, b:b + 1],
                                                    ALU.subtract, ALU.mult).then_inc(x1_ready, 1)

            with ExitStack() as t:
                idx = sb(t, "idx", [P, 4, 4], I32)
                a_rows = sb(t, "a_rows", [P, 4, 4, D])
                ohd = sb(t, "ohd_f", [P, 4, 4, P])
                dstT = sb(t, "dstT_b", [P, 2, 4, P])
                h = sb(t, "h", [P, 4, 4, D])
                ps_t = [ps(t, f"ps_tt{k}", [P, 512]) for k in range(2)]
                ps_h = [ps(t, f"ps_h{k}", [P, 4, D]) for k in range(2)]
                ps_s = [ps(t, f"ps_s{k}", [D, 4, P]) for k in range(2)]
                ps_n = [ps(t, f"ps_n{k}", [P, 512]) for k in range(2)]
                idx_ready = sem(t, "idx_ready")
                got = [sem(t, f"got{k}") for k in range(4)]
                passed = sem(t, "passed_d")
                oh_ready = sem(t, "oh_ready_c")
                dst_turned = sem(t, "dst_turned_b")
                dstT_ready = sem(t, "dstT_ready_b")
                pre_ready = sem(t, "pre_ready_b")
                h_ready = sem(t, "h_ready")
                sum_ready = sem(t, "sum_ready_b")
                add_chain = sem(t, "add_chain")
                with nc.Block() as block:
                    @block.gpsimd
                    def _(pool):
                        def fetch(i, u, n):
                            pool.wait_ge(idx_ready, i + 1)
                            wait(pool, pre_ready, i - 3)
                            pass_waits(pool, passed)
                            for j in range(4):
                                pool.indirect_dma_start(a_rows[:, u, j, :], None, a_d,
                                                        bass.IndirectOffsetOnAxis(idx[:, u, j:j + 1], 0)).then_inc(got[u], 16)
                        pipeline(pool, G, [(0, fetch)])

                    @block.vector
                    def _(dve):
                        v = nc.vector
                        adds = Chain(dve, add_chain, 8)

                        def add(i, u, n):
                            k = u % 2
                            adds.turn(i)
                            dve.wait_ge(sum_ready, i + 1)
                            to = offsets(nc, mybir.EngineType.DVE, dd_row[0:1, bass.ds(4 * i, 4)], NP - P)
                            of = offsets(nc, mybir.EngineType.DVE, db_row[0:1, bass.ds(4 * i, 4)], NB - 1)
                            for j in range(4):
                                at = hsumT[:, bass.ds(to[j], P)]
                                adds.add(v.tensor_tensor(at, at, ps_s[k][:, j, :], ALU.add))
                                dg = deg[:, bass.ds(of[j], 1)]
                                adds.add(v.tensor_tensor(dg, dg, ps_n[k][:, j:j + 1], ALU.add))
                                adds.settle()

                        def prepare(i, u, n):
                            s4, n4 = past(got, u, n, 4)
                            wait(dve, s4, 64 * n4)
                            v.tensor_copy(idx[:, u], src_s[:, bass.ds(4 * i, 4)]).then_inc(idx_ready, 1)

                        def onehot(i, u, n):
                            now = bass.ds(4 * i, 4)
                            wait(dve, sum_ready, i - 3)
                            v.tensor_tensor(ohd[:, u], bcast(dloc_s[:, now].unsqueeze(2), P, 4, P),
                                            bcast(iota_f[:].unsqueeze(1), P, 4, P), ALU.is_equal).then_inc(oh_ready, 1)
                        pipeline(dve, G, [(0, prepare), (2, onehot), (6, add)])

                    @block.tensor
                    def _(pe):
                        m = nc.tensor

                        def turn(i, u, n):
                            pe.wait_ge(oh_ready, i + 1)
                            wait(pe, dstT_ready, i - 1)
                            for j in range(4):
                                mm = m.transpose(ps_t[u % 2][:, P * j:P * j + P], ohd[:, u, j, :], ident[:])
                            mm.then_inc(dst_turned, 1)

                        def pre(i, u, n):
                            k = u % 2
                            pe.wait_ge(got[u], 64 * (n + 1))
                            wait(pe, h_ready, i - 1)
                            m.matmul(ps_h[k][:].rearrange("p j d -> p (j d)"), ident[:], a_rows[:, u].rearrange("p j d -> p (j d)"),
                                     start=True, stop=False, skip_group_check=True)
                            pe.wait_ge(dstT_ready, i + 1)
                            at = offsets(nc, mybir.EngineType.PE, dd_row[0:1, bass.ds(4 * i, 4)], NP - P)
                            for j in range(4):
                                mm = m.matmul(ps_h[k][:, j, :], dstT[:, k, j, :], bpart[:, bass.ds(at[j], D)],
                                              start=False, stop=True, skip_group_check=True)
                            mm.then_inc(pre_ready, 1)

                        def sums(i, u, n):
                            k = u % 2
                            pe.wait_ge(h_ready, i + 1)
                            wait(pe, add_chain, 8 * (i - 1))
                            for j in range(4):
                                m.matmul(ps_s[k][:, j, :], h[:, u, j, :], ohd[:, u, j, :], start=True, stop=True)
                                mm = m.matmul(ps_n[k][:, j:j + 1], ohd[:, u, j, :], onesf[:, 0:1], start=True, stop=True)
                            mm.then_inc(sum_ready, 1)
                        pipeline(pe, G, [(2, pre), (1, turn), (3, sums)])

                    @block.scalar
                    def _(act):
                        s = nc.scalar

                        def turned(i, u, n):
                            k = u % 2
                            act.wait_ge(dst_turned, i + 1)
                            wait(act, pre_ready, i - 1)
                            s.copy(dstT[:, k].rearrange("p j e -> p (j e)"), ps_t[k][:]).then_inc(dstT_ready, 1)

                        def gelu(i, u, n):
                            k = u % 2
                            act.wait_ge(pre_ready, i + 1)
                            wait(act, sum_ready, i - 3)
                            s.activation(h[:, u], ps_h[k][:], ACT.Gelu).then_inc(h_ready, 1)
                        pipeline(act, G, [(2, gelu), (1, turned)])

            with ExitStack() as t:
                diag = sb(t, "diag", [P, 4, P])
                hid = sb(t, "hid", [P, 4, P])
                stats = sb(t, "stats_b", [P, NB, 6])
                mv = sb(t, "mv_b", [P, NB, 2])
                std = sb(t, "std_b", [P, NB])
                rstd = sb(t, "rstd_b", [P, NB])
                yout = sb(t, "yout", [P, NB, D])
                ew2_s = sb(t, "ew2_s", [D, D])
                eb2_s = sb(t, "eb2_s", [D, 1])
                w2n_s = sb(t, "w2n_s", [D, D])
                b2n_s = sb(t, "b2n_s", [P, D])
                nw1a_s = sb(t, "nw1a_s", [D, D])
                nw1b_s = sb(t, "nw1b_s", [D, D])
                nb1_c = sb(t, "nb1_c", [D, 1])
                nw2_s = sb(t, "nw2_s", [D, D])
                nb2_s = sb(t, "nb2_s", [P, 1, D])
                eps_c = sb(t, "eps_d", [P, 1])
                ps_g = [ps(t, f"ps_g{k}", [P, 512]) for k in range(2)]
                ps_k = [ps(t, f"ps_k{k}", [P, 512]) for k in range(2)]
                ps_o = [ps(t, f"ps_o{k}", [P, 512]) for k in range(2)]
                w_in = sem(t, "w_in_b")
                eps_set = sem(t, "eps_set_b")
                diag_ready = sem(t, "diag_ready")
                combined = sem(t, "combined")
                weights_ready = sem(t, "weights_ready")
                doubled = sem(t, "doubled")
                k_ready = sem(t, "k_ready")
                hid_ready = sem(t, "hid_ready")
                o_ready = sem(t, "o_ready")
                y_ready = sem(t, "y_ready_b")
                stats_ready = sem(t, "stats_ready_b")
                mv_ready = sem(t, "mv_ready")
                var_ready = sem(t, "var_ready_b")
                std_ready = sem(t, "std_ready_b")
                r_ready = sem(t, "r_ready")
                out_ready = sem(t, "out_ready")
                stored = sem(t, "stored")
                with nc.Block() as block:
                    @block.gpsimd
                    def _(pool):
                        nc.gpsimd.memset(eps_c[:], EPS_LN).then_inc(eps_set, 1)

                    @block.sync
                    def _(sp):
                        for to, of in ((ew2_s[:], ew2), (eb2_s[:], eb2), (nw1a_s[:], nw1a), (nw1b_s[:], nw1b),
                                       (nb1_c[:], nb1), (nw2_s[:], nw2), (nb2_s[:, 0, :], nb2.broadcast_to([P, D]))):
                            sp.dma_start(to, of).then_inc(w_in, 16)
                        per = 7
                        count = 0
                        for b in range(0, NB, per):
                            full = min(b + per, N // P)
                            sp.wait_ge(out_ready, min(b + per, NB))
                            if full > b:
                                sp.dma_start(out[P * b:P * full, :].rearrange("(b p) d -> p b d", p=P), yout[:, b:full, :]).then_inc(stored, 16)
                                count += 1
                        if N % P:
                            sp.dma_start(out[P * (N // P):N, :], yout[0:N % P, NB - 1, :]).then_inc(stored, 16)
                            count += 1
                        sp.wait_ge(stored, 16 * count)

                    @block.vector
                    def _(dve):
                        v = nc.vector

                        def diagonal(b):
                            wait(dve, k_ready, b - 3)
                            v.tensor_scalar(diag[:, b % 4, :], ident[:], deg[:, b:b + 1], None, ALU.mult).then_inc(diag_ready, 1)

                        def later_diagonal(b):
                            if b >= 4:
                                diagonal(b)

                        def result(b):
                            dve.wait_ge(o_ready, b + 1)
                            v.tensor_tensor(x1[:, b, :], x1[:, b, :], ps_o[b % 2][:, 0:D], ALU.add).then_inc(y_ready, 1)

                        def statistics(b):
                            dve.wait_ge(y_ready, b + 1)
                            v.bn_stats(stats[:, b, :], x1[:, b, :]).then_inc(stats_ready, 1)

                        def variance(b):
                            dve.wait_ge(stats_ready, b + 1)
                            v.bn_aggr(mv[:, b, :], stats[:, b, :]).then_inc(mv_ready, 1)
                        for b in range(4):
                            if b < NB:
                                diagonal(b)
                        dve.wait_ge(w_in, 16 * 7)
                        for lo in range(0, NB, CH):
                            hi = min(lo + CH, NB)
                            v.scalar_tensor_tensor(out=x1[:, lo:hi, :], in0=x1[:, lo:hi, :], scalar=2.0,
                                                   in1=bcast(nb2_s[:], P, hi - lo, D), op0=ALU.mult, op1=ALU.add).then_inc(doubled, 1)
                        dve.wait_ge(doubled, -(-NB // CH))
                        for t in range(NB + 6):
                            for lag, stage in ((6, variance), (5, statistics), (4, result), (0, later_diagonal)):
                                if 0 <= t - lag < NB:
                                    stage(t - lag)
                        dve.wait_ge(mv_ready, NB)
                        v.engine_nop().then_inc(var_ready, 1)
                        dve.wait_ge(std_ready, 1)
                        v.reciprocal(rstd[:], std[:]).then_inc(r_ready, 1)
                        dve.wait_ge(r_ready, 1)

                        def normed(b, u, n):
                            one = bass.ds(b, 1)
                            v.tensor_scalar(yout[:, one, :].rearrange("p a f -> p (a f)"), x1[:, one, :].rearrange("p a f -> p (a f)"),
                                            mv[:, one, 0:1].rearrange("p a f -> p (a f)"), rstd[:, one], ALU.subtract, ALU.mult).then_inc(out_ready, 1)
                        pipeline(dve, NB, [(0, normed)])

                    @block.tensor
                    def _(pe):
                        m = nc.tensor
                        pe.wait_ge(w_in, 16 * 7)

                        m.matmul(ps_g[0][:, 0:D], ew2_s[:], nw1b_s[:], start=True, stop=True)
                        m.matmul(ps_g[1][:, 0:D], eb2_s[:].broadcast_to([D, P]), nw1b_s[:], start=True, stop=True).then_inc(combined, 1)

                        def hidden(b, u, n):
                            wait(pe, hid_ready, b - 1)
                            to = ps_k[u % 2][:, 0:P]
                            cols = bass.ds(P * b, P)
                            m.matmul(to, nw1a_s[:], x1T[:, cols], start=True, stop=False)
                            if isinstance(b, int) and b == 0:
                                pe.wait_ge(weights_ready, 1)
                            m.matmul(to, w2n_s[:], hsumT[:, cols], start=False, stop=False)
                            pe.wait_ge(diag_ready, b + 1)
                            m.matmul(to, b2n_s[:], diag[:, u, :], start=False, stop=True).then_inc(k_ready, 1)

                        def update(b, u, n):
                            pe.wait_ge(hid_ready, b + 1)
                            wait(pe, y_ready, b - 1)
                            m.matmul(ps_o[u % 2][:, 0:D], hid[:, u, :], nw2_s[:], start=True, stop=True).then_inc(o_ready, 1)
                        pipeline(pe, NB, [(2, update), (0, hidden)])

                    @block.scalar
                    def _(act):
                        s = nc.scalar
                        act.wait_ge(w_in, 16 * 7)

                        act.wait_ge(combined, 1)
                        s.copy(w2n_s[:], ps_g[0][:, 0:D])
                        s.copy(b2n_s[:], ps_g[1][:, 0:D]).then_inc(weights_ready, 1)

                        def gelu(b, u, n):
                            act.wait_ge(k_ready, b + 1)
                            wait(act, o_ready, b - 3)
                            s.activation(hid[:, u, :], ps_k[u % 2][:, 0:P], ACT.Gelu, bias=nb1_c[:]).then_inc(hid_ready, 1)
                        pipeline(act, NB, [(0, gelu)])
                        act.wait_ge(var_ready, 1)
                        act.wait_ge(eps_set, 1)
                        s.activation(std[:], mv[:, :, 1], ACT.Sqrt, bias=eps_c[:]).then_inc(std_ready, 1)


_ARGS = ["x", "xT", "src", "dst", "edge_attr", "wm12", "bm12", "w_e", "w_net", "b_net", "wo1", "wo2", "bo",
         "ew1a", "ew1b", "eb1", "ew2", "eb2", "nw1a", "nw1b", "nb1", "nw2", "nb2"]


def lay_out(i):
    import numpy as np
    a = {k: np.asarray(v) for k, v in i.items()}
    n, e = a["x"].shape[0], a["src"].shape[0]
    nb, q, _ = sizes(n, e)
    rows, edges = nb * P, q * P

    def pad(v, m, fill=0):
        return np.concatenate([v, np.full((m - v.shape[0],) + v.shape[1:], fill, v.dtype)])

    x = pad(a["x"], rows)
    ka = a["edge_attr_16"].shape[1]
    f = a["L0_gnn_W_net"].shape[0]
    d = x.shape[1]
    o = {
        "x": x, "xT": x.T,
        "src": pad(a["src"], edges, rows), "dst": pad(a["dst"], edges, rows),
        "edge_attr": pad(a["edge_attr_16"], edges),
        "wm12": np.concatenate([a["L0_gnn_W_m1"].T, a["L0_gnn_W_m2"].T], 1),
        "bm12": np.stack([np.concatenate([a["L0_gnn_b_m1"], a["L0_gnn_b_m2"]]),
                          np.concatenate([np.zeros_like(a["L0_gnn_b_me"]), a["L0_gnn_b_me"]])]),
        "w_e": pad(a["L0_gnn_W_me"].T, W),
        "w_net": a["L0_gnn_W_net"].T, "b_net": a["L0_gnn_b_net"][:, None],
        "wo1": a["L0_gnn_W_o1"].T, "wo2": a["L0_gnn_W_o2"].T,
        "bo": np.stack([a["L0_gnn_b_o1"], a["L0_gnn_b_o2"]]),
        "ew1a": a["L1_gnn_eW1"][:d], "ew1b": a["L1_gnn_eW1"][d:], "eb1": a["L1_gnn_eb1"][None],
        "ew2": a["L1_gnn_eW2"].T, "eb2": a["L1_gnn_eb2"][:, None],
        "nw1a": a["L1_gnn_nW1"][:d], "nw1b": a["L1_gnn_nW1"][d:], "nb1": a["L1_gnn_nb1"][:, None],
        "nw2": a["L1_gnn_nW2"], "nb2": a["L1_gnn_nb2"][None],
    }
    return {k: np.ascontiguousarray(o[k]) for k in _ARGS}, n, e


def program(nc, arrays, n, e):
    args = []
    for name in _ARGS:
        v = arrays[name]
        args.append(nc.dram_tensor(f"in_{name}", v.shape, mybir.dt.from_np(v.dtype), kind="ExternalInput").ap())
    out = nc.dram_tensor("out_0", (n, arrays["x"].shape[1]), F32, kind="ExternalOutput").ap()
    gnn(nc, e, *args, out)


def kernel(**inputs):
    import concourse.bacc as bacc
    from concourse.bass_utils import run_bass_kernel_spmd

    nc = bacc.Bacc("TRN2", target_bir_lowering=False, num_devices=1)
    arrays, n, e = lay_out(inputs)
    program(nc, arrays, n, e)
    r = run_bass_kernel_spmd(nc, [{f"in_{k}": v for k, v in arrays.items()}], core_ids=[0])
    return r.results[0]["out_0"]
```
